# Optimizing a Trainium2 kernel written in Bass

```python
import numpy as np
import jax
import jax.numpy as jnp

def _softmax(x, axis=-1):
    return jax.nn.softmax(x, axis=axis)

def _gelu(x):
    return jax.nn.gelu(x, approximate=True)

def _silu(x):
    return jax.nn.silu(x)

def _sigmoid(x):
    return jax.nn.sigmoid(x)

def _layernorm(x, axis=-1, eps=1e-05):
    m = jnp.mean(x, axis=axis, keepdims=True)
    v = jnp.var(x, axis=axis, keepdims=True)
    return (x - m) / jnp.sqrt(v + eps)

def _scatter_add(tgt, idx, src, axis=0):
    return tgt.at[idx].add(src)

def _segment_sum(src, seg, n):
    return jax.ops.segment_sum(src, seg, n)
kernel_name = 'mk_gps_d1_gnn_r32_6f88d7'

def setup_inputs(seed: int=0):
    np.random.seed(seed)
    _w = jnp.asarray

    def _rec_inputs():
        import jax
        import jax.numpy as jnp
        _gk = jax.random.key(seed)
        x = -8.776e-05 + 1 * jax.random.normal(jax.random.fold_in(_gk, 1), (625, 256), jnp.float32)
        _s = jax.random.randint(jax.random.fold_in(_gk, 2), (10000,), 0, 625, jnp.int32)
        _d = jax.random.randint(jax.random.fold_in(_gk, 3), (10000,), 0, 625, jnp.int32)
        _loop = jnp.arange(625, dtype=jnp.int32)
        src = jnp.concatenate([_s, _d, _loop])
        dst = jnp.concatenate([_d, _s, _loop])
        _o = jnp.argsort(dst, stable=True)
        src = src[_o]
        dst = dst[_o]
        edge_attr_64 = 1.36993e-05 + 0.999972 * jax.random.normal(jax.random.fold_in(_gk, 12), (20625, 64), jnp.float32)
        return (x, src, dst, edge_attr_64)
    x, src, dst, edge_attr_64 = _rec_inputs()

    def _L0_gnn_setup():
        import jax, jax.numpy as jnp
        import numpy as np
        N_NODES = 625
        N_EDGES = 10000
        D_IN = 256
        D_EDGE = 64
        D_HID = 256
        N_LAYERS = 3
        EPS = 1e-05

        def _conv(h, e, src, dst, Wn_l, bn_l, We_l, be_l, Wc_l, bc_l):
            hn = h @ Wn_l + bn_l
            et = e @ We_l + be_l
            m = hn[src] + et
            s = jax.ops.segment_sum(m, dst, num_segments=N_NODES)
            cnt = jax.ops.segment_sum(jnp.ones((m.shape[0],), m.dtype), dst, num_segments=N_NODES)
            agg = s / jnp.maximum(cnt, 1.0)[:, None]
            return jnp.concatenate([hn, agg], axis=1) @ Wc_l + bc_l

        def _layernorm(x, g, b):
            mu = jnp.mean(x, axis=-1, keepdims=True)
            var = jnp.mean(jnp.square(x - mu), axis=-1, keepdims=True)
            return (x - mu) / jnp.sqrt(var + EPS) * g + b
        key = jax.random.key(seed)
        ks = jax.random.split(key, 8)
        node_feat = jax.random.normal(ks[0], (N_NODES, D_IN), dtype=jnp.float32)
        edge_attr = jax.random.normal(ks[1], (N_EDGES, D_EDGE), dtype=jnp.float32)
        src = jax.random.randint(ks[2], (N_EDGES,), 0, N_NODES, dtype=jnp.int32)
        dst = jax.random.randint(ks[3], (N_EDGES,), 0, N_NODES, dtype=jnp.int32)
        Wn = jax.random.normal(ks[4], (N_LAYERS, D_IN, D_HID), dtype=jnp.float32) / np.sqrt(D_IN)
        We = jax.random.normal(ks[5], (N_LAYERS, D_EDGE, D_HID), dtype=jnp.float32) / np.sqrt(D_EDGE)
        Wc = jax.random.normal(ks[6], (N_LAYERS, 2 * D_HID, D_HID), dtype=jnp.float32) / np.sqrt(2 * D_HID)
        bn = jnp.zeros((N_LAYERS, D_HID), jnp.float32)
        be = jnp.zeros((N_LAYERS, D_HID), jnp.float32)
        bc = jnp.zeros((N_LAYERS, D_HID), jnp.float32)
        gamma = jnp.ones((N_LAYERS, D_HID), jnp.float32)
        beta = jnp.zeros((N_LAYERS, D_HID), jnp.float32)
        return {'node_feat': node_feat, 'edge_attr': edge_attr, 'src': src, 'dst': dst, 'Wn': Wn, 'bn': bn, 'We': We, 'be': be, 'Wc': Wc, 'bc': bc, 'gamma': gamma, 'beta': beta}
    _L0_gnn_all = _L0_gnn_setup()
    _L0_gnn_in = {k: v for k, v in _L0_gnn_all.items() if k in ('Wn', 'bn', 'We', 'be', 'Wc', 'bc', 'gamma', 'beta')}
    del _L0_gnn_all

    def _L0_mix_setup():
        import jax, jax.numpy as jnp
        import numpy as np
        DIM = 256
        HEADS = 4
        DIM_HEAD = 32
        NUM_MEM = 4
        HIDDEN = HEADS * DIM_HEAD
        SCALE = DIM_HEAD ** (-0.5)

        def rmsnorm(x, g):
            n = jnp.linalg.norm(x, axis=-1, keepdims=True)
            return x / jnp.maximum(n, 1e-12) * g * x.shape[-1] ** 0.5
        key = jax.random.key(seed)
        ks = jax.random.split(key, 8)
        B, N = (4, 512)
        return {'x': jax.random.normal(ks[0], (B, N, DIM), jnp.float32), 't': jax.random.normal(ks[1], (B,), jnp.float32), 'w_qkv': jax.random.normal(ks[2], (DIM, 3 * HIDDEN), jnp.float32) * 0.02, 'mem_kv': jax.random.normal(ks[3], (2, HEADS, DIM_HEAD, NUM_MEM), jnp.float32), 'w_out': jax.random.normal(ks[4], (HIDDEN, DIM), jnp.float32) * 0.02, 'b_out': jnp.zeros((DIM,), jnp.float32), 'g_out': jnp.ones((DIM,), jnp.float32), 'g_pre': jnp.ones((DIM,), jnp.float32)}
    _L0_mix_all = _L0_mix_setup()
    _L0_mix_in = {k: v for k, v in _L0_mix_all.items() if k in ('t', 'w_qkv', 'mem_kv', 'w_out', 'b_out', 'g_out', 'g_pre')}
    del _L0_mix_all

    def _L0_ffn_setup():
        import jax, jax.numpy as jnp
        import numpy as np
        INPUT_WIDTH = 256
        DEPTH = 7
        OUTPUT_WIDTH = 256
        N_NODES = 2 ** (DEPTH + 1) - 1
        key = jax.random.key(seed)
        k_x, k_w1, k_w2 = jax.random.split(key, 3)
        init1 = 1.0 / np.sqrt(INPUT_WIDTH)
        x = jax.random.normal(k_x, (2, 1024, INPUT_WIDTH), dtype=jnp.float32)
        w1s = jax.random.uniform(k_w1, (N_NODES, INPUT_WIDTH), jnp.float32, -init1, init1)
        b1s = jnp.zeros((N_NODES,), jnp.float32)
        w2s = jax.random.uniform(k_w2, (N_NODES, INPUT_WIDTH, OUTPUT_WIDTH), jnp.float32, -init1, init1)
        b2s = jnp.zeros((N_NODES, OUTPUT_WIDTH), jnp.float32)
        return {'x': x, 'w1s': w1s, 'b1s': b1s, 'w2s': w2s, 'b2s': b2s}
    _L0_ffn_all = _L0_ffn_setup()
    _L0_ffn_in = {k: v for k, v in _L0_ffn_all.items() if k in ('w1s', 'b1s', 'w2s', 'b2s')}
    del _L0_ffn_all
    return {'x': x, 'src': src, 'dst': dst, 'edge_attr_64': edge_attr_64, 'L0_gnn_Wn': _L0_gnn_in['Wn'], 'L0_gnn_bn': _L0_gnn_in['bn'], 'L0_gnn_We': _L0_gnn_in['We'], 'L0_gnn_be': _L0_gnn_in['be'], 'L0_gnn_Wc': _L0_gnn_in['Wc'], 'L0_gnn_bc': _L0_gnn_in['bc'], 'L0_gnn_gamma': _L0_gnn_in['gamma'], 'L0_gnn_beta': _L0_gnn_in['beta'], 'L0_mix_t': _L0_mix_in['t'], 'L0_mix_w_qkv': _L0_mix_in['w_qkv'], 'L0_mix_mem_kv': _L0_mix_in['mem_kv'], 'L0_mix_w_out': _L0_mix_in['w_out'], 'L0_mix_b_out': _L0_mix_in['b_out'], 'L0_mix_g_out': _L0_mix_in['g_out'], 'L0_mix_g_pre': _L0_mix_in['g_pre'], 'L0_ffn_w1s': _L0_ffn_in['w1s'], 'L0_ffn_b1s': _L0_ffn_in['b1s'], 'L0_ffn_w2s': _L0_ffn_in['w2s'], 'L0_ffn_b2s': _L0_ffn_in['b2s']}

def reference(x, src, dst, edge_attr_64, L0_gnn_Wn, L0_gnn_bn, L0_gnn_We, L0_gnn_be, L0_gnn_Wc, L0_gnn_bc, L0_gnn_gamma, L0_gnn_beta, L0_mix_t, L0_mix_w_qkv, L0_mix_mem_kv, L0_mix_w_out, L0_mix_b_out, L0_mix_g_out, L0_mix_g_pre, L0_ffn_w1s, L0_ffn_b1s, L0_ffn_w2s, L0_ffn_b2s):
    import jax
    import jax.numpy as jnp

    def _L0_gnn_ref(node_feat, edge_attr, src, dst, Wn, bn, We, be, Wc, bc, gamma, beta):
        import jax, jax.numpy as jnp
        import numpy as np
        N_NODES = 625
        N_EDGES = 10000
        D_IN = 256
        D_EDGE = 64
        D_HID = 256
        N_LAYERS = 3
        EPS = 1e-05

        def _conv(h, e, src, dst, Wn_l, bn_l, We_l, be_l, Wc_l, bc_l):
            hn = h @ Wn_l + bn_l
            et = e @ We_l + be_l
            m = hn[src] + et
            s = jax.ops.segment_sum(m, dst, num_segments=N_NODES)
            cnt = jax.ops.segment_sum(jnp.ones((m.shape[0],), m.dtype), dst, num_segments=N_NODES)
            agg = s / jnp.maximum(cnt, 1.0)[:, None]
            return jnp.concatenate([hn, agg], axis=1) @ Wc_l + bc_l

        def _layernorm(x, g, b):
            mu = jnp.mean(x, axis=-1, keepdims=True)
            var = jnp.mean(jnp.square(x - mu), axis=-1, keepdims=True)
            return (x - mu) / jnp.sqrt(var + EPS) * g + b
        h = node_feat
        for i in range(N_LAYERS):
            h = _conv(h, edge_attr, src, dst, Wn[i], bn[i], We[i], be[i], Wc[i], bc[i])
            h = jax.nn.relu(_layernorm(h, gamma[i], beta[i]))
        return h

    def _L0_mix_ref(x, t, w_qkv, mem_kv, w_out, b_out, g_out, g_pre):
        import jax, jax.numpy as jnp
        import numpy as np
        DIM = 256
        HEADS = 4
        DIM_HEAD = 32
        NUM_MEM = 4
        HIDDEN = HEADS * DIM_HEAD
        SCALE = DIM_HEAD ** (-0.5)

        def rmsnorm(x, g):
            n = jnp.linalg.norm(x, axis=-1, keepdims=True)
            return x / jnp.maximum(n, 1e-12) * g * x.shape[-1] ** 0.5
        b, n, c = x.shape
        xn = rmsnorm(x, g_pre)
        qkv = xn @ w_qkv
        q, k, v = jnp.split(qkv, 3, axis=-1)

        def to_heads(z):
            return z.reshape(b, n, HEADS, DIM_HEAD).transpose(0, 2, 3, 1)
        q, k, v = map(to_heads, (q, k, v))
        mk = jnp.broadcast_to(mem_kv[0], (b, HEADS, DIM_HEAD, NUM_MEM))
        mv = jnp.broadcast_to(mem_kv[1], (b, HEADS, DIM_HEAD, NUM_MEM))
        k = jnp.concatenate([mk, k], axis=-1)
        v = jnp.concatenate([mv, v], axis=-1)
        q = jax.nn.softmax(q, axis=-2) * SCALE
        k = jax.nn.softmax(k, axis=-1)
        context = jnp.einsum('bhdn,bhen->bhde', k, v)
        out = jnp.einsum('bhde,bhdn->bhen', context, q)
        out = out.transpose(0, 3, 1, 2).reshape(b, n, HIDDEN)
        out = rmsnorm(out @ w_out + b_out, g_out)
        return out + x

    def _L0_ffn_ref(x, w1s, b1s, w2s, b2s):
        import jax, jax.numpy as jnp
        import numpy as np
        INPUT_WIDTH = 256
        DEPTH = 7
        OUTPUT_WIDTH = 256
        N_NODES = 2 ** (DEPTH + 1) - 1
        B, S, D = x.shape
        flat_x = x.reshape(B * S, D)
        T = flat_x.shape[0]
        current = jnp.zeros((T,), dtype=jnp.int32)
        all_nodes = []
        all_logits = []
        for _ in range(DEPTH + 1):
            all_nodes.append(current)
            score = jnp.einsum('td,td->t', flat_x, w1s[current]) + b1s[current]
            all_logits.append(score)
            choice = ((jnp.sign(score) + 1.0) / 2.0).astype(jnp.int32)
            current = current * 2 + choice + 1
        logits = jnp.stack(all_logits, axis=1)
        path_weights = jax.nn.gelu(jnp.abs(logits), approximate=False)
        out = jnp.zeros((T, OUTPUT_WIDTH), dtype=x.dtype)
        for i in range(DEPTH + 1):
            nodes_i = all_nodes[i]
            t_i = jnp.einsum('td,tdo->to', flat_x, w2s[nodes_i]) + b2s[nodes_i]
            out = out + t_i * path_weights[:, i][:, None]
        return out.reshape(B, S, OUTPUT_WIDTH)
    xn = _layernorm(x, axis=-1)
    x = x + _L0_gnn_ref(xn, edge_attr_64, src, dst, L0_gnn_Wn, L0_gnn_bn, L0_gnn_We, L0_gnn_be, L0_gnn_Wc, L0_gnn_bc, L0_gnn_gamma, L0_gnn_beta) + _L0_mix_ref(xn[None], L0_mix_t, L0_mix_w_qkv, L0_mix_mem_kv, L0_mix_w_out, L0_mix_b_out, L0_mix_g_out, L0_mix_g_pre)[0]
    x = x + _L0_ffn_ref(_layernorm(x, axis=-1)[None], L0_ffn_w1s, L0_ffn_b1s, L0_ffn_w2s, L0_ffn_b2s)[0]
    return x

_drawn_inputs = setup_inputs


def setup_inputs(seed=0):
    import zlib

    import numpy as np

    out = dict(_drawn_inputs(seed))
    spreads = {'L0_gnn_bn': (0.0, 0.1),
     'L0_gnn_be': (0.0, 0.1),
     'L0_gnn_bc': (0.0, 0.1),
     'L0_gnn_gamma': (1.0, 0.2),
     'L0_gnn_beta': (0.0, 0.1),
     'L0_mix_b_out': (0.0, 0.1),
     'L0_mix_g_out': (1.0, 0.2),
     'L0_mix_g_pre': (1.0, 0.6),
     'L0_ffn_b1s': (0.0, 0.1),
     'L0_ffn_b2s': (0.0, 0.1)}
    factors = {'L0_mix_w_qkv': 3.963, 'L0_mix_mem_kv': 8.0, 'L0_mix_w_out': 3.094}
    for name, (base, spread) in spreads.items():
        noise = np.random.default_rng([zlib.crc32(name.encode()), seed]).standard_normal(out[name].shape)
        drawn = base * np.exp(spread * noise) if base else spread * noise
        out[name] = jnp.asarray(drawn.astype(out[name].dtype))
    for name, factor in factors.items():
        out[name] = (out[name] * factor).astype(out[name].dtype)
    return out
```

```python
import numpy as np
import concourse.bass as bass
from concourse import mybir
from contextlib import ExitStack

F32 = mybir.dt.float32
BF16 = mybir.dt.bfloat16
F16 = mybir.dt.float16
I32 = mybir.dt.int32
ALU = mybir.AluOpType
ACT = mybir.ActivationFunctionType
AX = mybir.AxisListType

N = 625
D = 256
TP = 125
NT = N // TP
DE = 64
E = 20625
EC = 5
NG = E // (TP * EC)
NL = 3
H, DH, MEM = 4, 32, 4
HID = H * DH
LEVELS = 8
NODES = 2 ** LEVELS - 1
LEAVES = 2 ** (LEVELS - 1)
WIN = 128
NW = 5
R = NW * WIN
RES = 3
NRES = 2 ** RES - 1
RING = 12
NLHS = 3
EPS_LN = 1e-5
EPS_NORM = 1e-12

UNITS = [2 ** l + NW - 1 for l in range(LEVELS)]
BASE = [sum(UNITS[:l]) for l in range(LEVELS + 1)]
U = BASE[-1]
U_RES = BASE[RES]


class Lane:

    def __init__(self, sem):
        self.sem, self.n, self.queue = sem, 0, []

    def do(self, make, *after, mark=True):
        def emit(eng):
            for sem, value in after:
                eng.wait_ge(sem, value)
            ins = make(eng)
            if mark:
                ins.then_inc(self.sem, 1)
        self.queue.append(emit)
        self.n += mark
        return (self.sem, self.n)

    def run(self, emit):
        self.queue.append(emit)


def graph_layer(nc, x, src, dst, edge, Wn, bn, We, be, Wc, bc, gamma, beta, w_qkv, mem_kv, w_out, b_out, g_out,
                g_pre, w1s, b1s, w2s, b2s, out):
    ctx = ExitStack()
    with ctx:
        def sem(name):
            return ctx.enter_context(nc.semaphore(name))

        def sb(name, shape, dt=F32):
            return ctx.enter_context(nc.sbuf_tensor(name, shape, dt))

        xin = sb("xin", [TP, NT, D])
        xn = sb("xn", [TP, NT, D])
        acc = sb("acc", [TP, NT, D])
        hT = sb("hT", [128, 2, N])
        W12 = sb("W12", [128, 2, NL, 2 * D])
        rhs_aug = sb("rhs_aug", [66, NL, D])
        gT = sb("gT", [128, 2, NL])
        bT = sb("bT", [128, 2, NL])
        gamma_b = sb("gamma_b", [TP, D])
        beta_b = sb("beta_b", [TP, D])
        gout_b = sb("gout_b", [TP, D])
        bout_b = sb("bout_b", [TP, D])
        b1_b = sb("b1_b", [TP, NODES])
        w1T = sb("w1T", [128, 2, 256])
        b2t = sb("b2t", [128, 2, D])
        ident = sb("ident", [128, 128])
        ones_b = sb("ones_b", [128, 128], BF16)
        zeros_b = sb("zeros_b", [128, 512], BF16)
        below = sb("below", [TP, TP], BF16)
        iota = sb("iota", [128, R], F16)
        cnt = sb("cnt", [TP, 4, NT])
        rc = sb("rc", [TP, NT])
        stats = sb("stats", [TP, NT, 6])
        mv = sb("mv", [TP, NT, 2])
        rv = sb("rv", [TP, 2, NT])
        rstd = sb("rstd", [TP, NT])
        tabs = sb("tabs", [1, 4, U], I32)
        w_res = sb("w_res", [128, NRES, 2, D])
        lhs = sb("lhs", [128, NLHS, 2, WIN])
        nid = sb("nid", [128, U])
        idxT = sb("idxT", [TP, 2, EC, NG])
        tiles_i = sb("tiles_i", [1, 2, NG], I32)

        reg_edge = sb("reg_edge", [128, NG * EC * DE])
        reg_hot = sb("reg_hot", [128, 9600])
        reg_mat = sb("reg_mat", [128, NT * N])
        reg_ring = sb("reg_ring", [128, RING * 2 * D])
        esplit = sb("esplit", [TP, 3, 3, EC * DE], BF16)

        def part(region, at, p, *dims):
            n = int(np.prod(dims))
            names = "abcd"[:len(dims)]
            flat = region[0:p, at:at + n]
            if len(dims) == 1:
                return flat
            return flat.rearrange(f"p ({' '.join(names)}) -> p {' '.join(names)}", **dict(zip(names, dims)))

        xin_flat = xin[:, :, :].rearrange("p t d -> p (t d)")
        erest = xin_flat[:, 0:3 * EC * DE].rearrange("p (b c) -> p b c", b=3)
        ET = xin_flat[0:66, 0:N]
        rows = xin_flat[0:9, 0:R]
        W12_flat = W12[:, :, :, :].rearrange("p k l d -> p (k l d)")
        gwT = W12_flat[:, 0:2 * N].rearrange("p (k t) -> p k t", k=2)
        xsT = W12_flat[:, 2 * N:2 * N + 2 * R].rearrange("p (k r) -> p k r", k=2)
        sel = part(reg_hot, 8320, 9, 9, 128)
        e_all = part(reg_edge, 0, TP, NG, EC * DE)
        AT = part(reg_edge, 0, TP, NT, N)
        Ec = part(reg_edge, 3125, TP, NL, NT, D)
        z1 = part(reg_edge, 6965, TP, NT, D)
        z2 = part(reg_edge, 8245, TP, NT, D)
        xhat = part(reg_hot, 0, TP, NT, D)
        y = part(reg_hot, 1280, TP, NT, D)
        xs = part(reg_edge, 0, 128, 2, LEVELS * R)
        hot = reg_hot[0:TP, :].bitcast(BF16).rearrange("p (b j c r) -> p b j c r", b=3, j=2, c=EC)
        qkv = part(reg_hot, 0, TP, NT, 3 * HID)
        Ek = part(reg_hot, 1920, TP, NT, HID)
        qT = part(reg_hot, 2560, HID, N)
        mo = part(reg_hot, 3185, TP, NT, D)
        xx = part(reg_hot, 4465, TP, NT, D)
        small = reg_hot[:, 5745:5745 + 1500]
        sq = part(reg_hot, 0, TP, NT, D)
        nrow = reg_hot[:, 0:LEVELS * R].bitcast(I32).rearrange("p (l r) -> p l r", l=LEVELS)
        nrow_flat = reg_hot[:, 0:LEVELS * R].bitcast(I32)
        Pm = part(reg_hot, 5120, TP, NT, R)
        idxf = part(reg_hot, 0, NG, 2, N)
        idxi = reg_hot[0:NG, 1250:2500].bitcast(I32).rearrange("p (j e) -> p j e", j=2)
        WnT = part(reg_mat, 0, 128, 2, NL, D)
        lhs_e = part(reg_mat, 1536, 128, 2, NL, 66)
        lhs_n = part(reg_mat, 1932, 128, 2, NL, 66)
        A = part(reg_mat, 0, TP, NT, N)
        PmT = part(reg_mat, 0, 128, NW, N)
        wn = part(reg_ring, 0, 128, 2, NL, D)
        wc = part(reg_ring, 1536, 128, 4, NL, D)
        we = part(reg_ring, 4608, DE, NL, D)
        wq = part(reg_ring, 5376, 128, 2, 3 * HID)
        ring = part(reg_ring, 0, 128, RING, 2, D)
        w1 = sb("w1", [128, 2, D])
        wo = sb("wo", [HID, D])
        gpT = sb("gpT", [128, 2])
        bnT = sb("bnT", [128, 2, NL])
        beT = sb("beT", [128, 2, NL])
        bcr = sb("bcr", [1, NL, D])
        e65 = sb("e65", [1, 66])
        bd = sb("bd", [HID, HID])
        mk = sb("mk", [HID, MEM])
        mkT = sb("mkT", [MEM, HID])
        mvT = sb("mvT", [MEM, HID])
        E_sb = sb("E_sb", [TP, NT, 66])

        ps = ctx.enter_context(nc.psum_tensor("ps", [128, 8, 512], F32))
        ps_flat = ps[:, :, :].rearrange("p b c -> p (b c)")

        V, S, G, T = Lane(sem("v_done")), Lane(sem("s_done")), Lane(sem("g_done")), Lane(sem("t_done"))
        Y = Lane(sem("y_unused"))

        def load(lane, name, to, frm, slow=False):
            s = sem(f"in_{name}")

            def emit(eng):
                eng.dma_start(to, frm, allow_slow_non_contiguous=slow).then_inc(s, 16)
            lane.run(emit)
            return (s, 16)

        def mm(to, lhsT, rhs, start, stop, *after, mark=False):
            return T.do(lambda e: e.matmul(to, lhsT, rhs, start=start, stop=stop, skip_group_check=True),
                        *after, mark=mark)

        def tr(to, frm, k, *after, mark=False):
            return T.do(lambda e: e.transpose(to, frm, ident[0:k, 0:k]), *after, mark=mark)

        groups = "(g e) -> g e"
        t_src = load(Y, "src", idxi[:, 0, :], src.rearrange(groups, g=NG))
        t_dst = load(Y, "dst", idxi[:, 1, :], dst.rearrange(groups, g=NG))
        t_x = load(Y, "x", xin[:, :, :], x.rearrange("(t p) d -> p t d", p=TP))
        t_wq = load(Y, "wq", wq, w_qkv.rearrange("(k p) d -> p k d", p=128))
        t_wn = [load(Y, f"wn{l}", wn[:, :, l, :], Wn[l].rearrange("(k p) d -> p k d", p=128)) for l in range(NL)]
        t_wc = [load(Y, f"wc{l}", wc[:, :, l, :], Wc[l].rearrange("(k p) d -> p k d", p=128)) for l in range(NL)]
        t_we = load(Y, "we", we, We.rearrange("l p d -> p l d"))
        t_e = []
        per = NG // 3
        for q in range(3):
            part_e = edge[q * per * EC * TP:(q + 1) * per * EC * TP, :]
            t_e.append(load(Y, f"e{q}", e_all[:, q * per:(q + 1) * per, :],
                            part_e.rearrange("(g p c) f -> p g (c f)", g=per, c=EC)))
        t_w1 = [load(Y, "w1a", w1[:, 0, :], w1s[0:128, :]), load(Y, "w1b", w1[0:127, 1, :], w1s[128:NODES, :])]
        t_b2 = [load(Y, "b2a", b2t[:, 0, :], b2s[0:128, :]), load(Y, "b2b", b2t[0:127, 1, :], b2s[128:NODES, :])]
        t_res = [load(Y, f"res{l}", w_res[:, 2 ** l - 1:2 ** (l + 1) - 1, :, :],
                      w2s[2 ** l - 1:2 ** (l + 1) - 1, :, :].rearrange("n (k p) d -> p n k d", p=128))
                 for l in range(RES)]

        t_gp = load(S, "gp", gpT[:, :], g_pre.rearrange("(k p) -> p k", p=128), True)
        t_mk = load(S, "mk", mk[:, :], mem_kv[0].rearrange("h d m -> (h d) m"))
        t_mkT = load(S, "mkT", mkT[:, :], mem_kv[0].rearrange("h d m -> m (h d)"), True)
        t_mvT = load(S, "mvT", mvT[:, :], mem_kv[1].rearrange("h d m -> m (h d)"), True)
        vec = {}
        for name, to, frm in (("bn", bnT, bn), ("be", beT, be), ("g", gT, gamma), ("b", bT, beta)):
            for k in range(2):
                vec[name, k] = load(S, f"{name}{k}", to[:, k, :],
                                    frm[:, k * 128:(k + 1) * 128].rearrange("l p -> p l"), True)
        t_wo = load(S, "wo", wo[:, :], w_out)
        t_bc = load(S, "bc", bcr[:, :, :], bc.unsqueeze(0))
        t_bo = load(S, "bout", bout_b[:, :], b_out.partition_broadcast(TP))
        t_go = load(S, "go", gout_b[:, :], g_out.partition_broadcast(TP))
        t_gl = load(S, "gl", gamma_b[:, :], gamma[NL - 1].partition_broadcast(TP))
        t_bl = load(S, "bl", beta_b[:, :], beta[NL - 1].partition_broadcast(TP))
        t_b1 = load(S, "b1s", b1_b[:, :], b1s.partition_broadcast(TP))

        g0 = G.do(lambda e: e.memset(ident[:, :], 0.0))
        t_id = G.do(lambda e: e.affine_select(out=ident[:, :], in_=ident[:, :], compare_op=ALU.not_equal, fill=1.0,
                                              base=0, pattern=[[-1, 128]], channel_multiplier=1), g0)
        t_io = G.do(lambda e: e.iota(iota[:, :], [[1, R]], base=0, channel_multiplier=0,
                                     allow_small_or_imprecise_dtypes=True))
        g0 = G.do(lambda e: e.memset(below[:, :], 1.0))
        t_be = G.do(lambda e: e.affine_select(out=below[:, :], in_=below[:, :], compare_op=ALU.is_gt, fill=0.0,
                                              base=0, pattern=[[1, TP]], channel_multiplier=-1), g0)
        row0 = sb("row0", [128, 1])
        t_row = G.do(lambda e: e.iota(row0[:, :], [[0, 1]], base=0, channel_multiplier=1,
                                      allow_small_or_imprecise_dtypes=True))
        kk = sb("kk", [128, U])
        for l in range(LEVELS):
            t_kk = G.do(lambda e, l=l: e.iota(kk[:, BASE[l]:BASE[l + 1]], [[1, UNITS[l]]], base=0,
                                              channel_multiplier=0, allow_small_or_imprecise_dtypes=True))
        t_one = G.do(lambda e: e.memset(ones_b[:, :], 1.0))
        ones = sb("ones", [128, 128])
        t_onef = G.do(lambda e: e.memset(ones[:, :], 1.0))
        t_zero = G.do(lambda e: e.memset(zeros_b[:, :], 0.0))
        t_lz = G.do(lambda e: e.memset(reg_mat[:, 1536:1536 + 792], 0.0))
        g0 = G.do(lambda e: e.memset(e65[:, :], 0.0))
        t_e65 = G.do(lambda e: e.memset(e65[:, 65:66], 1.0), g0)
        g0 = G.do(lambda e: e.memset(bd[:, :], 0.0))
        for h in range(H):
            t_bd = g0 = G.do(lambda e, h=h: e.memset(bd[h * DH:(h + 1) * DH, h * DH:(h + 1) * DH], DH ** -0.5), g0)

        i0 = V.do(lambda e: e.tensor_copy(idxf, idxi), t_src, t_dst)
        lim = small[0:NG, 0:2]
        tl = small[0:NG, 2:4]
        v0 = V.do(lambda e: e.tensor_reduce(out=lim[:, 0:1], in_=idxf[:, 1, :], axis=AX.X, op=ALU.min), i0)
        v0 = V.do(lambda e: e.tensor_reduce(out=lim[:, 1:2], in_=idxf[:, 1, :], axis=AX.X, op=ALU.max), i0)
        v0 = V.do(lambda e: e.tensor_scalar(tl[:, 0:1], lim[:, 0:1], float(TP), None, ALU.is_ge), v0)
        v0 = V.do(lambda e: e.tensor_scalar(tl[:, 1:2], lim[:, 1:2], float(TP), 1.0, ALU.is_ge, ALU.add), v0)
        for k in range(2, NT):
            v0 = V.do(lambda e, k=k: e.scalar_tensor_tensor(out=tl, in0=lim, scalar=float(k * TP), in1=tl,
                                                            op0=ALU.is_ge, op1=ALU.add), v0)
        for j in range(2):
            for c in range(EC):
                tr(ps[0:TP, 0, (j * EC + c) * NG:(j * EC + c + 1) * NG],
                   idxf[:, j, :].rearrange("g (p c) -> g c p", c=EC)[:, c, :], NG, t_id, i0)
        tr(ps[0:1, 1, 0:NG], tl[:, 0:1], NG, v0)
        p_idx = tr(ps[0:1, 1, NG:2 * NG], tl[:, 1:2], NG, mark=True)
        t_idx = V.do(lambda e: e.tensor_copy(idxT[:, :, :, :].rearrange("p j c g -> p (j c g)"),
                                             ps[0:TP, 0, 0:2 * EC * NG]), p_idx)
        t_til = V.do(lambda e: e.tensor_copy(tiles_i[:, :, :].rearrange("p j g -> p (j g)"), ps[0:1, 1, 0:2 * NG]))
        idx_free = t_til

        def norm(frm, to, *after):
            for i in range(NT):
                a = V.do(lambda e, i=i: e.bn_stats(stats[:, i, :], frm[:, i, :]), *after)
            for i in range(NT):
                a2 = V.do(lambda e, i=i: e.bn_aggr(mv[:, i, :], stats[:, i, :]), a)
            a = V.do(lambda e: e.tensor_scalar(rv[:, 0, :], mv[:, :, 1], EPS_LN, None, ALU.add), a2)
            a = V.do(lambda e: e.reciprocal(rv[:, 1, :], rv[:, 0, :]), a)
            b = S.do(lambda e: e.activation(rstd[:, :], rv[:, 1, :], ACT.Sqrt), a)
            last = []
            for i in range(NT):
                last.append(V.do(lambda e, i=i: e.tensor_scalar(to[:, i, :], frm[:, i, :], mv[:, i, 0:1],
                                                                rstd[:, i:i + 1], ALU.subtract, ALU.mult), b))
            return last

        t_xn = norm(xin, xn, t_x)

        t_col = None
        for l in range(NL):
            for k in range(2):
                t_col = V.do(lambda e, l=l, k=k: e.tensor_tensor(lhs_e[:, k, l, 64:65], bnT[:, k, l:l + 1],
                                                                 beT[:, k, l:l + 1], ALU.add),
                             t_lz, vec["bn", k], vec["be", k])
                t_col = V.do(lambda e, l=l, k=k: e.tensor_copy(lhs_n[:, k, l, 65:66], bnT[:, k, l:l + 1]))
        ev = {}
        for l in range(NL):
            b = 2 + l % 2
            for f in range(2):
                for k in range(2):
                    p = tr(ps[:, b, f * 256 + k * 128:f * 256 + (k + 1) * 128], wn[:, k, l, f * 128:(f + 1) * 128], 128,
                           t_wn[l], t_id, *([ev[l - 2]] if l >= 2 else []), mark=(f == 1 and k == 1))
            ev[l] = S.do(lambda e, l=l, b=b: e.copy(WnT[:, :, l, :], ps[:, b, :].rearrange("p (f k) -> p f k", f=2)),
                         p, t_lz)
            for f in range(2):
                p = tr(ps[:, 6, (l * 2 + f) * DE:(l * 2 + f + 1) * DE], we[:, l, f * 128:(f + 1) * 128], DE, t_we,
                       mark=True)
        s_we = S.do(lambda e: e.copy(lhs_e[:, :, :, 0:DE].rearrange("p f l c -> p l f c"),
                                     ps[:, 6, 0:NL * 2 * DE].rearrange("p (l f c) -> p l f c", l=NL, f=2)), p, t_lz)
        free = {4: None, 5: None, 7: None}
        for l in range(NL):
            for k in range(2):
                b = 4 + k
                for half in range(2):
                    for f in range(2):
                        p = mm(ps[:, b, half * D:(half + 1) * D], WnT[:, f, l, k * 128:(k + 1) * 128],
                               wc[:, 2 * half + f, l, :], f == 0, f == 1, ev[l], t_wc[l],
                               *([free[b]] if free[b] else []), mark=(half == 1 and f == 1))
                free[b] = S.do(lambda e, l=l, k=k, b=b: e.copy(W12[:, k, l, :], ps[:, b, :]), p)
            for f in range(2):
                mm(ps[0:66, 7, 0:D], lhs_e[:, f, l, :], wc[:, 2 + f, l, :], f == 0, False, s_we, t_col,
                   *([free[7]] if free[7] else []))
            for f in range(2):
                mm(ps[0:66, 7, 0:D], lhs_n[:, f, l, :], wc[:, f, l, :], False, False)
            p = mm(ps[0:66, 7, 0:D], e65[:, :], bcr[:, l, :], False, True, t_e65, t_bc, mark=True)
            free[7] = S.do(lambda e, l=l: e.copy(rhs_aug[:, l, :], ps[0:66, 7, 0:D]), p)
        t_W12, t_raug = free[5], free[7]

        for k in range(2):
            tr(ps[:, 0, k * 256:k * 256 + 128], w1[:, 0, k * 128:(k + 1) * 128], 128, t_w1[0], t_idx)
            p = tr(ps[:, 0, k * 256 + 128:k * 256 + 255], w1[0:127, 1, k * 128:(k + 1) * 128], 127, t_w1[1], mark=True)
        t_w1T = S.do(lambda e: e.copy(w1T[:, :, 0:NODES], ps[:, 0, :].rearrange("p (k n) -> p k n", k=2)[:, :, 0:NODES]),
                     p)

        def to_feature_major(frm, to, banks, when, free_at):
            done = []
            for i in range(NT):
                b = banks[i % 2]
                for k in range(2):
                    p = tr(ps[:, b, k * TP:(k + 1) * TP], frm[:, i, k * 128:(k + 1) * 128], TP, when[i],
                           *(done[i - 2:i - 1] if i >= 2 else free_at), mark=(k == 1))
                done.append(S.do(lambda e, i=i, b=b: e.copy(to[:, :, i * TP:(i + 1) * TP],
                                                            ps[:, b, 0:2 * TP].rearrange("p (k t) -> p k t", k=2)), p))
            return done

        for k in range(2):
            t_wqg = V.do(lambda e, k=k: e.tensor_scalar(wq[:, k, :], wq[:, k, :], gpT[:, k:k + 1], None, ALU.mult),
                         t_wq, t_gp)
        t_xnT = to_feature_major(xn, hT, (2, 3), t_xn, [ev[1], ev[2]])
        ss = small[0:TP, 8:8 + NT]
        nrm = small[0:TP, 16:16 + NT]
        s16 = small[0:TP, 24:24 + NT]
        for i in range(NT):
            a = S.do(lambda e, i=i: e.activation(mo[:, i, :], xn[:, i, :], ACT.Square, accum_out=ss[:, i:i + 1]), t_xn[i],
                     idx_free)
        a = S.do(lambda e: e.activation(nrm, ss, ACT.Sqrt), a)
        a = V.do(lambda e: e.tensor_scalar(nrm, nrm, EPS_NORM, float(1.0 / np.sqrt(D)), ALU.max, ALU.mult), a)
        t_s16 = V.do(lambda e: e.reciprocal(s16, nrm), a)
        t_xx = G.do(lambda e: e.tensor_tensor(xx, xin[:, :, :], xn[:, :, :], ALU.add), t_xn[-1], idx_free, t_bd)
        q_ev = []
        for i in range(NT):
            b = 4 + i % 2
            for k in range(2):
                p = mm(ps[0:TP, b, 0:3 * HID], hT[:, k, i * TP:(i + 1) * TP], wq[:, k, :], k == 0, k == 1, t_wqg,
                       t_xnT[i], free[4], free[5], *(q_ev[i - 2:i - 1]), mark=(k == 1))
            q_ev.append(S.do(lambda e, i=i, b=b: e.activation(qkv[:, i, :], ps[0:TP, b, 0:3 * HID], ACT.Copy,
                                                              scale=s16[:, i:i + 1]), p, t_s16, idx_free))
        km = small[:, 32:36]
        for i in range(NT):
            b, c = (6, i) if i < 4 else (7, 0)
            p = tr(ps[:, b, c * TP:(c + 1) * TP], qkv[:, i, HID:2 * HID], TP, q_ev[i], s_we, t_raug, mark=True)
        V.do(lambda e: e.tensor_reduce(out=km[:, 0:1], in_=ps[:, 6, 0:4 * TP], axis=AX.X, op=ALU.max), p)
        V.do(lambda e: e.tensor_reduce(out=km[:, 1:2], in_=ps[:, 7, 0:TP], axis=AX.X, op=ALU.max))
        a = V.do(lambda e: e.tensor_reduce(out=km[:, 2:3], in_=mk[:, :], axis=AX.X, op=ALU.max), t_mk)
        a = V.do(lambda e: e.tensor_reduce(out=km[:, 3:4], in_=km[:, 0:3], axis=AX.X, op=ALU.max), a)
        kdiag = small[:, 40:168]
        a = V.do(lambda e: e.tensor_scalar(kdiag, ident[:, :], km[:, 3:4], None, ALU.mult), a, t_id)
        p_kmax = mm(ps[:, 0, 0:HID], ones[:, :], kdiag, True, True, a, t_onef, t_w1T, mark=True)
        qv = qkv[:, :, 0:HID].rearrange("p t (h d) -> p t h d", h=H)
        qs = small[0:TP, 176:176 + NT * H]
        qb = qs.rearrange("p (t h) -> p t h", t=NT).unsqueeze(3).broadcast_to([TP, NT, H, DH])
        a = V.do(lambda e: e.tensor_reduce(out=qs.rearrange("p (t h) -> p t h", t=NT), in_=qv, axis=AX.X, op=ALU.max),
                 q_ev[-1])
        a = V.do(lambda e: e.tensor_tensor(qv, qv, qb, ALU.subtract), a)
        a = S.do(lambda e: e.activation(qkv[:, :, 0:HID], qkv[:, :, 0:HID], ACT.Exp), a)
        Em = small[0:MEM, 200:200 + HID]
        V.do(lambda e: e.tensor_tensor(Em, mkT[:, :], ps[0:MEM, 0, 0:HID], ALU.subtract), p_kmax, t_mkT)
        v1 = V.do(lambda e: e.tensor_tensor(Ek, qkv[:, :, HID:2 * HID],
                                            ps[0:TP, 0, 0:HID].unsqueeze(1).broadcast_to([TP, NT, HID]), ALU.subtract),
                  p_kmax, idx_free)
        S.do(lambda e: e.activation(Em, Em, ACT.Exp), v1)
        s_E = S.do(lambda e: e.activation(Ek, Ek, ACT.Exp))
        a = V.do(lambda e: e.tensor_reduce(out=qs.rearrange("p (t h) -> p t h", t=NT), in_=qv, axis=AX.X, op=ALU.add),
                 a)
        a = V.do(lambda e: e.reciprocal(qs, qs), a)
        v_q = V.do(lambda e: e.tensor_tensor(qv, qv, qb, ALU.mult), a)
        for i in range(NT):
            mm(ps[:, 1, 0:HID], qkv[:, i, 2 * HID:], Ek[:, i, :], i == 0, False, s_E, t_til)
        p_ctx = mm(ps[:, 1, 0:HID], mvT[:, :], Em, False, True, t_mvT, mark=True)
        for i in range(NT):
            mm(ps[:, 2, 0:1], Ek[:, i, :], ones[0:TP, 0:1], i == 0, False, t_xnT[-1], t_xnT[-2])
        p_ks = mm(ps[:, 2, 0:1], Em, ones[0:MEM, 0:1], False, True, mark=True)
        ctxm = small[:, 340:340 + HID]
        rks = small[:, 330:331]
        a1 = V.do(lambda e: e.tensor_tensor(ctxm, ps[:, 1, 0:HID], bd[:, :], ALU.mult), p_ctx, t_bd)
        a2 = V.do(lambda e: e.reciprocal(rks, ps[:, 2, 0:1]), p_ks)
        p = mm(ps[:, 3, 0:D], ctxm, wo[:, :], True, True, a1, t_wo, mark=True)
        ctxw = small[:, 480:480 + D]
        v_cw = V.do(lambda e: e.tensor_scalar(ctxw, ps[:, 3, 0:D], rks, None, ALU.mult), p, a2)
        for i in range(NT):
            b, c = (4, i) if i < 4 else (5, 0)
            p = tr(ps[:, b, c * TP:(c + 1) * TP], qkv[:, i, 0:HID], TP, v_q, q_ev[-1], mark=True)
        S.do(lambda e: e.copy(qT[:, 0:4 * TP], ps[:, 4, 0:4 * TP]), p, idx_free)
        s_qT = S.do(lambda e: e.copy(qT[:, 4 * TP:], ps[:, 5, 0:TP]))
        ss2 = small[0:TP, 740:740 + NT]
        v_mo = []
        for i in range(NT):
            b = 6 + i % 2
            p = mm(ps[0:TP, b, 0:D], qT[:, i * TP:(i + 1) * TP], ctxw, True, True, s_qT, v_cw, *(v_mo[i - 2:i - 1]),
                   mark=True)
            v_mo.append(V.do(lambda e, i=i, b=b: e.tensor_tensor(mo[:, i, :], ps[0:TP, b, 0:D], bout_b[:, :], ALU.add),
                             p, t_bo))
            a = S.do(lambda e, i=i: e.activation(sq[:, i, :], mo[:, i, :], ACT.Square, accum_out=ss2[:, i:i + 1]), v_mo[i])
        a = S.do(lambda e: e.activation(ss2, ss2, ACT.Sqrt), a)
        a = V.do(lambda e: e.tensor_scalar(ss2, ss2, EPS_NORM, float(1.0 / np.sqrt(D)), ALU.max, ALU.mult), a)
        a = V.do(lambda e: e.reciprocal(ss2, ss2), a)
        for i in range(NT):
            b2 = V.do(lambda e, i=i: e.scalar_tensor_tensor(out=mo[:, i, :], in0=mo[:, i, :], scalar=ss2[:, i:i + 1],
                                                            in1=gout_b[:, :], op0=ALU.mult, op1=ALU.mult), a, t_go)
        t_acc = V.do(lambda e: e.tensor_tensor(acc[:, :, :], mo, xx, ALU.add), b2, t_xx)

        s_hot, s_hotfree, s_hi, s_r1, s_mid, s_esp = (sem(n) for n in
                                                     ("hot", "hotfree", "ehi", "erest1", "emid", "esplit"))
        for b in range(8):
            p_z = mm(ps[:, b, :], zeros_b[:, 0:128], zeros_b[:, :], True, True, t_zero, t_acc, s_qT, t_xnT[-1],
                     t_raug, mark=True)

        def edges_pe(e):
            e.sem_inc(s_hotfree, 3)
            with e.Fori(0, NG // 3) as it:
                for b in range(3):
                    g = it * 3 + b
                    lo = e.value_load(tiles_i[0:1, 0, bass.ds(g, 1)], min_val=0, max_val=NT - 1)
                    hi = e.value_load(tiles_i[0:1, 1, bass.ds(g, 1)], min_val=1, max_val=NT)
                    with e.Fori(lo, hi) as t:
                        e.wait_ge(s_hot, g + 1)
                        e.wait_ge(s_esp, g + 1)
                        for c in range(EC):
                            lhsT = hot[:, b, 1, c, bass.ds(t * TP, TP)]
                            e.matmul(ps_flat[0:TP, bass.ds(t * 512, 512)], lhsT, hot[:, b, 0, c, 0:512],
                                     start=False, stop=False, skip_group_check=True)
                            e.matmul(ps_flat[0:TP, bass.ds(t * 256 + 2560, N - 512)], lhsT, hot[:, b, 0, c, 512:N],
                                     start=False, stop=False, skip_group_check=True)
                            for q in range(3):
                                e.matmul(ps_flat[0:TP, bass.ds(t * 256 + 2560 + N - 512, DE)], lhsT,
                                         esplit[:, b, q, c * DE:(c + 1) * DE],
                                         start=False, stop=False, skip_group_check=True)
                    e.drain().then_inc(s_hotfree, 1)
        T.run(lambda e: e.wait_ge(*t_til))
        T.run(edges_pe)
        edges_done = (s_hotfree, 3 + NG)

        def edges_dve(e):
            e.wait_ge(*p_z)
            with e.Fori(0, NG // 3) as it:
                for b in range(3):
                    g = it * 3 + b
                    e.wait_ge(s_hotfree, g + 1)
                    for j in range(2):
                        for c in range(EC):
                            ins = e.tensor_scalar(hot[:, b, j, c, :], iota[0:TP, :], idxT[:, j, c, bass.ds(g, 1)],
                                                  None, ALU.is_equal)
                    ins.then_inc(s_hot, 1)
        V.run(lambda e: e.wait_ge(*t_io))
        V.run(lambda e: e.wait_ge(*t_idx))
        V.run(edges_dve)

        def edges_act(e):
            for q in range(3):
                e.wait_ge(*t_e[q])
            with e.Fori(0, NG // 3) as it:
                for b in range(3):
                    g = it * 3 + b
                    e.wait_ge(s_hotfree, g + 1)
                    e.copy(esplit[:, b, 0, :], e_all[:, bass.ds(g, 1), :].rearrange("p o c -> p (o c)")).then_inc(s_hi, 1)
                    e.wait_ge(s_r1, g + 1)
                    e.copy(esplit[:, b, 1, :], erest[:, b, :]).then_inc(s_mid, 1)
        S.run(edges_act)

        def edges_pool(e):
            with e.Fori(0, NG // 3) as it:
                for b in range(3):
                    g = it * 3 + b
                    e.wait_ge(s_hi, g + 1)
                    e.tensor_tensor(erest[:, b, :], e_all[:, bass.ds(g, 1), :].rearrange("p o c -> p (o c)"),
                                    esplit[:, b, 0, :], ALU.subtract).then_inc(s_r1, 1)
                    e.wait_ge(s_mid, g + 1)
                    e.tensor_tensor(esplit[:, b, 2, :], erest[:, b, :], esplit[:, b, 1, :],
                                    ALU.subtract).then_inc(s_esp, 1)
        G.run(edges_pool)

        for t in range(NT):
            a = S.do(lambda e, t=t: e.activation(A[:, t, 0:512], ps[0:TP, t, :], ACT.Copy,
                                                 accum_out=cnt[:, 0, t:t + 1]), edges_done)
        s_A = a
        tail = ps_flat[0:TP, 2560:2560 + NT * 256].rearrange("p (t c) -> p t c", t=NT)
        V.do(lambda e: e.tensor_copy(A[:, :, 512:N], tail[:, :, 0:N - 512]), edges_done)
        v_A = V.do(lambda e: e.tensor_reduce(out=cnt[:, 1, :], in_=tail[:, :, 0:N - 512], axis=AX.X, op=ALU.add))
        a = V.do(lambda e: e.tensor_tensor(cnt[:, 2, :], cnt[:, 0, :], cnt[:, 1, :], ALU.add), v_A, s_A)
        a2 = V.do(lambda e: e.tensor_scalar(cnt[:, 3, :], cnt[:, 2, :], 1.0, None, ALU.max), a)
        v_rc = V.do(lambda e: e.reciprocal(rc[:, :], cnt[:, 3, :]), a2)
        a = V.do(lambda e: e.tensor_tensor(E_sb[:, :, 0:DE], tail[:, :, N - 512:N - 512 + DE],
                                           rc[:, :].unsqueeze(2).broadcast_to([TP, NT, DE]), ALU.mult), v_rc)
        a = V.do(lambda e: e.tensor_tensor(E_sb[:, :, 64], rc[:, :], cnt[:, 2, :], ALU.mult), v_rc)
        v_E = V.do(lambda e: e.memset(E_sb[:, :, 65:66], 1.0))
        at_ev = []
        for j in range(NT):
            b = 2 * (j % 2)
            for i in range(NT):
                to = ps[0:TP, b, i * TP:(i + 1) * TP] if i < 4 else ps[0:TP, b + 1, 0:TP]
                p = tr(to, A[:, i, j * TP:(j + 1) * TP], TP, s_A, v_A, *(at_ev[j - 2:j - 1]), mark=(i == NT - 1))
            S.do(lambda e, j=j, b=b: e.copy(AT[:, j, 0:4 * TP], ps[0:TP, b, 0:4 * TP]), p)
            at_ev.append(S.do(lambda e, j=j, b=b: e.copy(AT[:, j, 4 * TP:], ps[0:TP, b + 1, 0:TP])))
        t_AT = at_ev[-1]
        for i in range(NT):
            b, c = (4, i) if i < 4 else (5, 0)
            p = tr(ps[0:66, b, c * TP:(c + 1) * TP], E_sb[:, i, :], TP, v_E, s_A, mark=True)
        V.do(lambda e: e.tensor_copy(ET[:, 0:4 * TP], ps[0:66, 4, 0:4 * TP]), p)
        v_ET = V.do(lambda e: e.tensor_copy(ET[:, 4 * TP:], ps[0:66, 5, 0:TP]))
        ec_ev = []
        for i in range(NT):
            ET_i = ET[:, i * TP:(i + 1) * TP]
            mm(ps[0:TP, 6, :], ET_i, rhs_aug[:, 0:2, :].rearrange("p l d -> p (l d)"), True, True, v_ET,
               *(ec_ev[-1:]))
            p = mm(ps[0:TP, 7, 0:D], ET_i, rhs_aug[:, 2, :], True, True, mark=True)
            V.do(lambda e, i=i: e.tensor_copy(Ec[:, 0:2, i, :], ps[0:TP, 6, :].rearrange("p (l d) -> p l d", l=2)), p)
            ec_ev.append(V.do(lambda e, i=i: e.tensor_copy(Ec[:, 2, i, :], ps[0:TP, 7, 0:D])))
        t_Ec = ec_ev[-1]

        L = {n: sem(f"l_{n}") for n in ("z1", "z2", "z1e", "z2e", "a", "y", "st", "ag", "v", "r", "sq", "xh", "t", "hT", "gb")}
        gb = sb("gb", [128, 2, 2])
        tick = sb("tick", [TP, 1])

        def layer_pe(e, it, last):
            for i in range(NT):
                if i == 0:
                    e.wait_ge(L["hT"], it * NT + NT)
                for n, half, b in (("z1", 0, i % 2), ("z2", 1, 2 + i % 2)):
                    if i >= 2:
                        e.wait_ge(L[n + "e"], it * NT + (i - 1))
                    for k in range(2):
                        ins = e.matmul(ps[0:TP, b, 0:D], hT[:, k, i * TP:(i + 1) * TP],
                                       W12[:, k, bass.ds(it, 1), half * D:(half + 1) * D].rearrange("p o d -> p (o d)"),
                                       start=(k == 0), stop=(k == 1))
                    ins.then_inc(L[n], 1)

            def back(i):
                e.wait_ge(L["xh"], it * NT + i + 1)
                if i >= 2:
                    e.wait_ge(L["hT"], it * NT + NT + (i - 1))
                for k in range(2):
                    ins = e.transpose(ps[:, 6 + i % 2, k * TP:(k + 1) * TP], xhat[:, i, k * 128:(k + 1) * 128],
                                      ident[0:TP, 0:TP])
                ins.then_inc(L["t"], 1)
            for i in range(NT):
                if i == 0:
                    e.wait_ge(L["z2e"], it * NT + NT)
                if i >= 2:
                    e.wait_ge(L["y"], it * NT + (i - 1))
                for j in range(NT):
                    ins = e.matmul(ps[0:TP, 4 + i % 2, 0:D], AT[:, j, i * TP:(i + 1) * TP], z2[:, j, :],
                                   start=(j == 0), stop=(j == NT - 1))
                ins.then_inc(L["a"], 1)
                if i >= 3 and not last:
                    back(i - 3)
            if not last:
                for i in range(NT - 3, NT):
                    back(i)

        def layer_dve(e, it):
            for i in range(NT):
                e.wait_ge(L["z1"], it * NT + i + 1)
                e.tensor_tensor(z1[:, i, :], ps[0:TP, i % 2, 0:D],
                                Ec[:, bass.ds(it, 1), i, :].rearrange("p o d -> p (o d)"), ALU.add).then_inc(L["z1e"], 1)

            def stats_of(i):
                e.wait_ge(L["a"], it * NT + i + 1)
                if i == 0:
                    e.wait_ge(L["z1e"], it * NT + NT)
                e.scalar_tensor_tensor(out=y[:, i, :], in0=ps[0:TP, 4 + i % 2, 0:D], scalar=rc[:, i:i + 1],
                                       in1=z1[:, i, :], op0=ALU.mult, op1=ALU.add).then_inc(L["y"], 1)
                e.wait_ge(L["y"], it * NT + i + 1)
                e.bn_stats(stats[:, i, :], y[:, i, :]).then_inc(L["st"], 1)
                e.wait_ge(L["st"], it * NT + i + 1)
                e.tensor_copy(tick[:, :], stats[:, i, 0:1])
                e.bn_aggr(mv[:, i, :], stats[:, i, :]).then_inc(L["ag"], 1)
                e.wait_ge(L["ag"], it * NT + i + 1)
                e.tensor_scalar(rv[:, 0, i:i + 1], mv[:, i, 1:2], EPS_LN, None, ALU.add).then_inc(L["v"], 1)
                e.wait_ge(L["v"], it * NT + i + 1)
                e.reciprocal(rv[:, 1, i:i + 1], rv[:, 0, i:i + 1]).then_inc(L["r"], 1)

            def scale(i):
                e.wait_ge(L["sq"], it * NT + i + 1)
                e.tensor_scalar(xhat[:, i, :], y[:, i, :], mv[:, i, 0:1], rstd[:, i:i + 1], ALU.subtract,
                                ALU.mult).then_inc(L["xh"], 1)
            for i in range(NT):
                stats_of(i)
                if i >= 1:
                    scale(i - 1)
            scale(NT - 1)

        def layer_act(e, it, last):
            for i in range(NT):
                e.wait_ge(L["z2"], it * NT + i + 1)
                e.copy(z2[:, i, :], ps[0:TP, 2 + i % 2, 0:D]).then_inc(L["z2e"], 1)
            if not last:
                e.copy(gb[:, 0, :], gT[:, :, bass.ds(it, 1)].rearrange("p k o -> p (k o)"))
                e.copy(gb[:, 1, :], bT[:, :, bass.ds(it, 1)].rearrange("p k o -> p (k o)")).then_inc(L["gb"], 1)

            def relu(i):
                if i == 0:
                    e.wait_ge(L["gb"], it + 1)
                e.wait_ge(L["t"], it * NT + i + 1)
                for k in range(2):
                    ins = e.activation(hT[:, k, i * TP:(i + 1) * TP], ps[:, 6 + i % 2, k * TP:(k + 1) * TP], ACT.Relu,
                                       bias=gb[:, 1, k:k + 1], scale=gb[:, 0, k:k + 1])
                ins.then_inc(L["hT"], 1)
            for i in range(NT):
                e.wait_ge(L["r"], it * NT + i + 1)
                e.activation(rstd[:, i:i + 1], rv[:, 1, i:i + 1], ACT.Sqrt).then_inc(L["sq"], 1)
                if i >= 3 and not last:
                    relu(i - 3)
            if not last:
                for i in range(NT - 3, NT):
                    relu(i)

        def layers(lane, start, body):
            def emit(e):
                start(e)
                with e.Fori(0, NL - 1) as it:
                    body(e, it, False)
                body(e, NL - 1, True)
            lane.run(emit)

        def start_pe(e):
            for w in (t_AT, t_Ec, t_W12, *t_xnT):
                e.wait_ge(*w)
            e.sem_inc(L["hT"], NT)

        def start_act(e):
            for k in range(2):
                e.wait_ge(*vec["g", k])
                e.wait_ge(*vec["b", k])
        layers(T, start_pe, layer_pe)
        layers(V, lambda e: e.wait_ge(*t_Ec), lambda e, it, last: layer_dve(e, it))
        layers(S, start_act, layer_act)

        t_x1 = []
        for i in range(NT):
            a = V.do(lambda e, i=i: e.tensor_tensor(y[:, i, :], xhat[:, i, :], gamma_b[:, :], ALU.mult),
                     (L["xh"], NL * NT), t_gl)
        for i in range(NT):
            b2 = V.do(lambda e, i=i: e.tensor_tensor(y[:, i, :], y[:, i, :], beta_b[:, :], ALU.add), a, t_bl)
        t_x1 = V.do(lambda e: e.scalar_tensor_tensor(out=acc[:, :, :].rearrange("p t d -> p (t d)"),
                                                     in0=y.rearrange("p t d -> p (t d)"), scalar=0.0,
                                                     in1=acc[:, :, :].rearrange("p t d -> p (t d)"),
                                                     op0=ALU.max, op1=ALU.add), b2, t_acc)
        xf = xn
        t_xf = norm(acc, xf, t_x1)
        t_xfT = to_feature_major(xf, hT, (6, 7), t_xf, [t_x1])
        logit = part(reg_edge, 0, TP, NT, 256)
        gw = part(reg_edge, 1280, TP, NT, 256)
        path = part(reg_edge, 2560, TP, NT, 256)
        pos = part(reg_edge, 3840, TP, NT, 256)
        lg_ev = []
        for i in range(NT):
            b = i % 2
            for k in range(2):
                p = mm(ps[0:TP, b, 0:NODES], hT[:, k, i * TP:(i + 1) * TP], w1T[:, k, 0:NODES], k == 0, k == 1,
                       t_xfT[i], t_w1T, t_x1, *(lg_ev[i - 2:i - 1]), mark=(k == 1))
            lg_ev.append(V.do(lambda e, i=i, b=b: e.tensor_tensor(logit[:, i, 0:NODES], ps[0:TP, b, 0:NODES],
                                                                  b1_b[:, :], ALU.add), p, t_b1))
        a = lg_ev[-1]
        v0 = V.do(lambda e: e.tensor_scalar(pos[:, :, 0:NODES], logit[:, :, 0:NODES], 0.0, None, ALU.is_gt), a)
        v_ab = V.do(lambda e: e.scalar_tensor_tensor(out=gw[:, :, 0:NODES], in0=logit[:, :, 0:NODES], scalar=-1.0,
                                                     in1=logit[:, :, 0:NODES], op0=ALU.mult, op1=ALU.max), a)
        s_gw = S.do(lambda e: e.activation(gw[:, :, 0:NODES], gw[:, :, 0:NODES], ACT.Gelu), v_ab)
        a = V.do(lambda e: e.memset(path[:, :, 0:1], 1.0), a)
        for l in range(LEVELS - 1):
            n = 2 ** l
            parent = path[:, :, n - 1:2 * n - 1]
            kids = path[:, :, 2 * n - 1:4 * n - 1].rearrange("p t (k two) -> p t k two", two=2)
            a = V.do(lambda e, n=n, parent=parent, kids=kids: e.tensor_tensor(kids[:, :, :, 1], parent,
                                                                              pos[:, :, n - 1:2 * n - 1], ALU.mult),
                     a, v0)
            a = V.do(lambda e, parent=parent, kids=kids: e.tensor_tensor(kids[:, :, :, 0], parent, kids[:, :, :, 1],
                                                                         ALU.subtract), a)
        leafm = path[:, :, LEAVES - 1:NODES]
        rb = part(reg_edge, 5120, TP, NT, HID)
        cols = sb("cols", [TP, NT, 9])
        leafb = part(reg_edge, 5760, TP, 320).bitcast(BF16).rearrange("p (t n) -> p t n", t=NT)
        under = part(reg_edge, 6080, TP, 320).bitcast(BF16).rearrange("p (t n) -> p t n", t=NT)
        v1 = V.do(lambda e: e.tensor_copy(leafb, leafm), a)
        v2 = V.do(lambda e: e.tensor_tensor(rb, leafm, iota[0:TP, 0:LEAVES].unsqueeze(1).broadcast_to([TP, NT, LEAVES]),
                                            ALU.mult), a)
        v2 = V.do(lambda e: e.tensor_reduce(out=cols[:, :, 0], in_=rb, axis=AX.X, op=ALU.add), v2)
        for i in range(NT):
            v3 = V.do(lambda e, i=i: e.tensor_scalar(under[:, i, :], iota[0:TP, 0:LEAVES], cols[:, i, 0:1], None,
                                                     ALU.is_gt), v2)
        for j in range(NT):
            p_pre = mm(ps[:, 2, 0:LEAVES], ones_b[0:TP, :], under[:, j, :], j == 0, j == NT - 1, v3, t_one, mark=True)
        for i in range(NT):
            to = ps[0:TP, 3, i * LEAVES:(i + 1) * LEAVES] if i < 4 else ps[0:TP, 4, 0:LEAVES]
            for j in range(NT):
                mm(to, ones_b[0:TP, 0:TP], under[:, j, :], j == 0, False)
            for j in range(i):
                mm(to, ones_b[0:TP, 0:TP], leafb[:, j, :], False, False)
            p_rk = mm(to, below[:, :], leafb[:, i, :], False, True, t_be, mark=True)
        rank = sb("rank", [TP, NT])
        V.do(lambda e: e.tensor_tensor(rb[:, 0:4, :], leafm[:, 0:4, :],
                                       ps[0:TP, 3, :].rearrange("p (t n) -> p t n", t=4), ALU.mult), p_rk, v2)
        a = V.do(lambda e: e.tensor_tensor(rb[:, 4, :], leafm[:, 4, :], ps[0:TP, 4, 0:LEAVES], ALU.mult))
        a = V.do(lambda e: e.tensor_reduce(out=rank[:, :], in_=rb, axis=AX.X, op=ALU.add), a)
        for i in range(NT):
            v_Pm = V.do(lambda e, i=i: e.tensor_scalar(Pm[:, i, :], iota[0:TP, :], rank[:, i:i + 1], None,
                                                       ALU.is_equal), a)
        a = V.do(lambda e: e.tensor_tensor(gw[:, :, 0:NODES], gw[:, :, 0:NODES], path[:, :, 0:NODES], ALU.mult), s_gw)
        v_gw = a
        for l in range(LEVELS):
            v_cols = V.do(lambda e, l=l: e.tensor_reduce(out=cols[:, :, 1 + l], in_=gw[:, :, 2 ** l - 1:2 ** (l + 1) - 1],
                                                         axis=AX.X, op=ALU.add), v_gw)
        gt_ev = []
        for i in range(NT):
            b = i % 2
            tr(ps[:, b, 0:TP], gw[:, i, 0:128], TP, v_gw, *(gt_ev[i - 2:i - 1]))
            p = tr(ps[0:127, b, TP:2 * TP], gw[:, i, 128:NODES], TP, mark=True)
            S.do(lambda e, i=i, b=b: e.copy(gwT[:, 0, i * TP:(i + 1) * TP], ps[:, b, 0:TP]), p)
            gt_ev.append(S.do(lambda e, i=i, b=b: e.copy(gwT[0:127, 1, i * TP:(i + 1) * TP], ps[0:127, b, TP:2 * TP])))
        t_gwT = gt_ev[-1]
        pre = sb("pre", [128, LEAVES])
        G4 = part(reg_edge, 6400, 128, NW - 1, LEAVES)
        F4 = sb("F4", [128, LEVELS, NW - 1])
        win = sb("win", [128, U])
        cmp = part(reg_edge, 7000, 128, UNITS[-1], NW - 1)
        a = V.do(lambda e: e.tensor_copy(pre[:, :], ps[:, 2, 0:LEAVES]), p_pre)
        for w in range(1, NW):
            a2 = V.do(lambda e, w=w: e.tensor_scalar(G4[:, w - 1, :], pre[:, :], float(w * WIN), None, ALU.is_le), a)
        a = V.do(lambda e: e.memset(F4[:, 0, :], 0.0))
        for l in range(1, LEVELS):
            step = LEAVES >> l
            a = V.do(lambda e, l=l, step=step: e.tensor_reduce(out=F4[:, l, :], in_=G4[:, :, step::step], axis=AX.X,
                                                               op=ALU.add), a2)
        for w in range(1, NW):
            a2 = V.do(lambda e, w=w: e.tensor_scalar(F4[:, :, w - 1], F4[:, :, w - 1], float(w), None, ALU.add), a)
        for l in range(LEVELS):
            n = UNITS[l]
            a = V.do(lambda e, l=l, n=n: e.tensor_tensor(cmp[:, 0:n, :],
                                                         kk[:, BASE[l]:BASE[l + 1]].unsqueeze(2).broadcast_to([128, n, NW - 1]),
                                                         F4[:, l, :].unsqueeze(1).broadcast_to([128, n, NW - 1]),
                                                         ALU.is_ge), a2, t_kk)
            a2 = V.do(lambda e, l=l, n=n: e.tensor_reduce(out=win[:, BASE[l]:BASE[l + 1]], in_=cmp[:, 0:n, :],
                                                          axis=AX.X, op=ALU.add), a)
        t_nid = V.do(lambda e: e.tensor_tensor(nid[:, :], kk[:, :], win[:, :], ALU.subtract), a2)
        for l in range(LEVELS):
            s_ = slice(BASE[l], BASE[l + 1])
            V.do(lambda e, l=l, s_=s_: e.tensor_scalar(tabs[:, 0, s_], win[0:1, s_], float(WIN), float(l * R), ALU.mult,
                                                       ALU.add), t_nid)
            V.do(lambda e, l=l, s_=s_: e.tensor_scalar(tabs[:, 2, s_], nid[0:1, s_], float(2 ** l - 1), None, ALU.add))
            V.do(lambda e, l=l, s_=s_: e.tensor_scalar(tabs[:, 3, s_], nid[0:1, s_], float(2 * D),
                                                       float((2 ** l - 1) * 2 * D), ALU.mult, ALU.add))
        t_tab = V.do(lambda e: e.tensor_scalar(tabs[:, 1, :], win[0:1, :], float(D), None, ALU.mult))

        half = ((0, 512), (512, R))
        for n, (c0, c1) in enumerate(half):
            for i in range(NT):
                p = mm(ps[0:9, 5 + n, 0:c1 - c0], cols[:, i, :], Pm[:, i, c0:c1], i == 0, i == NT - 1, v_cols, v_Pm,
                       mark=True)
        S.do(lambda e: e.copy(rows[:, 0:512], ps[0:9, 5, 0:512]), p)
        s_rows = S.do(lambda e: e.copy(rows[:, 512:R], ps[0:9, 6, 0:R - 512]))
        v_sel = V.do(lambda e: e.tensor_copy(sel[:, :, :], ident[0:9, 0:9].unsqueeze(2).broadcast_to([9, 9, 128])))
        xs_ev = None
        for k in range(2):
            for n, (c0, c1) in enumerate(half):
                for i in range(NT):
                    p = mm(ps[:, n + 2 * k, 0:c1 - c0], xf[:, i, k * 128:(k + 1) * 128], Pm[:, i, c0:c1], i == 0,
                           i == NT - 1, v_Pm, v_cols, a2, t_gwT, mark=True)
                xs_ev = S.do(lambda e, k=k, n=n, c0=c0, c1=c1: e.copy(xsT[:, k, c0:c1], ps[:, n + 2 * k, 0:c1 - c0]), p)
        for n, (c0, c1) in enumerate(half):
            p = mm(ps[:, 6 + n, 0:c1 - c0], sel[:, 0, :], rows[:, c0:c1], True, True, v_sel, s_rows, mark=True)
        for n, (c0, c1) in enumerate(half):
            a = V.do(lambda e, n=n, c0=c0, c1=c1: e.tensor_copy(nrow[:, LEVELS - 1, c0:c1], ps[:, 6 + n, 0:c1 - c0]), p)
        v_leaf = a
        for l in range(LEVELS - 1):
            v_nr = V.do(lambda e, l=l: e.tensor_scalar(nrow[:, l, :], nrow[:, LEVELS - 1, :], LEVELS - 1 - l, None,
                                                       ALU.logical_shift_right), v_leaf)
        pw_ev = {}
        v_xs = []
        for l in range(LEVELS):
            b = 4 + 2 * (l % 2)
            for n, (c0, c1) in enumerate(half):
                p = mm(ps[:, b + n, 0:c1 - c0], sel[:, 1 + l, :], rows[:, c0:c1], True, True, v_leaf,
                       *([v_xs[l - 2]] if l >= 2 else []), mark=True)
            for n, (c0, c1) in enumerate(half):
                a = V.do(lambda e, l=l, n=n, b=b, c0=c0, c1=c1: e.tensor_tensor(
                    xs[:, :, l * R + c0:l * R + c1], xsT[:, :, c0:c1],
                    ps[:, b + n, 0:c1 - c0].unsqueeze(1).broadcast_to([128, 2, c1 - c0]), ALU.mult), p, xs_ev, t_nid, t_gwT)
            v_xs.append(a)
        s_lhs, s_use, s_node = sem("lhs"), sem("use"), sem("node")
        s_ring = [sem(f"ring{b}") for b in range(RING)]
        for b in range(3):
            p_za = mm(ps[:, b, :], zeros_b[:, 0:128], zeros_b[:, :], True, True, xs_ev, mark=True)

        def units_dve(e):
            e.wait_ge(*v_xs[-1])
            e.wait_ge(*v_nr)
            e.wait_ge(*t_tab)

            def unit(u, b):
                off = e.value_load(tabs[0:1, 0, bass.ds(u, 1)], min_val=0, max_val=LEVELS * R - WIN)
                e.wait_ge(s_use, u + 1)
                e.scalar_tensor_tensor(out=lhs[:, b, :, :],
                                       in0=nrow_flat[:, bass.ds(off, WIN)].unsqueeze(1).broadcast_to([128, 2, WIN]),
                                       scalar=nid[:, bass.ds(u, 1)], in1=xs[:, :, bass.ds(off, WIN)],
                                       op0=ALU.is_equal, op1=ALU.mult).then_inc(s_lhs, 1)
            with e.Fori(0, U // NLHS) as it:
                for b in range(NLHS):
                    unit(it * NLHS + b, b)
            for u in range(U - U % NLHS, U):
                unit(u, u % NLHS)
        V.run(units_dve)

        def units_pe(e):
            e.sem_inc(s_use, NLHS)
            for t in t_res:
                e.wait_ge(*t)
            e.wait_ge(*t_tab)

            def unit(u, b, rhs, *waits):
                wo_ = e.value_load(tabs[0:1, 1, bass.ds(u, 1)], min_val=0, max_val=(NW - 1) * D)
                e.wait_ge(s_lhs, u + 1)
                for s, v in waits:
                    e.wait_ge(s, v)
                for k in range(2):
                    ins = e.matmul(ps_flat[:, bass.ds(wo_, D)], lhs[:, b, k, :], rhs(k), start=False, stop=False,
                                   skip_group_check=True)
                ins.then_inc(s_use, 1)
            res_flat = w_res[:, :, :, :].rearrange("p n k d -> p (n k d)")

            def resident(u, b):
                at = e.value_load(tabs[0:1, 3, bass.ds(u, 1)], min_val=0, max_val=(NRES - 1) * 2 * D)
                unit(u, b, lambda k: res_flat[:, bass.ds(at + k * D, D)])
            with e.Fori(0, U_RES // NLHS) as it:
                for b in range(NLHS):
                    resident(it * NLHS + b, b)
            for u in range(U_RES - U_RES % NLHS, U_RES):
                resident(u, u % NLHS)
            n_loop = (U - U_RES) // RING
            with e.Fori(0, n_loop) as it:
                for b in range(RING):
                    unit(it * RING + (U_RES + b), (U_RES + b) % NLHS, lambda k, b=b: ring[:, b, k, :],
                         (s_ring[b], it * 16 + 16))
            for v in range(n_loop * RING, U - U_RES):
                b = v % RING
                unit(U_RES + v, (U_RES + v) % NLHS, lambda k, b=b: ring[:, b, k, :], (s_ring[b], n_loop * 16 + 16))
        T.run(units_pe)
        units_done = (s_use, NLHS + U)

        def units_load(e):
            e.wait_ge(*t_tab)
            e.wait_ge(*t_raug)
            e.wait_ge(*q_ev[-1])

            def fill(v, b):
                n = e.value_load(tabs[0:1, 2, bass.ds(v + U_RES, 1)], min_val=0, max_val=NODES - 1)
                e.wait_ge(s_use, v + (U_RES - RING + 1 + NLHS))
                e.dma_start(ring[:, b, :, :],
                            w2s[bass.ds(n, 1), :, :].rearrange("o (k p) d -> p (o k) d", p=128)).then_inc(s_ring[b], 16)

            def first(v, b):
                n = e.value_load(tabs[0:1, 2, bass.ds(v + U_RES, 1)], min_val=0, max_val=NODES - 1)
                e.dma_start(ring[:, b, :, :],
                            w2s[bass.ds(n, 1), :, :].rearrange("o (k p) d -> p (o k) d", p=128)).then_inc(s_ring[b], 16)
            for b in range(RING):
                first(b, b)
            n_loop = (U - U_RES) // RING
            with e.Fori(1, n_loop) as it:
                for b in range(RING):
                    fill(it * RING + b, b)
            for v in range(n_loop * RING, U - U_RES):
                fill(v, v % RING)
        Y.run(units_load)

        rk = sb("rk", [TP, TP])
        rowid = sb("rowid", [128, NW])
        for w in range(NW):
            a = V.do(lambda e, w=w: e.tensor_scalar(rowid[:, w:w + 1], row0[:, :], float(w * WIN), None, ALU.add), t_row)
        prev = None
        for i in range(NT):
            a = V.do(lambda e, i=i: e.tensor_scalar(rk[:, :], ident[0:TP, 0:TP], rank[:, i:i + 1], None, ALU.mult),
                     *([prev] if prev else []), a)
            prev = mm(ps[:, 7, 0:TP], ones[0:TP, :], rk[:, :], True, True, a, v_xs[-1], mark=True)
            for w in range(NW):
                a = V.do(lambda e, i=i, w=w: e.tensor_scalar(PmT[:, w, i * TP:(i + 1) * TP], ps[:, 7, 0:TP],
                                                             rowid[:, w:w + 1], None, ALU.is_equal), prev)
        v_PmT = a
        os_ = part(reg_edge, 0, 128, NW, D)
        v_os = V.do(lambda e: e.tensor_copy(os_, ps_flat[:, 0:NW * D].rearrange("p (w d) -> p w d", w=NW)), units_done)
        fin = part(reg_edge, 1280, TP, NT, D)
        f_ev = []
        for i in range(NT):
            b = 4 + i % 2
            for k, n in ((0, 128), (1, 127)):
                mm(ps[0:TP, b, 0:D], gwT[0:n, k, i * TP:(i + 1) * TP], b2t[0:n, k, :], k == 0, False, *t_b2,
                   *(f_ev[i - 2:i - 1]), v_PmT)
            for w in range(NW):
                p = mm(ps[0:TP, b, 0:D], PmT[:, w, i * TP:(i + 1) * TP], os_[:, w, :], False, w == NW - 1, v_os,
                       mark=(w == NW - 1))
            f_ev.append(V.do(lambda e, i=i, b=b: e.tensor_tensor(fin[:, i, :], ps[0:TP, b, 0:D], acc[:, i, :], ALU.add),
                             p))
        s_out = sem("stored")
        out_v = out.rearrange("(t p) d -> p t d", p=TP)

        def store(e):
            for i in range(NT):
                e.wait_ge(*f_ev[i])
                e.dma_start(out_v[:, i, :], fin[:, i, :]).then_inc(s_out, 16)
            e.wait_ge(s_out, 16 * NT)
        Y.run(store)

        block = ctx.enter_context(nc.Block())
        for name, lane in (("sync", Y), ("gpsimd", G), ("scalar", S), ("vector", V), ("tensor", T)):
            def program(eng, lane=lane):
                for emit in lane.queue:
                    emit(eng)
            {"sync": block.sync, "gpsimd": block.gpsimd, "scalar": block.scalar, "vector": block.vector,
             "tensor": block.tensor}[name](program)


_INS = ["x", "src", "dst", "edge_attr_64", "L0_gnn_Wn", "L0_gnn_bn", "L0_gnn_We", "L0_gnn_be", "L0_gnn_Wc", "L0_gnn_bc",
        "L0_gnn_gamma", "L0_gnn_beta", "L0_mix_w_qkv", "L0_mix_mem_kv", "L0_mix_w_out", "L0_mix_b_out",
        "L0_mix_g_out", "L0_mix_g_pre", "L0_ffn_w1s", "L0_ffn_b1s", "L0_ffn_w2s", "L0_ffn_b2s"]


def kernel(**inputs):
    import numpy as _np
    import concourse.bacc as _bacc
    from concourse import mybir as _mybir
    from concourse.bass_utils import run_bass_kernel_spmd as _run

    nc = _bacc.Bacc("TRN2", target_bir_lowering=False, num_devices=1)
    arrays, args = {}, []
    for name in _INS:
        a = _np.ascontiguousarray(inputs[name])
        arrays[f"in_{name}_dram"] = a
        args.append(nc.dram_tensor(f"in_{name}_dram", a.shape, _mybir.dt.from_np(a.dtype), kind="ExternalInput").ap())
    out = nc.dram_tensor("out_0_dram", (N, D), F32, kind="ExternalOutput").ap()
    graph_layer(nc, *args, out)
    r = _run(nc, [arrays], core_ids=[0])
    return r.results[0]["out_0_dram"]
```

```python
import numpy as np
import concourse.bass as bass
from concourse import mybir
from contextlib import ExitStack

F32 = mybir.dt.float32
BF16 = mybir.dt.bfloat16
F16 = mybir.dt.float16
I32 = mybir.dt.int32
ALU = mybir.AluOpType
ACT = mybir.ActivationFunctionType
AX = mybir.AxisListType

N = 625
D = 256
TP = 125
NT = N // TP
DE = 64
E = 20625
EC = 5
NG = E // (TP * EC)
EB = 3
A0 = 512 - DE
NL = 3
H, DH, MEM = 4, 32, 4
HID = H * DH
LEVELS = 8
NODES = 2 ** LEVELS - 1
LEAVES = 2 ** (LEVELS - 1)
WIN = 128
NW = 5
R = NW * WIN
RES = 3
NRES = 2 ** RES - 1
RING = 12
NLHS = 3
EPS_LN = 1e-5
EPS_NORM = 1e-12

UNITS = [2 ** l + NW - 1 for l in range(LEVELS)]
BASE = [sum(UNITS[:l]) for l in range(LEVELS + 1)]
U = BASE[-1]
U_RES = BASE[RES]
T_PAD = -U_RES % 4


class Lane:

    def __init__(self, sem):
        self.sem, self.n, self.queue = sem, 0, []

    def do(self, make, *after, mark=True):
        def emit(eng):
            for sem, value in after:
                eng.wait_ge(sem, value)
            ins = make(eng)
            if mark:
                ins.then_inc(self.sem, 1)
        self.queue.append(emit)
        self.n += mark
        return (self.sem, self.n)

    def run(self, emit):
        self.queue.append(emit)


def graph_layer(nc, x, src, dst, edge, Wn, bn, We, be, Wc, bc, gamma, beta, w_qkv, mem_kv, w_out, b_out, g_out,
                g_pre, w1s, b1s, w2s, b2s, out):
    ctx = ExitStack()
    with ctx:
        def sem(name):
            return ctx.enter_context(nc.semaphore(name))

        def sb(name, shape, dt=F32):
            return ctx.enter_context(nc.sbuf_tensor(name, shape, dt))

        xin = sb("xin", [TP, NT, D])
        xn = sb("xn", [TP, NT, D])
        acc = sb("acc", [TP, NT, D])
        hT = sb("hT", [128, 2, N])
        W12 = sb("W12", [128, 2, NL, 2 * D])
        rhs_aug = sb("rhs_aug", [66, NL, D])
        gT = sb("gT", [128, 2, NL])
        bT = sb("bT", [128, 2, NL])
        gamma_b = sb("gamma_b", [TP, D])
        beta_b = sb("beta_b", [TP, D])
        gout_b = sb("gout_b", [TP, D])
        bout_b = sb("bout_b", [TP, D])
        b1_b = sb("b1_b", [TP, NODES])
        w1T = sb("w1T", [128, 2, 256])
        b2t = sb("b2t", [128, 2, D])
        ident = sb("ident", [128, 128])
        ones_b = sb("ones_b", [128, 128], BF16)
        zeros_b = sb("zeros_b", [128, 512], BF16)
        below = sb("below", [TP, TP], BF16)
        iota = sb("iota", [128, R], F16)
        cnt = sb("cnt", [TP, 4, NT])
        rc = sb("rc", [TP, NT])
        stats = sb("stats", [TP, NT, 6])
        mv = sb("mv", [TP, NT, 2])
        rv = sb("rv", [TP, 2, NT])
        rstd = sb("rstd", [TP, NT])
        tabs = sb("tabs", [1, 4, U + T_PAD], I32)
        w_res = sb("w_res", [128, NRES, 2, D])
        lhs = sb("lhs", [128, NLHS, 2, WIN])
        nid = sb("nid", [128, U])
        idxT = sb("idxT", [TP, 2, EC, NG])
        tiles_i = sb("tiles_i", [1, NG // EB, 8], I32)

        reg_edge = sb("reg_edge", [128, NG * EC * DE])
        reg_hot = sb("reg_hot", [128, 10080])
        reg_mat = sb("reg_mat", [128, NT * N])
        reg_ring = sb("reg_ring", [128, RING * 2 * D])
        esplit = sb("esplit", [TP, EB, 2, EC * DE], BF16)

        def part(region, at, p, *dims):
            n = int(np.prod(dims))
            names = "abcd"[:len(dims)]
            flat = region[0:p, at:at + n]
            if len(dims) == 1:
                return flat
            return flat.rearrange(f"p ({' '.join(names)}) -> p {' '.join(names)}", **dict(zip(names, dims)))

        xin_flat = xin[:, :, :].rearrange("p t d -> p (t d)")
        erest = xin_flat[:, 0:3 * EC * DE].rearrange("p (b c) -> p b c", b=3)
        ET = xin_flat[0:66, 0:N]
        rows = xin_flat[0:9, 0:R]
        W12_flat = W12[:, :, :, :].rearrange("p k l d -> p (k l d)")
        gwT = W12_flat[:, 0:2 * N].rearrange("p (k t) -> p k t", k=2)
        xsT = W12_flat[:, 2 * N:2 * N + 2 * R].rearrange("p (k r) -> p k r", k=2)
        sel = part(reg_hot, 8320, 9, 9, 128)
        e_all = part(reg_edge, 0, TP, NG, EC * DE)
        AT = part(reg_edge, 0, TP, NT, N)
        Ec = part(reg_edge, 3125, TP, NL, NT, D)
        z1 = part(reg_edge, 6965, TP, NT, D)
        z2 = part(reg_edge, 8245, TP, NT, D)
        xhat = part(reg_hot, 0, TP, NT, D)
        y = part(reg_hot, 1280, TP, NT, D)
        xs = part(reg_edge, 0, 128, 2, LEVELS * R)
        hot_src = reg_hot[0:TP, 0:EB * EC * (DE + R) // 2].bitcast(BF16).rearrange("p (b c r) -> p b c r", b=EB, c=EC)
        hot_dst = reg_hot[0:TP, EB * EC * (DE + R) // 2:EB * EC * (DE + 2 * R) // 2].bitcast(BF16).rearrange(
            "p (b c r) -> p b c r", b=EB, c=EC)
        qkv = part(reg_hot, 0, TP, NT, 3 * HID)
        Ek = part(reg_hot, 1920, TP, NT, HID)
        qT = part(reg_hot, 2560, HID, N)
        mo = part(reg_hot, 3185, TP, NT, D)
        xx = part(reg_hot, 4465, TP, NT, D)
        small = reg_hot[:, 5745:5745 + 1500]
        sq = part(reg_hot, 0, TP, NT, D)
        nrow = reg_hot[:, 0:LEVELS * R].bitcast(I32).rearrange("p (l r) -> p l r", l=LEVELS)
        nrow_flat = reg_hot[:, 0:LEVELS * R].bitcast(I32)
        Pm = part(reg_hot, 5120, TP, NT, R)
        idxf = part(reg_hot, 0, NG, 2, N)
        idxi = reg_hot[0:NG, 1250:2500].bitcast(I32).rearrange("p (j e) -> p j e", j=2)
        WnT = part(reg_mat, 0, 128, 2, NL, D)
        lhs_e = part(reg_mat, 1536, 128, 2, NL, 66)
        lhs_n = part(reg_mat, 1932, 128, 2, NL, 66)
        A = part(reg_mat, 0, TP, NT, N)
        PmT = part(reg_mat, 0, 128, NW, N)
        wn = part(reg_ring, 0, 128, 2, NL, D)
        wc = part(reg_ring, 1536, 128, 4, NL, D)
        we = part(reg_ring, 4608, DE, NL, D)
        wq = part(reg_ring, 5376, 128, 2, 3 * HID)
        ring = part(reg_ring, 0, 128, RING, 2, D)
        w1 = sb("w1", [128, 2, D])
        wo = sb("wo", [HID, D])
        gpT = sb("gpT", [128, 2])
        bnT = sb("bnT", [128, 2, NL])
        beT = sb("beT", [128, 2, NL])
        bcr = sb("bcr", [1, NL, D])
        e65 = sb("e65", [1, 66])
        bd = sb("bd", [HID, HID])
        mk = sb("mk", [HID, MEM])
        mkT = sb("mkT", [MEM, HID])
        mvT = sb("mvT", [MEM, HID])
        E_sb = sb("E_sb", [TP, NT, 66])

        ps = ctx.enter_context(nc.psum_tensor("ps", [128, 8, 512], F32))
        ps_flat = ps[:, :, :].rearrange("p b c -> p (b c)")

        V, S, G, T = Lane(sem("v_done")), Lane(sem("s_done")), Lane(sem("g_done")), Lane(sem("t_done"))
        Y = Lane(sem("y_unused"))

        def load(lane, name, to, frm, slow=False):
            s = sem(f"in_{name}")

            def emit(eng):
                eng.dma_start(to, frm, allow_slow_non_contiguous=slow).then_inc(s, 16)
            lane.run(emit)
            return (s, 16)

        def mm(to, lhsT, rhs, start, stop, *after, mark=False):
            return T.do(lambda e: e.matmul(to, lhsT, rhs, start=start, stop=stop, skip_group_check=True),
                        *after, mark=mark)

        def tr(to, frm, k, *after, mark=False):
            return T.do(lambda e: e.transpose(to, frm, ident[0:k, 0:k]), *after, mark=mark)

        groups = "(g e) -> g e"
        t_src = load(Y, "src", idxi[:, 0, :], src.rearrange(groups, g=NG))
        t_dst = load(Y, "dst", idxi[:, 1, :], dst.rearrange(groups, g=NG))
        t_x = load(Y, "x", xin[:, :, :], x.rearrange("(t p) d -> p t d", p=TP))
        t_wq = load(Y, "wq", wq, w_qkv.rearrange("(k p) d -> p k d", p=128))
        t_wn = [load(Y, f"wn{l}", wn[:, :, l, :], Wn[l].rearrange("(k p) d -> p k d", p=128)) for l in range(NL)]
        t_wc = [load(Y, f"wc{l}", wc[:, :, l, :], Wc[l].rearrange("(k p) d -> p k d", p=128)) for l in range(NL)]
        t_we = load(Y, "we", we, We.rearrange("l p d -> p l d"))
        t_e = []
        per = NG // 3
        for q in range(3):
            part_e = edge[q * per * EC * TP:(q + 1) * per * EC * TP, :]
            t_e.append(load(Y, f"e{q}", e_all[:, q * per:(q + 1) * per, :],
                            part_e.rearrange("(g p c) f -> p g (c f)", g=per, c=EC)))
        t_w1 = [load(Y, "w1a", w1[:, 0, :], w1s[0:128, :]), load(Y, "w1b", w1[0:127, 1, :], w1s[128:NODES, :])]
        t_b2 = [load(Y, "b2a", b2t[:, 0, :], b2s[0:128, :]), load(Y, "b2b", b2t[0:127, 1, :], b2s[128:NODES, :])]
        t_res = [load(Y, f"res{l}", w_res[:, 2 ** l - 1:2 ** (l + 1) - 1, :, :],
                      w2s[2 ** l - 1:2 ** (l + 1) - 1, :, :].rearrange("n (k p) d -> p n k d", p=128))
                 for l in range(RES)]

        t_gp = load(S, "gp", gpT[:, :], g_pre.rearrange("(k p) -> p k", p=128), True)
        t_mk = load(S, "mk", mk[:, :], mem_kv[0].rearrange("h d m -> (h d) m"))
        t_mkT = load(S, "mkT", mkT[:, :], mem_kv[0].rearrange("h d m -> m (h d)"), True)
        t_mvT = load(S, "mvT", mvT[:, :], mem_kv[1].rearrange("h d m -> m (h d)"), True)
        vec = {}
        for name, to, frm in (("bn", bnT, bn), ("be", beT, be), ("g", gT, gamma), ("b", bT, beta)):
            for k in range(2):
                vec[name, k] = load(S, f"{name}{k}", to[:, k, :],
                                    frm[:, k * 128:(k + 1) * 128].rearrange("l p -> p l"), True)
        t_wo = load(S, "wo", wo[:, :], w_out)
        t_bc = load(S, "bc", bcr[:, :, :], bc.unsqueeze(0))
        t_bo = load(S, "bout", bout_b[:, :], b_out.partition_broadcast(TP))
        t_go = load(S, "go", gout_b[:, :], g_out.partition_broadcast(TP))
        t_gl = load(S, "gl", gamma_b[:, :], gamma[NL - 1].partition_broadcast(TP))
        t_bl = load(S, "bl", beta_b[:, :], beta[NL - 1].partition_broadcast(TP))
        t_b1 = load(S, "b1s", b1_b[:, :], b1s.partition_broadcast(TP))

        g0 = G.do(lambda e: e.memset(ident[:, :], 0.0))
        t_id = G.do(lambda e: e.affine_select(out=ident[:, :], in_=ident[:, :], compare_op=ALU.not_equal, fill=1.0,
                                              base=0, pattern=[[-1, 128]], channel_multiplier=1), g0)
        t_io = G.do(lambda e: e.iota(iota[:, :], [[1, R]], base=0, channel_multiplier=0,
                                     allow_small_or_imprecise_dtypes=True))
        g0 = G.do(lambda e: e.memset(below[:, :], 1.0))
        t_be = G.do(lambda e: e.affine_select(out=below[:, :], in_=below[:, :], compare_op=ALU.is_gt, fill=0.0,
                                              base=0, pattern=[[1, TP]], channel_multiplier=-1), g0)
        row0 = sb("row0", [128, 1])
        t_row = G.do(lambda e: e.iota(row0[:, :], [[0, 1]], base=0, channel_multiplier=1,
                                      allow_small_or_imprecise_dtypes=True))
        kk = sb("kk", [128, U])
        for l in range(LEVELS):
            t_kk = G.do(lambda e, l=l: e.iota(kk[:, BASE[l]:BASE[l + 1]], [[1, UNITS[l]]], base=0,
                                              channel_multiplier=0, allow_small_or_imprecise_dtypes=True))
        t_one = G.do(lambda e: e.memset(ones_b[:, :], 1.0))
        ones = sb("ones", [128, 128])
        t_onef = G.do(lambda e: e.memset(ones[:, :], 1.0))
        t_zero = G.do(lambda e: e.memset(zeros_b[:, :], 0.0))
        t_lz = G.do(lambda e: e.memset(reg_mat[:, 1536:1536 + 792], 0.0))
        g0 = G.do(lambda e: e.memset(e65[:, :], 0.0))
        t_e65 = G.do(lambda e: e.memset(e65[:, 65:66], 1.0), g0)
        g0 = G.do(lambda e: e.memset(bd[:, :], 0.0))
        for h in range(H):
            t_bd = g0 = G.do(lambda e, h=h: e.memset(bd[h * DH:(h + 1) * DH, h * DH:(h + 1) * DH], DH ** -0.5), g0)

        i0 = V.do(lambda e: e.tensor_copy(idxf, idxi), t_src, t_dst)
        lim = small[0:NG, 0:2]
        tl = small[0:NG, 2:4]
        v0 = V.do(lambda e: e.tensor_reduce(out=lim[:, 0:1], in_=idxf[:, 1, :], axis=AX.X, op=ALU.min), i0)
        v0 = V.do(lambda e: e.tensor_reduce(out=lim[:, 1:2], in_=idxf[:, 1, :], axis=AX.X, op=ALU.max), i0)
        v0 = V.do(lambda e: e.tensor_scalar(tl[:, 0:1], lim[:, 0:1], float(TP), None, ALU.is_ge), v0)
        v0 = V.do(lambda e: e.tensor_scalar(tl[:, 1:2], lim[:, 1:2], float(TP), 1.0, ALU.is_ge, ALU.add), v0)
        for k in range(2, NT):
            v0 = V.do(lambda e, k=k: e.scalar_tensor_tensor(out=tl, in0=lim, scalar=float(k * TP), in1=tl,
                                                            op0=ALU.is_ge, op1=ALU.add), v0)
        for j in range(2):
            for c in range(EC):
                tr(ps[0:TP, 0, (j * EC + c) * NG:(j * EC + c + 1) * NG],
                   idxf[:, j, :].rearrange("g (p c) -> g c p", c=EC)[:, c, :], NG, t_id, i0)
        tr(ps[0:1, 1, 0:NG], tl[:, 0:1], NG, v0)
        p_idx = tr(ps[0:1, 1, NG:2 * NG], tl[:, 1:2], NG, mark=True)
        t_idx = V.do(lambda e: e.tensor_copy(idxT[:, :, :, :].rearrange("p j c g -> p (j c g)"),
                                             ps[0:TP, 0, 0:2 * EC * NG]), p_idx)
        for j in range(2):
            t_til = V.do(lambda e, j=j: e.tensor_copy(tiles_i[:, :, j * EB:(j + 1) * EB],
                                                      ps[0:1, 1, j * NG:(j + 1) * NG].rearrange("p (i b) -> p i b", b=EB)))
        idx_free = t_til

        def norm(frm, to, *after):
            for i in range(NT):
                a = V.do(lambda e, i=i: e.bn_stats(stats[:, i, :], frm[:, i, :]), *after)
            for i in range(NT):
                a2 = V.do(lambda e, i=i: e.bn_aggr(mv[:, i, :], stats[:, i, :]), a)
            a = V.do(lambda e: e.tensor_scalar(rv[:, 0, :], mv[:, :, 1], EPS_LN, None, ALU.add), a2)
            a = V.do(lambda e: e.reciprocal(rv[:, 1, :], rv[:, 0, :]), a)
            b = S.do(lambda e: e.activation(rstd[:, :], rv[:, 1, :], ACT.Sqrt), a)
            last = []
            for i in range(NT):
                last.append(V.do(lambda e, i=i: e.tensor_scalar(to[:, i, :], frm[:, i, :], mv[:, i, 0:1],
                                                                rstd[:, i:i + 1], ALU.subtract, ALU.mult), b))
            return last

        t_xn = norm(xin, xn, t_x)

        t_col = None
        for l in range(NL):
            for k in range(2):
                t_col = V.do(lambda e, l=l, k=k: e.tensor_tensor(lhs_e[:, k, l, 64:65], bnT[:, k, l:l + 1],
                                                                 beT[:, k, l:l + 1], ALU.add),
                             t_lz, vec["bn", k], vec["be", k])
                t_col = V.do(lambda e, l=l, k=k: e.tensor_copy(lhs_n[:, k, l, 65:66], bnT[:, k, l:l + 1]))
        for l in range(NL):
            for f in range(2):
                p = tr(ps[:, 7, (l * 2 + f) * DE:(l * 2 + f + 1) * DE], we[:, l, f * 128:(f + 1) * 128], DE, t_we,
                       mark=True)
        s_we = S.do(lambda e: e.copy(lhs_e[:, :, :, 0:DE].rearrange("p f l c -> p l f c"),
                                     ps[:, 7, 0:NL * 2 * DE].rearrange("p (l f c) -> p l f c", l=NL, f=2)), p, t_lz)
        taken = {5: s_we, 6: s_we, 7: s_we}

        def combine(l):
            for f in range(2):
                for k in range(2):
                    p = tr(ps[:, 6, f * 256 + k * 128:f * 256 + (k + 1) * 128], wn[:, k, l, f * 128:(f + 1) * 128], 128,
                           t_wn[l], t_id, taken[6], mark=(f == 1 and k == 1))
            taken[6] = S.do(lambda e: e.copy(WnT[:, :, l, :], ps[:, 6, :].rearrange("p (f k) -> p f k", f=2)), p, t_lz)
            for f in range(2):
                mm(ps[0:66, 7, 0:D], lhs_e[:, f, l, :], wc[:, 2 + f, l, :], f == 0, False, taken[7], t_col, t_wc[l])
            for f in range(2):
                mm(ps[0:66, 7, 0:D], lhs_n[:, f, l, :], wc[:, f, l, :], False, False)
            p = mm(ps[0:66, 7, 0:D], e65[:, :], bcr[:, l, :], False, True, t_e65, t_bc, mark=True)
            taken[7] = S.do(lambda e: e.copy(rhs_aug[:, l, :], ps[0:66, 7, 0:D]), p)
            for k in range(2):
                for half in range(2):
                    for f in range(2):
                        p = mm(ps[:, 5, half * D:(half + 1) * D], WnT[:, f, l, k * 128:(k + 1) * 128],
                               wc[:, 2 * half + f, l, :], f == 0, f == 1, taken[6], taken[5],
                               mark=(half == 1 and f == 1))
                taken[5] = S.do(lambda e, k=k: e.copy(W12[:, k, l, :], ps[:, 5, :]), p)

        def to_feature_major(frm, to, banks, when, free_at):
            done = []
            for i in range(NT):
                b = banks[i % 2]
                for k in range(2):
                    p = tr(ps[:, b, k * TP:(k + 1) * TP], frm[:, i, k * 128:(k + 1) * 128], TP, when[i],
                           *(done[i - 2:i - 1] if i >= 2 else free_at), mark=(k == 1))
                done.append(S.do(lambda e, i=i, b=b: e.copy(to[:, :, i * TP:(i + 1) * TP],
                                                            ps[:, b, 0:2 * TP].rearrange("p (k t) -> p k t", k=2)), p))
            return done

        for k in range(2):
            t_wqg = V.do(lambda e, k=k: e.tensor_scalar(wq[:, k, :], wq[:, k, :], gpT[:, k:k + 1], None, ALU.mult),
                         t_wq, t_gp)
        t_xnT = to_feature_major(xn, hT, (2, 3), t_xn, [])
        ss = small[0:TP, 8:8 + NT]
        nrm = small[0:TP, 16:16 + NT]
        s16 = small[0:TP, 24:24 + NT]
        for i in range(NT):
            a = S.do(lambda e, i=i: e.activation(mo[:, i, :], xn[:, i, :], ACT.Square, accum_out=ss[:, i:i + 1]), t_xn[i],
                     idx_free)
        a = S.do(lambda e: e.activation(nrm, ss, ACT.Sqrt), a)
        a = V.do(lambda e: e.tensor_scalar(nrm, nrm, EPS_NORM, float(1.0 / np.sqrt(D)), ALU.max, ALU.mult), a)
        t_s16 = V.do(lambda e: e.reciprocal(s16, nrm), a)
        t_xx = G.do(lambda e: e.tensor_tensor(xx, xin[:, :, :], xn[:, :, :], ALU.add), t_xn[-1], idx_free, t_bd)
        q_ev = []
        for i in range(NT):
            b = i % 2
            for k in range(2):
                p = mm(ps[0:TP, b, 0:3 * HID], hT[:, k, i * TP:(i + 1) * TP], wq[:, k, :], k == 0, k == 1, t_wqg,
                       t_xnT[i], t_til, *(q_ev[i - 2:i - 1]), mark=(k == 1))
            q_ev.append(S.do(lambda e, i=i, b=b: e.activation(qkv[:, i, :], ps[0:TP, b, 0:3 * HID], ACT.Copy,
                                                              scale=s16[:, i:i + 1]), p, t_s16, idx_free))
        km = small[:, 32:36]
        for i in range(NT):
            b, c = (2, i) if i < 4 else (3, 0)
            p = tr(ps[:, b, c * TP:(c + 1) * TP], qkv[:, i, HID:2 * HID], TP, q_ev[i], t_xnT[-1], mark=True)
        combine(0)
        V.do(lambda e: e.tensor_reduce(out=km[:, 0:1], in_=ps[:, 2, 0:4 * TP], axis=AX.X, op=ALU.max), p)
        V.do(lambda e: e.tensor_reduce(out=km[:, 1:2], in_=ps[:, 3, 0:TP], axis=AX.X, op=ALU.max))
        a = V.do(lambda e: e.tensor_reduce(out=km[:, 2:3], in_=mk[:, :], axis=AX.X, op=ALU.max), t_mk)
        a = V.do(lambda e: e.tensor_reduce(out=km[:, 3:4], in_=km[:, 0:3], axis=AX.X, op=ALU.max), a)
        kdiag = small[:, 40:168]
        a = V.do(lambda e: e.tensor_scalar(kdiag, ident[:, :], km[:, 3:4], None, ALU.mult), a, t_id)
        v_kd = a
        p_kmax = mm(ps[:, 4, 0:HID], ones[:, :], kdiag, True, True, a, t_onef, mark=True)
        combine(1)
        qv = qkv[:, :, 0:HID].rearrange("p t (h d) -> p t h d", h=H)
        qs = small[0:TP, 176:176 + NT * H]
        qb = qs.rearrange("p (t h) -> p t h", t=NT).unsqueeze(3).broadcast_to([TP, NT, H, DH])
        a = V.do(lambda e: e.tensor_reduce(out=qs.rearrange("p (t h) -> p t h", t=NT), in_=qv, axis=AX.X, op=ALU.max),
                 q_ev[-1])
        a = V.do(lambda e: e.tensor_tensor(qv, qv, qb, ALU.subtract), a)
        a = S.do(lambda e: e.activation(qkv[:, :, 0:HID], qkv[:, :, 0:HID], ACT.Exp), a)
        Em = small[0:MEM, 200:200 + HID]
        V.do(lambda e: e.tensor_tensor(Em, mkT[:, :], ps[0:MEM, 4, 0:HID], ALU.subtract), p_kmax, t_mkT)
        v1 = V.do(lambda e: e.tensor_tensor(Ek, qkv[:, :, HID:2 * HID],
                                            ps[0:TP, 4, 0:HID].unsqueeze(1).broadcast_to([TP, NT, HID]), ALU.subtract),
                  p_kmax, idx_free)
        S.do(lambda e: e.activation(Em, Em, ACT.Exp), v1)
        s_E = S.do(lambda e: e.activation(Ek, Ek, ACT.Exp))
        a = V.do(lambda e: e.tensor_reduce(out=qs.rearrange("p (t h) -> p t h", t=NT), in_=qv, axis=AX.X, op=ALU.add),
                 a)
        a = V.do(lambda e: e.reciprocal(qs, qs), a)
        v_q = V.do(lambda e: e.tensor_tensor(qv, qv, qb, ALU.mult), a)
        for i in range(NT):
            mm(ps[:, 0, 0:HID], qkv[:, i, 2 * HID:], Ek[:, i, :], i == 0, False, s_E, q_ev[-1])
        p_ctx = mm(ps[:, 0, 0:HID], mvT[:, :], Em, False, True, t_mvT, mark=True)
        for i in range(NT):
            mm(ps[:, 1, 0:1], Ek[:, i, :], ones[0:TP, 0:1], i == 0, False)
        p_ks = mm(ps[:, 1, 0:1], Em, ones[0:MEM, 0:1], False, True, mark=True)
        ctxm = small[:, 340:340 + HID]
        rks = small[:, 330:331]
        a1 = V.do(lambda e: e.tensor_tensor(ctxm, ps[:, 0, 0:HID], bd[:, :], ALU.mult), p_ctx, t_bd)
        a2 = V.do(lambda e: e.reciprocal(rks, ps[:, 1, 0:1]), p_ks)
        for i in range(NT):
            b, c = (3, i) if i < 4 else (4, 0)
            p_q = tr(ps[:, b, c * TP:(c + 1) * TP], qkv[:, i, 0:HID], TP, v_q, v_kd, mark=True)
        S.do(lambda e: e.copy(qT[:, 0:4 * TP], ps[:, 3, 0:4 * TP]), p_q, idx_free)
        s_qT = S.do(lambda e: e.copy(qT[:, 4 * TP:], ps[:, 4, 0:TP]))
        p_cw = mm(ps[:, 2, 0:D], ctxm, wo[:, :], True, True, a1, t_wo, v_kd, mark=True)
        combine(2)
        t_W12, t_raug = taken[5], taken[7]
        
        for k in range(2):
            tr(ps[:, 4, k * 256:k * 256 + 128], w1[:, 0, k * 128:(k + 1) * 128], 128, t_w1[0], s_qT)
            p = tr(ps[:, 4, k * 256 + 128:k * 256 + 255], w1[0:127, 1, k * 128:(k + 1) * 128], 127, t_w1[1], mark=True)
        t_w1T = S.do(lambda e: e.copy(w1T[:, :, 0:NODES], ps[:, 4, :].rearrange("p (k n) -> p k n", k=2)[:, :, 0:NODES]),
                     p)

        ctxw = small[:, 480:480 + D]
        v_cw = V.do(lambda e: e.tensor_scalar(ctxw, ps[:, 2, 0:D], rks, None, ALU.mult), p_cw, a2)
        ss2 = small[0:TP, 740:740 + NT]
        v_mo = []
        for i in range(NT):
            b = i % 2
            p = mm(ps[0:TP, b, 0:D], qT[:, i * TP:(i + 1) * TP], ctxw, True, True, s_qT, v_cw, a1, a2, *(v_mo[i - 2:i - 1]),
                   mark=True)
            v_mo.append(V.do(lambda e, i=i, b=b: e.tensor_tensor(mo[:, i, :], ps[0:TP, b, 0:D], bout_b[:, :], ALU.add),
                             p, t_bo))
            a = S.do(lambda e, i=i: e.activation(sq[:, i, :], mo[:, i, :], ACT.Square, accum_out=ss2[:, i:i + 1]), v_mo[i])
        a = S.do(lambda e: e.activation(ss2, ss2, ACT.Sqrt), a)
        a = V.do(lambda e: e.tensor_scalar(ss2, ss2, EPS_NORM, float(1.0 / np.sqrt(D)), ALU.max, ALU.mult), a)
        a = V.do(lambda e: e.reciprocal(ss2, ss2), a)
        for i in range(NT):
            b2 = V.do(lambda e, i=i: e.scalar_tensor_tensor(out=mo[:, i, :], in0=mo[:, i, :], scalar=ss2[:, i:i + 1],
                                                            in1=gout_b[:, :], op0=ALU.mult, op1=ALU.mult), a, t_go)
        t_acc = V.do(lambda e: e.tensor_tensor(acc[:, :, :], mo, xx, ALU.add), b2, t_xx)

        s_hot, s_hotfree, s_hi, s_r1, s_mid, s_esp, s_dist = (sem(n) for n in (
            "hot", "hotfree", "ehi", "erest1", "emid", "esplit", "dist"))
        for b in range(8):
            p_z = mm(ps[:, b, :], zeros_b[:, 0:128], zeros_b[:, :], True, True, t_zero, t_acc, s_qT, t_W12, t_raug, t_w1T,
                     mark=True)
        ON_ACT = EC - 1

        def edges_pe(e):
            e.sem_inc(s_hotfree, EB)
            with e.Fori(0, NG // EB) as it:
                _, tiles = nc.values_load_multi_w_load_instructions(
                    tiles_i[0:1, bass.ds(it, 1), 0:2 * EB].rearrange("p o c -> p (o c)"),
                    engines=[mybir.EngineType.PE], min_val=0, max_val=NT,
                    skip_runtime_bounds_check_because="counts of tile starts, at most NT")
                for b in range(EB):
                    with e.Fori(tiles[b], tiles[EB + b]) as t:
                        e.wait_ge(s_hot, it * EB + (b + 1))
                        e.wait_ge(s_esp, it * EB + (b + 1))
                        for c in range(EC):
                            lhsT = hot_dst[:, b, c, bass.ds(t * TP, TP)]
                            for to, rhs in ((ps_flat[0:TP, bass.ds(t * 512, 512)], hot_src[:, b, c, 0:512]),
                                            (ps_flat[0:TP, bass.ds(t * 512, DE)], esplit[:, b, 0, c * DE:(c + 1) * DE]),
                                            (ps_flat[0:TP, bass.ds(t * 512, DE)], esplit[:, b, 1, c * DE:(c + 1) * DE]),
                                            (ps_flat[0:TP, bass.ds(t * 256 + NT * 512, N - A0)],
                                             hot_src[:, b, c, 512:DE + N])):
                                e.matmul(to, lhsT, rhs, start=False, stop=False, skip_group_check=True)
                    e.matmul(ps_flat[:, NT * 768:NT * 768 + 1], zeros_b[:, 0:128], zeros_b[:, 0:1], start=False,
                             stop=False, skip_group_check=True).then_inc(s_hotfree, 1)
        T.run(lambda e: e.wait_ge(*t_til))
        T.run(edges_pe)
        edges_done = (s_hotfree, EB + NG)

        def edge_groups(e, body):
            with e.Fori(0, NG // EB) as it:
                for b in range(EB):
                    body(it * EB + b, b)

        def edges_dve(e):
            e.wait_ge(*p_z)

            def group(g, b):
                e.wait_ge(s_hotfree, g + 1)
                for j, to in ((0, hot_src[:, b, :, DE:]), (1, hot_dst[:, b, :, :])):
                    for c in range(EC):
                        if (j, c) != (0, ON_ACT):
                            ins = e.tensor_scalar(to[:, c, :], iota[0:TP, :], idxT[:, j, c, bass.ds(g, 1)],
                                                  None, ALU.is_equal)
                ins.then_inc(s_hot, 1)
            edge_groups(e, group)
        V.run(lambda e: e.wait_ge(*t_io))
        V.run(lambda e: e.wait_ge(*t_idx))
        V.run(edges_dve)

        def edges_act(e):
            e.wait_ge(*t_io)
            e.wait_ge(*t_idx)
            for q in range(3):
                e.wait_ge(*t_e[q])

            def group(g, b):
                one_hot = hot_src[:, b, ON_ACT, DE:]
                e.wait_ge(s_hotfree, g + 1)
                e.copy(hot_src[:, b, :, 0:DE],
                       e_all[:, bass.ds(g, 1), :].rearrange("p o (c f) -> p (o c) f", c=EC)).then_inc(s_hi, 1)
                e.activation(one_hot, iota[0:TP, :], ACT.Square, scale=-1.0,
                             bias=idxT[:, 0, ON_ACT, bass.ds(g, 1)]).then_inc(s_dist, 1)
                e.wait_ge(s_dist, g + 1)
                e.activation(one_hot, one_hot, ACT.Relu, scale=-1.0, bias=1.0)
                e.wait_ge(s_r1, g + 1)
                e.copy(esplit[:, b, 0, :], erest[:, b, :]).then_inc(s_mid, 1)
            edge_groups(e, group)
        S.run(edges_act)

        def edges_pool(e):
            e.wait_ge(*t_idx)

            def group(g, b):
                e.wait_ge(s_hi, g + 1)
                e.tensor_tensor(erest[:, b, :].rearrange("p (c f) -> p c f", c=EC),
                                e_all[:, bass.ds(g, 1), :].rearrange("p o (c f) -> p (o c) f", c=EC),
                                hot_src[:, b, :, 0:DE], ALU.subtract).then_inc(s_r1, 1)
                e.wait_ge(s_mid, g + 1)
                e.tensor_tensor(esplit[:, b, 1, :], erest[:, b, :], esplit[:, b, 0, :],
                                ALU.subtract).then_inc(s_esp, 1)
            edge_groups(e, group)
        G.run(edges_pool)

        for t in range(NT):
            a = S.do(lambda e, t=t: e.activation(A[:, t, 0:A0], ps[0:TP, t, DE:512], ACT.Copy,
                                                 accum_out=cnt[:, 0, t:t + 1]), edges_done)
        s_A = a
        tail = ps_flat[0:TP, NT * 512:NT * 768].rearrange("p (t c) -> p t c", t=NT)[:, :, 0:N - A0]
        V.do(lambda e: e.tensor_copy(A[:, :, A0:N], tail), edges_done)
        v_A = V.do(lambda e: e.tensor_reduce(out=cnt[:, 1, :], in_=tail, axis=AX.X, op=ALU.add))
        a = V.do(lambda e: e.tensor_tensor(cnt[:, 2, :], cnt[:, 0, :], cnt[:, 1, :], ALU.add), v_A, s_A)
        a2 = V.do(lambda e: e.tensor_scalar(cnt[:, 3, :], cnt[:, 2, :], 1.0, None, ALU.max), a)
        v_rc = V.do(lambda e: e.reciprocal(rc[:, :], cnt[:, 3, :]), a2)
        a = V.do(lambda e: e.tensor_tensor(E_sb[:, :, 0:DE], ps[0:TP, 0:NT, 0:DE],
                                           rc[:, :].unsqueeze(2).broadcast_to([TP, NT, DE]), ALU.mult), v_rc)
        a = V.do(lambda e: e.tensor_tensor(E_sb[:, :, 64], rc[:, :], cnt[:, 2, :], ALU.mult), v_rc)
        v_E = V.do(lambda e: e.memset(E_sb[:, :, 65:66], 1.0))
        at_ev = []
        for j in range(NT):
            b = 2 * (j % 2)
            for i in range(NT):
                to = ps[0:TP, b, i * TP:(i + 1) * TP] if i < 4 else ps[0:TP, b + 1, 0:TP]
                p = tr(to, A[:, i, j * TP:(j + 1) * TP], TP, s_A, v_E, *(at_ev[j - 2:j - 1]), mark=(i == NT - 1))
            S.do(lambda e, j=j, b=b: e.copy(AT[:, j, 0:4 * TP], ps[0:TP, b, 0:4 * TP]), p)
            at_ev.append(S.do(lambda e, j=j, b=b: e.copy(AT[:, j, 4 * TP:], ps[0:TP, b + 1, 0:TP])))
        t_AT = at_ev[-1]
        for i in range(NT):
            b, c = (4, i) if i < 4 else (5, 0)
            p = tr(ps[0:66, b, c * TP:(c + 1) * TP], E_sb[:, i, :], TP, v_E, s_A, mark=True)
        V.do(lambda e: e.tensor_copy(ET[:, 0:4 * TP], ps[0:66, 4, 0:4 * TP]), p)
        v_ET = V.do(lambda e: e.tensor_copy(ET[:, 4 * TP:], ps[0:66, 5, 0:TP]))
        ec_ev = []
        for i in range(NT):
            ET_i = ET[:, i * TP:(i + 1) * TP]
            mm(ps[0:TP, 6, :], ET_i, rhs_aug[:, 0:2, :].rearrange("p l d -> p (l d)"), True, True, v_ET,
               *(ec_ev[-1:]))
            p = mm(ps[0:TP, 7, 0:D], ET_i, rhs_aug[:, 2, :], True, True, mark=True)
            V.do(lambda e, i=i: e.tensor_copy(Ec[:, 0:2, i, :], ps[0:TP, 6, :].rearrange("p (l d) -> p l d", l=2)), p)
            ec_ev.append(V.do(lambda e, i=i: e.tensor_copy(Ec[:, 2, i, :], ps[0:TP, 7, 0:D])))
        t_Ec = ec_ev[-1]

        L = {n: sem(f"l_{n}") for n in ("z1", "z2", "z1e", "z2e", "a", "y", "st", "ag", "v", "r", "sq", "xh", "t", "hT", "gb")}
        gb = sb("gb", [128, 2, 2])
        tick = sb("tick", [TP, 1])

        def layer_pe(e, it, last):
            for i in range(NT):
                if i == 0:
                    e.wait_ge(L["hT"], it * NT + NT)
                for n, half, b in (("z1", 0, i % 2), ("z2", 1, 2 + i % 2)):
                    if i >= 2:
                        e.wait_ge(L[n + "e"], it * NT + (i - 1))
                    for k in range(2):
                        ins = e.matmul(ps[0:TP, b, 0:D], hT[:, k, i * TP:(i + 1) * TP],
                                       W12[:, k, bass.ds(it, 1), half * D:(half + 1) * D].rearrange("p o d -> p (o d)"),
                                       start=(k == 0), stop=(k == 1))
                    ins.then_inc(L[n], 1)

            def back(i):
                e.wait_ge(L["xh"], it * NT + i + 1)
                if i >= 2:
                    e.wait_ge(L["hT"], it * NT + NT + (i - 1))
                for k in range(2):
                    ins = e.transpose(ps[:, 6 + i % 2, k * TP:(k + 1) * TP], xhat[:, i, k * 128:(k + 1) * 128],
                                      ident[0:TP, 0:TP])
                ins.then_inc(L["t"], 1)
            for i in range(NT):
                if i == 0:
                    e.wait_ge(L["z2e"], it * NT + NT)
                if i >= 2:
                    e.wait_ge(L["y"], it * NT + (i - 1))
                for j in range(NT):
                    ins = e.matmul(ps[0:TP, 4 + i % 2, 0:D], AT[:, j, i * TP:(i + 1) * TP], z2[:, j, :],
                                   start=(j == 0), stop=(j == NT - 1))
                ins.then_inc(L["a"], 1)
                if i >= 3 and not last:
                    back(i - 3)
            if not last:
                for i in range(NT - 3, NT):
                    back(i)

        def layer_dve(e, it):
            for i in range(NT):
                e.wait_ge(L["z1"], it * NT + i + 1)
                e.tensor_tensor(z1[:, i, :], ps[0:TP, i % 2, 0:D],
                                Ec[:, bass.ds(it, 1), i, :].rearrange("p o d -> p (o d)"), ALU.add).then_inc(L["z1e"], 1)

            def stats_of(i):
                e.wait_ge(L["a"], it * NT + i + 1)
                if i == 0:
                    e.wait_ge(L["z1e"], it * NT + NT)
                e.scalar_tensor_tensor(out=y[:, i, :], in0=ps[0:TP, 4 + i % 2, 0:D], scalar=rc[:, i:i + 1],
                                       in1=z1[:, i, :], op0=ALU.mult, op1=ALU.add).then_inc(L["y"], 1)
                e.wait_ge(L["y"], it * NT + i + 1)
                e.bn_stats(stats[:, i, :], y[:, i, :]).then_inc(L["st"], 1)
                e.wait_ge(L["st"], it * NT + i + 1)
                e.tensor_copy(tick[:, :], stats[:, i, 0:1])
                e.bn_aggr(mv[:, i, :], stats[:, i, :]).then_inc(L["ag"], 1)
                e.wait_ge(L["ag"], it * NT + i + 1)
                e.tensor_scalar(rv[:, 0, i:i + 1], mv[:, i, 1:2], EPS_LN, None, ALU.add).then_inc(L["v"], 1)
                e.wait_ge(L["v"], it * NT + i + 1)
                e.reciprocal(rv[:, 1, i:i + 1], rv[:, 0, i:i + 1]).then_inc(L["r"], 1)

            def scale(i):
                e.wait_ge(L["sq"], it * NT + i + 1)
                e.tensor_scalar(xhat[:, i, :], y[:, i, :], mv[:, i, 0:1], rstd[:, i:i + 1], ALU.subtract,
                                ALU.mult).then_inc(L["xh"], 1)
            for i in range(NT):
                stats_of(i)
                if i >= 1:
                    scale(i - 1)
            scale(NT - 1)

        def layer_act(e, it, last):
            for i in range(NT):
                e.wait_ge(L["z2"], it * NT + i + 1)
                e.copy(z2[:, i, :], ps[0:TP, 2 + i % 2, 0:D]).then_inc(L["z2e"], 1)
            if not last:
                e.copy(gb[:, 0, :], gT[:, :, bass.ds(it, 1)].rearrange("p k o -> p (k o)"))
                e.copy(gb[:, 1, :], bT[:, :, bass.ds(it, 1)].rearrange("p k o -> p (k o)")).then_inc(L["gb"], 1)

            def relu(i):
                if i == 0:
                    e.wait_ge(L["gb"], it + 1)
                e.wait_ge(L["t"], it * NT + i + 1)
                for k in range(2):
                    ins = e.activation(hT[:, k, i * TP:(i + 1) * TP], ps[:, 6 + i % 2, k * TP:(k + 1) * TP], ACT.Relu,
                                       bias=gb[:, 1, k:k + 1], scale=gb[:, 0, k:k + 1])
                ins.then_inc(L["hT"], 1)
            for i in range(NT):
                e.wait_ge(L["r"], it * NT + i + 1)
                e.activation(rstd[:, i:i + 1], rv[:, 1, i:i + 1], ACT.Sqrt).then_inc(L["sq"], 1)
                if i >= 3 and not last:
                    relu(i - 3)
            if not last:
                for i in range(NT - 3, NT):
                    relu(i)

        def layers(lane, start, body):
            def emit(e):
                start(e)
                with e.Fori(0, NL - 1) as it:
                    body(e, it, False)
                body(e, NL - 1, True)
            lane.run(emit)

        def start_pe(e):
            for w in (t_AT, t_Ec, t_W12, *t_xnT):
                e.wait_ge(*w)
            e.sem_inc(L["hT"], NT)

        def start_act(e):
            for k in range(2):
                e.wait_ge(*vec["g", k])
                e.wait_ge(*vec["b", k])
        layers(T, start_pe, layer_pe)
        layers(V, lambda e: e.wait_ge(*t_Ec), lambda e, it, last: layer_dve(e, it))
        layers(S, start_act, layer_act)

        t_x1 = []
        for i in range(NT):
            a = V.do(lambda e, i=i: e.tensor_tensor(y[:, i, :], xhat[:, i, :], gamma_b[:, :], ALU.mult),
                     (L["xh"], NL * NT), t_gl)
        for i in range(NT):
            b2 = V.do(lambda e, i=i: e.tensor_tensor(y[:, i, :], y[:, i, :], beta_b[:, :], ALU.add), a, t_bl)
        t_x1 = V.do(lambda e: e.scalar_tensor_tensor(out=acc[:, :, :].rearrange("p t d -> p (t d)"),
                                                     in0=y.rearrange("p t d -> p (t d)"), scalar=0.0,
                                                     in1=acc[:, :, :].rearrange("p t d -> p (t d)"),
                                                     op0=ALU.max, op1=ALU.add), b2, t_acc)
        xf = xn
        t_xf = norm(acc, xf, t_x1)
        t_xfT = to_feature_major(xf, hT, (6, 7), t_xf, [t_x1])
        logit = part(reg_edge, 0, TP, NT, 256)
        gw = part(reg_edge, 1280, TP, NT, 256)
        path = part(reg_edge, 2560, TP, NT, 256)
        pos = part(reg_edge, 3840, TP, NT, 256)
        lg_ev = []
        for i in range(NT):
            b = i % 2
            for k in range(2):
                p = mm(ps[0:TP, b, 0:NODES], hT[:, k, i * TP:(i + 1) * TP], w1T[:, k, 0:NODES], k == 0, k == 1,
                       t_xfT[i], t_w1T, t_x1, *(lg_ev[i - 2:i - 1]), mark=(k == 1))
            lg_ev.append(V.do(lambda e, i=i, b=b: e.tensor_tensor(logit[:, i, 0:NODES], ps[0:TP, b, 0:NODES],
                                                                  b1_b[:, :], ALU.add), p, t_b1))
        a = lg_ev[-1]
        v0 = V.do(lambda e: e.tensor_scalar(pos[:, :, 0:NODES], logit[:, :, 0:NODES], 0.0, None, ALU.is_gt), a)
        v_ab = V.do(lambda e: e.scalar_tensor_tensor(out=gw[:, :, 0:NODES], in0=logit[:, :, 0:NODES], scalar=-1.0,
                                                     in1=logit[:, :, 0:NODES], op0=ALU.mult, op1=ALU.max), a)
        s_gw = S.do(lambda e: e.activation(gw[:, :, 0:NODES], gw[:, :, 0:NODES], ACT.Gelu), v_ab)
        a = V.do(lambda e: e.memset(path[:, :, 0:1], 1.0), a)
        for l in range(LEVELS - 1):
            n = 2 ** l
            parent = path[:, :, n - 1:2 * n - 1]
            kids = path[:, :, 2 * n - 1:4 * n - 1].rearrange("p t (k two) -> p t k two", two=2)
            a = V.do(lambda e, n=n, parent=parent, kids=kids: e.tensor_tensor(kids[:, :, :, 1], parent,
                                                                              pos[:, :, n - 1:2 * n - 1], ALU.mult),
                     a, v0)
            a = V.do(lambda e, parent=parent, kids=kids: e.tensor_tensor(kids[:, :, :, 0], parent, kids[:, :, :, 1],
                                                                         ALU.subtract), a)
        leafm = path[:, :, LEAVES - 1:NODES]
        rb = part(reg_edge, 5120, TP, NT, HID)
        cols = sb("cols", [TP, NT, 9])
        leafb = part(reg_edge, 5760, TP, 320).bitcast(BF16).rearrange("p (t n) -> p t n", t=NT)
        under = part(reg_edge, 6080, TP, 320).bitcast(BF16).rearrange("p (t n) -> p t n", t=NT)
        v1 = V.do(lambda e: e.tensor_copy(leafb, leafm), a)
        v2 = V.do(lambda e: e.tensor_tensor(rb, leafm, iota[0:TP, 0:LEAVES].unsqueeze(1).broadcast_to([TP, NT, LEAVES]),
                                            ALU.mult), a)
        v2 = V.do(lambda e: e.tensor_reduce(out=cols[:, :, 0], in_=rb, axis=AX.X, op=ALU.add), v2)
        for i in range(NT):
            v3 = V.do(lambda e, i=i: e.tensor_scalar(under[:, i, :], iota[0:TP, 0:LEAVES], cols[:, i, 0:1], None,
                                                     ALU.is_gt), v2)
        for j in range(NT):
            p_pre = mm(ps[:, 2, 0:LEAVES], ones_b[0:TP, :], under[:, j, :], j == 0, j == NT - 1, v3, t_one, mark=True)
        for i in range(NT):
            to = ps[0:TP, 3, i * LEAVES:(i + 1) * LEAVES] if i < 4 else ps[0:TP, 4, 0:LEAVES]
            for j in range(NT):
                mm(to, ones_b[0:TP, 0:TP], under[:, j, :], j == 0, False)
            for j in range(i):
                mm(to, ones_b[0:TP, 0:TP], leafb[:, j, :], False, False)
            p_rk = mm(to, below[:, :], leafb[:, i, :], False, True, t_be, mark=True)
        rank = sb("rank", [TP, NT])
        V.do(lambda e: e.tensor_tensor(rb[:, 0:4, :], leafm[:, 0:4, :],
                                       ps[0:TP, 3, :].rearrange("p (t n) -> p t n", t=4), ALU.mult), p_rk, v2)
        a = V.do(lambda e: e.tensor_tensor(rb[:, 4, :], leafm[:, 4, :], ps[0:TP, 4, 0:LEAVES], ALU.mult))
        a = V.do(lambda e: e.tensor_reduce(out=rank[:, :], in_=rb, axis=AX.X, op=ALU.add), a)
        for i in range(NT):
            v_Pm = V.do(lambda e, i=i: e.tensor_scalar(Pm[:, i, :], iota[0:TP, :], rank[:, i:i + 1], None,
                                                       ALU.is_equal), a)
        a = V.do(lambda e: e.tensor_tensor(gw[:, :, 0:NODES], gw[:, :, 0:NODES], path[:, :, 0:NODES], ALU.mult), s_gw)
        v_gw = a
        for l in range(LEVELS):
            v_cols = V.do(lambda e, l=l: e.tensor_reduce(out=cols[:, :, 1 + l], in_=gw[:, :, 2 ** l - 1:2 ** (l + 1) - 1],
                                                         axis=AX.X, op=ALU.add), v_gw)
        gt_ev = []
        for i in range(NT):
            b = i % 2
            tr(ps[:, b, 0:TP], gw[:, i, 0:128], TP, v_gw, *(gt_ev[i - 2:i - 1]))
            p = tr(ps[0:127, b, TP:2 * TP], gw[:, i, 128:NODES], TP, mark=True)
            S.do(lambda e, i=i, b=b: e.copy(gwT[:, 0, i * TP:(i + 1) * TP], ps[:, b, 0:TP]), p)
            gt_ev.append(S.do(lambda e, i=i, b=b: e.copy(gwT[0:127, 1, i * TP:(i + 1) * TP], ps[0:127, b, TP:2 * TP])))
        t_gwT = gt_ev[-1]
        pre = sb("pre", [128, LEAVES])
        G4 = part(reg_edge, 6400, 128, NW - 1, LEAVES)
        F4 = sb("F4", [128, LEVELS, NW - 1])
        win = sb("win", [128, U])
        cmp = part(reg_edge, 7000, 128, UNITS[-1], NW - 1)
        a = V.do(lambda e: e.tensor_copy(pre[:, :], ps[:, 2, 0:LEAVES]), p_pre)
        for w in range(1, NW):
            a2 = V.do(lambda e, w=w: e.tensor_scalar(G4[:, w - 1, :], pre[:, :], float(w * WIN), None, ALU.is_le), a)
        a = V.do(lambda e: e.memset(F4[:, 0, :], 0.0))
        for l in range(1, LEVELS):
            step = LEAVES >> l
            a = V.do(lambda e, l=l, step=step: e.tensor_reduce(out=F4[:, l, :], in_=G4[:, :, step::step], axis=AX.X,
                                                               op=ALU.add), a2)
        for w in range(1, NW):
            a2 = V.do(lambda e, w=w: e.tensor_scalar(F4[:, :, w - 1], F4[:, :, w - 1], float(w), None, ALU.add), a)
        for l in range(LEVELS):
            n = UNITS[l]
            a = V.do(lambda e, l=l, n=n: e.tensor_tensor(cmp[:, 0:n, :],
                                                         kk[:, BASE[l]:BASE[l + 1]].unsqueeze(2).broadcast_to([128, n, NW - 1]),
                                                         F4[:, l, :].unsqueeze(1).broadcast_to([128, n, NW - 1]),
                                                         ALU.is_ge), a2, t_kk)
            a2 = V.do(lambda e, l=l, n=n: e.tensor_reduce(out=win[:, BASE[l]:BASE[l + 1]], in_=cmp[:, 0:n, :],
                                                          axis=AX.X, op=ALU.add), a)
        t_nid = V.do(lambda e: e.tensor_tensor(nid[:, :], kk[:, :], win[:, :], ALU.subtract), a2)
        for l in range(LEVELS):
            s_ = slice(BASE[l], BASE[l + 1])
            t_ = s_ if l < RES else slice(BASE[l] + T_PAD, BASE[l + 1] + T_PAD)
            V.do(lambda e, l=l, s_=s_, t_=t_: e.tensor_scalar(tabs[:, 0, t_], win[0:1, s_], float(WIN), float(l * R),
                                                              ALU.mult, ALU.add), t_nid)
            V.do(lambda e, s_=s_, t_=t_: e.tensor_scalar(tabs[:, 1, t_], win[0:1, s_], float(D), None, ALU.mult))
            if l < RES:
                t_tab = V.do(lambda e, l=l, s_=s_, t_=t_: e.tensor_scalar(
                    tabs[:, 3, t_], nid[0:1, s_], float(2 * D), float((2 ** l - 1) * 2 * D), ALU.mult, ALU.add))
            else:
                t_tab = V.do(lambda e, l=l, s_=s_, t_=t_: e.tensor_scalar(tabs[:, 2, t_], nid[0:1, s_],
                                                                          float(2 ** l - 1), None, ALU.add))

        half = ((0, 512), (512, R))
        for n, (c0, c1) in enumerate(half):
            for i in range(NT):
                p = mm(ps[0:9, 5 + n, 0:c1 - c0], cols[:, i, :], Pm[:, i, c0:c1], i == 0, i == NT - 1, v_cols, v_Pm,
                       mark=True)
        S.do(lambda e: e.copy(rows[:, 0:512], ps[0:9, 5, 0:512]), p)
        s_rows = S.do(lambda e: e.copy(rows[:, 512:R], ps[0:9, 6, 0:R - 512]))
        v_sel = V.do(lambda e: e.tensor_copy(sel[:, :, :], ident[0:9, 0:9].unsqueeze(2).broadcast_to([9, 9, 128])))
        xs_ev = None
        for k in range(2):
            for n, (c0, c1) in enumerate(half):
                for i in range(NT):
                    p = mm(ps[:, n + 2 * k, 0:c1 - c0], xf[:, i, k * 128:(k + 1) * 128], Pm[:, i, c0:c1], i == 0,
                           i == NT - 1, v_Pm, v_cols, a2, t_gwT, mark=True)
                xs_ev = S.do(lambda e, k=k, n=n, c0=c0, c1=c1: e.copy(xsT[:, k, c0:c1], ps[:, n + 2 * k, 0:c1 - c0]), p)
        for n, (c0, c1) in enumerate(half):
            p = mm(ps[:, 6 + n, 0:c1 - c0], sel[:, 0, :], rows[:, c0:c1], True, True, v_sel, s_rows, mark=True)
        for n, (c0, c1) in enumerate(half):
            a = V.do(lambda e, n=n, c0=c0, c1=c1: e.tensor_copy(nrow[:, LEVELS - 1, c0:c1], ps[:, 6 + n, 0:c1 - c0]), p)
        v_leaf = a
        for l in range(LEVELS - 1):
            v_nr = V.do(lambda e, l=l: e.tensor_scalar(nrow[:, l, :], nrow[:, LEVELS - 1, :], LEVELS - 1 - l, None,
                                                       ALU.logical_shift_right), v_leaf)
        pw_ev = {}
        v_xs = []
        for l in range(LEVELS):
            b = 4 + 2 * (l % 2)
            for n, (c0, c1) in enumerate(half):
                p = mm(ps[:, b + n, 0:c1 - c0], sel[:, 1 + l, :], rows[:, c0:c1], True, True, v_leaf,
                       *([v_xs[l - 2]] if l >= 2 else []), mark=True)
            for n, (c0, c1) in enumerate(half):
                a = V.do(lambda e, l=l, n=n, b=b, c0=c0, c1=c1: e.tensor_tensor(
                    xs[:, :, l * R + c0:l * R + c1], xsT[:, :, c0:c1],
                    ps[:, b + n, 0:c1 - c0].unsqueeze(1).broadcast_to([128, 2, c1 - c0]), ALU.mult), p, xs_ev, t_nid, t_gwT)
            v_xs.append(a)
        s_lhs, s_use, s_node = sem("lhs"), sem("use"), sem("node")
        s_ring = [sem(f"ring{b}") for b in range(RING)]
        for b in range(3):
            p_za = mm(ps[:, b, :], zeros_b[:, 0:128], zeros_b[:, :], True, True, xs_ev, mark=True)

        n_ring = (U - U_RES) // RING

        def table(engine, row, start, n, top):
            _, values = nc.values_load_multi_w_load_instructions(
                tabs[0:1, row, bass.ds(start, n)], engines=[engine], min_val=0, max_val=top,
                skip_runtime_bounds_check_because="windows are below NW and nodes below their level's size by counting")
            return values

        def bodies(e, resident, others):
            for u in range(0, U_RES, RING):
                resident(u, min(RING, U_RES - u))
            with e.Fori(0, n_ring) as it:
                others(it, it * RING, RING)
            if (U - U_RES) % RING:
                others(n_ring, n_ring * RING, (U - U_RES) % RING)

        def units_dve(e):
            e.wait_ge(*v_xs[-1])
            e.wait_ge(*v_nr)
            e.wait_ge(*t_tab)

            def body(u0, at, n, b0):
                offs = table(mybir.EngineType.DVE, 0, at, n, LEVELS * R - WIN)
                for m in range(n):
                    e.wait_ge(s_use, u0 + (m + 1))
                    e.scalar_tensor_tensor(out=lhs[:, (b0 + m) % NLHS, :, :],
                                           in0=nrow_flat[:, bass.ds(offs[m], WIN)].unsqueeze(1).broadcast_to([128, 2, WIN]),
                                           scalar=nid[:, bass.ds(u0 + m, 1)], in1=xs[:, :, bass.ds(offs[m], WIN)],
                                           op0=ALU.is_equal, op1=ALU.mult).then_inc(s_lhs, 1)
            bodies(e, lambda u, n: body(u, u, n, 0), lambda it, v, n: body(v + U_RES, v + (U_RES + T_PAD), n, U_RES))
        V.run(units_dve)

        def units_pe(e):
            e.sem_inc(s_use, NLHS)
            for t in t_res:
                e.wait_ge(*t)
            e.wait_ge(*t_tab)

            def unit(u, b, window, rhs, *waits):
                e.wait_ge(s_lhs, u)
                for s, v in waits:
                    e.wait_ge(s, v)
                for k in range(2):
                    ins = e.matmul(ps_flat[:, bass.ds(window, D)], lhs[:, b, k, :], rhs(k), start=False, stop=False,
                                   skip_group_check=True)
                ins.then_inc(s_use, 1)
            res_flat = w_res[:, :, :, :].rearrange("p n k d -> p (n k d)")

            def resident(u, n):
                wins = table(mybir.EngineType.PE, 1, u, n, (NW - 1) * D)
                mats = table(mybir.EngineType.PE, 3, u, n, (NRES - 1) * 2 * D)
                for m in range(n):
                    unit(u + (m + 1), m % NLHS, wins[m], lambda k, m=m: res_flat[:, bass.ds(mats[m] + k * D, D)])

            def others(it, v, n):
                wins = table(mybir.EngineType.PE, 1, v + (U_RES + T_PAD), n, (NW - 1) * D)
                for b in range(n):
                    unit(v + (U_RES + b + 1), (U_RES + b) % NLHS, wins[b], lambda k, b=b: ring[:, b, k, :],
                         (s_ring[b], it * 16 + 16))
            bodies(e, resident, others)
        T.run(units_pe)
        units_done = (s_use, NLHS + U)

        def units_load(e):
            e.wait_ge(*t_tab)
            e.wait_ge(*t_raug)
            e.wait_ge(*q_ev[-1])

            def fill(v, n, waits):
                nodes = table(mybir.EngineType.SP, 2, v + (U_RES + T_PAD), n, NODES - 1)
                for b in range(n):
                    if waits:
                        e.wait_ge(s_use, v + (b + U_RES - RING + 1 + NLHS))
                    e.dma_start(ring[:, b, :, :],
                                w2s[bass.ds(nodes[b], 1), :, :].rearrange("o (k p) d -> p (o k) d", p=128)
                                ).then_inc(s_ring[b], 16)
            fill(0, RING, False)
            with e.Fori(1, n_ring) as it:
                fill(it * RING, RING, True)
            if (U - U_RES) % RING:
                fill(n_ring * RING, (U - U_RES) % RING, True)
        Y.run(units_load)

        rk = sb("rk", [TP, TP])
        rowid = sb("rowid", [128, NW])
        for w in range(NW):
            a = V.do(lambda e, w=w: e.tensor_scalar(rowid[:, w:w + 1], row0[:, :], float(w * WIN), None, ALU.add), t_row)
        prev = None
        for i in range(NT):
            a = V.do(lambda e, i=i: e.tensor_scalar(rk[:, :], ident[0:TP, 0:TP], rank[:, i:i + 1], None, ALU.mult),
                     *([prev] if prev else []), a)
            prev = mm(ps[:, 7, 0:TP], ones[0:TP, :], rk[:, :], True, True, a, v_xs[-1], mark=True)
            for w in range(NW):
                a = V.do(lambda e, i=i, w=w: e.tensor_scalar(PmT[:, w, i * TP:(i + 1) * TP], ps[:, 7, 0:TP],
                                                             rowid[:, w:w + 1], None, ALU.is_equal), prev)
        v_PmT = a
        os_ = part(reg_edge, 0, 128, NW, D)
        v_os = V.do(lambda e: e.tensor_copy(os_, ps_flat[:, 0:NW * D].rearrange("p (w d) -> p w d", w=NW)), units_done)
        fin = part(reg_edge, 1280, TP, NT, D)
        f_ev = []
        for i in range(NT):
            b = 4 + i % 2
            for k, n in ((0, 128), (1, 127)):
                mm(ps[0:TP, b, 0:D], gwT[0:n, k, i * TP:(i + 1) * TP], b2t[0:n, k, :], k == 0, False, *t_b2,
                   *(f_ev[i - 2:i - 1]), v_PmT)
            for w in range(NW):
                p = mm(ps[0:TP, b, 0:D], PmT[:, w, i * TP:(i + 1) * TP], os_[:, w, :], False, w == NW - 1, v_os,
                       mark=(w == NW - 1))
            f_ev.append(V.do(lambda e, i=i, b=b: e.tensor_tensor(fin[:, i, :], ps[0:TP, b, 0:D], acc[:, i, :], ALU.add),
                             p))
        s_out = sem("stored")
        out_v = out.rearrange("(t p) d -> p t d", p=TP)

        def store(e):
            for i in range(NT):
                e.wait_ge(*f_ev[i])
                e.dma_start(out_v[:, i, :], fin[:, i, :]).then_inc(s_out, 16)
            e.wait_ge(s_out, 16 * NT)
        Y.run(store)

        block = ctx.enter_context(nc.Block())
        for name, lane in (("sync", Y), ("gpsimd", G), ("scalar", S), ("vector", V), ("tensor", T)):
            def program(eng, lane=lane):
                for emit in lane.queue:
                    emit(eng)
            {"sync": block.sync, "gpsimd": block.gpsimd, "scalar": block.scalar, "vector": block.vector,
             "tensor": block.tensor}[name](program)


_INS = ["x", "src", "dst", "edge_attr_64", "L0_gnn_Wn", "L0_gnn_bn", "L0_gnn_We", "L0_gnn_be", "L0_gnn_Wc", "L0_gnn_bc",
        "L0_gnn_gamma", "L0_gnn_beta", "L0_mix_w_qkv", "L0_mix_mem_kv", "L0_mix_w_out", "L0_mix_b_out",
        "L0_mix_g_out", "L0_mix_g_pre", "L0_ffn_w1s", "L0_ffn_b1s", "L0_ffn_w2s", "L0_ffn_b2s"]


def kernel(**inputs):
    import numpy as _np
    import concourse.bacc as _bacc
    from concourse import mybir as _mybir
    from concourse.bass_utils import run_bass_kernel_spmd as _run

    nc = _bacc.Bacc("TRN2", target_bir_lowering=False, num_devices=1)
    arrays, args = {}, []
    for name in _INS:
        a = _np.ascontiguousarray(inputs[name])
        arrays[f"in_{name}_dram"] = a
        args.append(nc.dram_tensor(f"in_{name}_dram", a.shape, _mybir.dt.from_np(a.dtype), kind="ExternalInput").ap())
    out = nc.dram_tensor("out_0_dram", (N, D), F32, kind="ExternalOutput").ap()
    graph_layer(nc, *args, out)
    r = _run(nc, [arrays], core_ids=[0])
    return r.results[0]["out_0_dram"]
```

```python
import numpy as np
import concourse.bass as bass
from concourse import mybir
from contextlib import ExitStack

F32 = mybir.dt.float32
BF16 = mybir.dt.bfloat16
F16 = mybir.dt.float16
I32 = mybir.dt.int32
ALU = mybir.AluOpType
ACT = mybir.ActivationFunctionType
AX = mybir.AxisListType

N = 625
D = 256
TP = 125
NT = N // TP
DE = 64
E = 20625
EC = 5
NG = E // (TP * EC)
EB = 3
DS = DE + 2
A0 = 512 - DS
NL = 3
H, DH, MEM = 4, 32, 4
HID = H * DH
LEVELS = 8
NODES = 2 ** LEVELS - 1
LEAVES = 2 ** (LEVELS - 1)
WIN = 128
NW = 5
R = NW * WIN
RES = 3
NRES = 2 ** RES - 1
RING = 12
NLHS = 3
EPS_LN = 1e-5
EPS_NORM = 1e-12

UNITS = [0] + [2 ** l + NW - 1 for l in range(1, LEVELS)]
BASE = [sum(UNITS[:l]) for l in range(LEVELS + 1)]
U = BASE[-1]
U_RES = BASE[RES]
T_PAD = -U_RES % 4
UC = U + T_PAD
SORTED = range(1, LEVELS)
COLS = [slice(BASE[l] + T_PAD * (l >= RES), BASE[l + 1] + T_PAD * (l >= RES - 1)) for l in range(LEVELS)]


class Lane:

    def __init__(self, sem):
        self.sem, self.n, self.queue, self.waited = sem, 0, [], {}

    def do(self, make, *after, mark=True):
        new = [(sem, value) for sem, value in after if value > self.waited.get(sem.name, 0)]
        self.waited.update((sem.name, value) for sem, value in new)

        def emit(eng):
            for sem, value in new:
                eng.wait_ge(sem, value)
            ins = make(eng)
            if mark:
                ins.then_inc(self.sem, 1)
        self.queue.append(emit)
        self.n += mark
        return (self.sem, self.n)

    def run(self, emit):
        self.queue.append(emit)


def graph_layer(nc, x, src, dst, edge, Wn, bn, We, be, Wc, bc, gamma, beta, w_qkv, mem_kv, w_out, b_out, g_out,
                g_pre, w1s, b1s, w2s, b2s, out):
    ctx = ExitStack()
    with ctx:
        def sem(name):
            return ctx.enter_context(nc.semaphore(name))

        def sb(name, shape, dt=F32):
            return ctx.enter_context(nc.sbuf_tensor(name, shape, dt))

        xin = sb("xin", [TP, NT, D])
        xn = sb("xn", [TP, NT, D])
        acc = sb("acc", [TP, NT, D])
        hT = sb("hT", [128, 2, N])
        W12 = sb("W12", [128, 2, NL, 2 * D])
        rhs_aug = sb("rhs_aug", [66, NL, D])
        gT = sb("gT", [128, 2, NL])
        bT = sb("bT", [128, 2, NL])
        gamma_b = sb("gamma_b", [TP, D])
        beta_b = sb("beta_b", [TP, D])
        gout_b = sb("gout_b", [TP, D])
        bout_b = sb("bout_b", [TP, D])
        b1_b = sb("b1_b", [TP, NODES])
        w1T = sb("w1T", [128, 2, 256])
        b2t = sb("b2t", [128, 2, D])
        ident = sb("ident", [128, 128])
        ones_b = sb("ones_b", [128, 128], BF16)
        zeros_b = sb("zeros_b", [128, 512], BF16)
        below = sb("below", [TP, TP], BF16)
        iota = sb("iota", [128, R], F16)
        cnt = sb("cnt", [TP, NT])
        rc = sb("rc", [TP, NT])
        stats = sb("stats", [TP, NT, 6])
        mv = sb("mv", [TP, NT, 2])
        rv = sb("rv", [TP, 2, NT])
        rstd = sb("rstd", [TP, NT])
        tabs = sb("tabs", [1, 4, UC], I32)
        w_res = sb("w_res", [128, NRES, 2, D])
        lhs = sb("lhs", [128, NLHS, 2, WIN])
        nid = sb("nid", [128, UC])
        idxT = sb("idxT", [TP, 2, EC, NG])
        tiles_i = sb("tiles_i", [1, NG // EB, 12], I32)

        reg_edge = sb("reg_edge", [128, NG * EC * DE])
        reg_hot = sb("reg_hot", [128, EB * EC * (DS + 2 * R) // 2])
        reg_mat = sb("reg_mat", [128, NT * N])
        reg_ring = sb("reg_ring", [128, RING * 2 * D])
        esplit = sb("esplit", [TP, EB, 2, EC * DE], BF16)

        def part(region, at, p, *dims):
            n = int(np.prod(dims))
            names = "abcd"[:len(dims)]
            flat = region[0:p, at:at + n]
            if len(dims) == 1:
                return flat
            return flat.rearrange(f"p ({' '.join(names)}) -> p {' '.join(names)}", **dict(zip(names, dims)))

        xin_flat = xin[:, :, :].rearrange("p t d -> p (t d)")
        erest = xin_flat[:, 0:3 * EC * DE].rearrange("p (b c) -> p b c", b=3)
        ET = xin_flat[0:66, 0:N]
        rows = xin_flat[0:3 * LEVELS, 0:R // 2].bitcast(BF16)
        W12_flat = W12[:, :, :, :].rearrange("p k l d -> p (k l d)")
        gwT = W12_flat[:, 0:2 * N].rearrange("p (k t) -> p k t", k=2)
        xsT = W12_flat[:, 2 * N:2 * N + 2 * R].rearrange("p (k r) -> p k r", k=2)
        sel = reg_hot[0:3 * LEVELS, 8320:8320 + LEVELS * 64].bitcast(BF16).rearrange("p (q r) -> p q r", q=LEVELS)
        weight_sb = part(reg_hot, 7000, 128, 2, R)
        root = part(reg_hot, 0, TP, NT, D)
        rank_row = part(reg_hot, 9000, 128, N)
        diag = part(reg_hot, 7000, TP, NT, TP)
        win = part(reg_hot, 9650, 128, UC)
        pre = part(reg_hot, 9940, 128, LEAVES)
        first = part(xin_flat, 640, 1, 2, UC)
        e_all = part(reg_edge, 0, TP, NG, EC * DE)
        AT = part(reg_edge, 0, TP, NT, N)
        z2 = part(reg_edge, NT * N, TP, NT, D)
        xhat = part(reg_hot, 0, TP, NT, D)
        y = part(reg_hot, 1280, TP, NT, D)
        xs = part(reg_edge, 0, 128, 2, LEVELS * R)
        n_src = EB * EC * (DS + R) // 2
        hot_src = reg_hot[0:TP, 0:n_src].bitcast(BF16).rearrange("p (b c r) -> p b c r", b=EB, c=EC)
        hot_dst = reg_hot[0:TP, n_src:n_src + EB * EC * R // 2].bitcast(BF16).rearrange("p (b c r) -> p b c r", b=EB, c=EC)
        qkv = part(reg_hot, 0, TP, NT, 3 * HID)
        Ek = part(reg_hot, 1920, TP, NT, HID)
        qT = part(reg_hot, 2560, HID, N)
        mo = part(reg_hot, 3185, TP, NT, D)
        xx = part(reg_hot, 4465, TP, NT, D)
        small = reg_hot[:, 5745:5745 + 1500]
        sq = part(reg_hot, 0, TP, NT, D)
        nrow = reg_hot[:, 0:LEVELS * R].bitcast(I32).rearrange("p (l r) -> p l r", l=LEVELS)
        nrow_flat = reg_hot[:, 0:LEVELS * R].bitcast(I32)
        Pm = reg_hot[0:TP, 5120:5120 + NT * R // 2].bitcast(BF16).rearrange("p (t r) -> p t r", t=NT)
        idxf = part(reg_hot, 0, NG, 2, N)
        idxi = reg_hot[0:NG, 1250:2500].bitcast(I32).rearrange("p (j e) -> p j e", j=2)
        WnT = part(reg_mat, 0, 128, 2, NL, D)
        lhs_e = part(reg_mat, 1536, 128, 2, NL, 66)
        lhs_n = part(reg_mat, 1932, 128, 2, NL, 66)
        A = part(reg_mat, 0, TP, NT, N)
        PmT = part(reg_mat, 0, 128, NW, N)
        wn = part(reg_ring, 0, 128, 2, NL, D)
        wc = part(reg_ring, 1536, 128, 4, NL, D)
        we = part(reg_ring, 4608, DE, NL, D)
        wq = part(reg_ring, 5376, 128, 2, 3 * HID)
        ring = part(reg_ring, 0, 128, RING, 2, D)
        w1 = sb("w1", [128, 2, D])
        wo = sb("wo", [HID, D])
        gpT = sb("gpT", [128, 2])
        bnT = sb("bnT", [128, 2, NL])
        beT = sb("beT", [128, 2, NL])
        bcr = sb("bcr", [1, NL, D])
        e65 = sb("e65", [1, 66])
        bd = sb("bd", [HID, HID])
        mk = sb("mk", [HID, MEM])
        mkT = sb("mkT", [MEM, HID])
        mvT = sb("mvT", [MEM, HID])
        E_sb = sb("E_sb", [TP, NT, 66])

        ps = ctx.enter_context(nc.psum_tensor("ps", [128, 8, 512], F32))
        ps_flat = ps[:, :, :].rearrange("p b c -> p (b c)")

        V, S, G, T = Lane(sem("v_done")), Lane(sem("s_done")), Lane(sem("g_done")), Lane(sem("t_done"))
        Y = Lane(sem("y_unused"))

        def load(lane, name, to, frm, slow=False):
            s = sem(f"in_{name}")

            def emit(eng):
                eng.dma_start(to, frm, allow_slow_non_contiguous=slow).then_inc(s, 16)
            lane.run(emit)
            return (s, 16)

        def mm(to, lhsT, rhs, start, stop, *after, mark=False):
            return T.do(lambda e: e.matmul(to, lhsT, rhs, start=start, stop=stop, skip_group_check=True),
                        *after, mark=mark)

        def tr(to, frm, k, *after, mark=False):
            return T.do(lambda e: e.transpose(to, frm, ident[0:k, 0:k]), *after, mark=mark)

        s_hot, s_hotfree, s_hi, s_r1, s_mid, s_esp, s_dist = (sem(n) for n in (
            "hot", "hotfree", "ehi", "erest1", "emid", "esplit", "dist"))
        T.run(lambda e: e.sem_inc(s_hotfree, EB))

        groups = "(g e) -> g e"
        t_src = load(Y, "src", idxi[:, 0, :], src.rearrange(groups, g=NG))
        t_dst = load(Y, "dst", idxi[:, 1, :], dst.rearrange(groups, g=NG))
        t_x = load(Y, "x", xin[:, :, :], x.rearrange("(t p) d -> p t d", p=TP))
        vec = {}

        def load_vec(name, to, frm):
            for k in range(2):
                vec[name, k] = load(Y, f"{name}{k}", to[:, k, :],
                                    frm[:, k * 128:(k + 1) * 128].rearrange("l p -> p l"), True)
        t_we = load(Y, "we", we, We.rearrange("l p d -> p l d"))
        load_vec("bn", bnT, bn)
        load_vec("be", beT, be)
        t_wn, t_wc = [], []

        def load_w(l):
            t_wn.append(load(Y, f"wn{l}", wn[:, :, l, :], Wn[l].rearrange("(k p) d -> p k d", p=128)))
            t_wc.append(load(Y, f"wc{l}", wc[:, :, l, :], Wc[l].rearrange("(k p) d -> p k d", p=128)))
        load_w(0)
        t_bc = load(Y, "bc", bcr[:, :, :], bc.unsqueeze(0))
        t_wq = load(Y, "wq", wq, w_qkv.rearrange("(k p) d -> p k d", p=128))
        t_gp = load(Y, "gp", gpT[:, :], g_pre.rearrange("(k p) -> p k", p=128), True)
        t_mk = load(Y, "mk", mk[:, :], mem_kv[0].rearrange("h d m -> (h d) m"))
        t_mkT = load(Y, "mkT", mkT[:, :], mem_kv[0].rearrange("h d m -> m (h d)"), True)
        t_mvT = load(Y, "mvT", mvT[:, :], mem_kv[1].rearrange("h d m -> m (h d)"), True)
        load_w(1)
        t_wo = load(Y, "wo", wo[:, :], w_out)
        t_bo = load(Y, "bout", bout_b[:, :], b_out.partition_broadcast(TP))
        t_go = load(Y, "go", gout_b[:, :], g_out.partition_broadcast(TP))
        load_w(2)
        t_w1 = [load(Y, "w1a", w1[:, 0, :], w1s[0:128, :]), load(Y, "w1b", w1[0:127, 1, :], w1s[128:NODES, :])]
        t_e = []
        per = NG // 3
        for q in range(3):
            part_e = edge[q * per * EC * TP:(q + 1) * per * EC * TP, :]
            t_e.append(load(Y, f"e{q}", e_all[:, q * per:(q + 1) * per, :],
                            part_e.rearrange("(g p c) f -> p g (c f)", g=per, c=EC)))
        load_vec("g", gT, gamma)
        load_vec("b", bT, beta)
        t_gl = load(Y, "gl", gamma_b[:, :], gamma[NL - 1].partition_broadcast(TP))
        t_bl = load(Y, "bl", beta_b[:, :], beta[NL - 1].partition_broadcast(TP))
        t_b1 = load(Y, "b1s", b1_b[:, :], b1s.partition_broadcast(TP))
        t_b2 = [load(Y, "b2a", b2t[:, 0, :], b2s[0:128, :]), load(Y, "b2b", b2t[0:127, 1, :], b2s[128:NODES, :])]
        t_res = [load(Y, f"res{l}", w_res[:, 2 ** l - 1:2 ** (l + 1) - 1, :, :],
                      w2s[2 ** l - 1:2 ** (l + 1) - 1, :, :].rearrange("n (k p) d -> p n k d", p=128))
                 for l in range(RES)]

        g0 = G.do(lambda e: e.memset(ident[:, :], 0.0))
        t_id = G.do(lambda e: e.affine_select(out=ident[:, :], in_=ident[:, :], compare_op=ALU.not_equal, fill=1.0,
                                              base=0, pattern=[[-1, 128]], channel_multiplier=1), g0)
        t_lz = G.do(lambda e: e.memset(reg_mat[:, 1536:1536 + 792], 0.0))
        g0 = G.do(lambda e: e.memset(e65[:, :], 0.0))
        t_e65 = G.do(lambda e: e.memset(e65[:, 65:66], 1.0), g0)
        t_io = G.do(lambda e: e.iota(iota[:, :], [[1, R]], base=0, channel_multiplier=0,
                                     allow_small_or_imprecise_dtypes=True))
        g0 = G.do(lambda e: e.memset(below[:, :], 1.0))
        t_be = G.do(lambda e: e.affine_select(out=below[:, :], in_=below[:, :], compare_op=ALU.is_gt, fill=0.0,
                                              base=0, pattern=[[1, TP]], channel_multiplier=-1), g0)
        row0 = sb("row0", [128, 1])
        t_row = G.do(lambda e: e.iota(row0[:, :], [[0, 1]], base=0, channel_multiplier=1,
                                      allow_small_or_imprecise_dtypes=True))
        kk = sb("kk", [128, UC])
        for l in SORTED:
            t_kk = G.do(lambda e, l=l: e.iota(kk[:, COLS[l]], [[1, COLS[l].stop - COLS[l].start]], base=0,
                                              channel_multiplier=0, allow_small_or_imprecise_dtypes=True))
        t_one = G.do(lambda e: e.memset(ones_b[:, :], 1.0))
        ones = sb("ones", [128, 128])
        t_onef = G.do(lambda e: e.memset(ones[:, :], 1.0))
        t_zero = G.do(lambda e: e.memset(zeros_b[:, :], 0.0))
        g0 = G.do(lambda e: e.memset(bd[:, :], 0.0))
        for h in range(H):
            t_bd = g0 = G.do(lambda e, h=h: e.memset(bd[h * DH:(h + 1) * DH, h * DH:(h + 1) * DH], DH ** -0.5), g0)

        i0 = V.do(lambda e: e.tensor_copy(idxf, idxi), t_src, t_dst)
        lim = small[0:NG, 0:2]
        tl = small[0:NG, 2:7]
        v0 = V.do(lambda e: e.tensor_reduce(out=lim[:, 0:1], in_=idxf[:, 1, :], axis=AX.X, op=ALU.min), i0)
        v0 = V.do(lambda e: e.tensor_reduce(out=lim[:, 1:2], in_=idxf[:, 1, :], axis=AX.X, op=ALU.max), i0)
        v0 = V.do(lambda e: e.tensor_scalar(tl[:, 0:1], lim[:, 0:1], float(TP), None, ALU.is_ge), v0)
        v0 = V.do(lambda e: e.tensor_scalar(tl[:, 1:2], lim[:, 1:2], float(TP), 1.0, ALU.is_ge, ALU.add), v0)
        for k in range(2, NT):
            v0 = V.do(lambda e, k=k: e.scalar_tensor_tensor(out=tl[:, 0:2], in0=lim, scalar=float(k * TP), in1=tl[:, 0:2],
                                                            op0=ALU.is_ge, op1=ALU.add), v0)
        V.do(lambda e: e.tensor_tensor(tl[:, 2:3], tl[:, 1:2], tl[:, 0:1], ALU.subtract), v0)
        v0 = V.do(lambda e: e.tensor_scalar(tl[:, 3:4], tl[:, 0:1], float(TP), None, ALU.mult), v0)
        i1 = V.do(lambda e: e.tensor_scalar(idxf[:, 1, :], idxf[:, 1, :], tl[:, 3:4], None, ALU.subtract), v0)
        for j in range(2):
            for c in range(EC):
                tr(ps[0:TP, 0, (j * EC + c) * NG:(j * EC + c + 1) * NG],
                   idxf[:, j, :].rearrange("g (p c) -> g c p", c=EC)[:, c, :], NG, t_id, i1)
        for r in range(3):
            p_idx = tr(ps[0:1, 1, r * NG:(r + 1) * NG], tl[:, r:r + 1], NG, mark=True)
        t_idx = V.do(lambda e: e.tensor_copy(idxT[:, :, :, :].rearrange("p j c g -> p (j c g)"),
                                             ps[0:TP, 0, 0:2 * EC * NG]), p_idx)
        for r, at in enumerate((0, EB, 8)):
            t_til = V.do(lambda e, r=r, at=at: e.tensor_copy(
                tiles_i[:, :, at:at + EB], ps[0:1, 1, r * NG:(r + 1) * NG].rearrange("p (i b) -> p i b", b=EB)))
        idx_free = t_til

        t_col = None
        for l in range(NL):
            for k in range(2):
                t_col = V.do(lambda e, l=l, k=k: e.tensor_tensor(lhs_e[:, k, l, 64:65], bnT[:, k, l:l + 1],
                                                                 beT[:, k, l:l + 1], ALU.add),
                             t_lz, vec["bn", k], vec["be", k])
                t_col = V.do(lambda e, l=l, k=k: e.tensor_copy(lhs_n[:, k, l, 65:66], bnT[:, k, l:l + 1]))
        for l in range(NL):
            for f in range(2):
                p = tr(ps[:, 7, (l * 2 + f) * DE:(l * 2 + f + 1) * DE], we[:, l, f * 128:(f + 1) * 128], DE, t_we,
                       mark=True)
        s_we = S.do(lambda e: e.copy(lhs_e[:, :, :, 0:DE].rearrange("p f l c -> p l f c"),
                                     ps[:, 7, 0:NL * 2 * DE].rearrange("p (l f c) -> p l f c", l=NL, f=2)), p, t_lz)
        taken = {5: s_we, 6: s_we, 7: s_we}

        def combine(l):
            for f in range(2):
                for k in range(2):
                    p = tr(ps[:, 6, f * 256 + k * 128:f * 256 + (k + 1) * 128], wn[:, k, l, f * 128:(f + 1) * 128], 128,
                           t_wn[l], t_id, taken[6], mark=(f == 1 and k == 1))
            taken[6] = S.do(lambda e: e.copy(WnT[:, :, l, :], ps[:, 6, :].rearrange("p (f k) -> p f k", f=2)), p, t_lz)
            for f in range(2):
                mm(ps[0:66, 7, 0:D], lhs_e[:, f, l, :], wc[:, 2 + f, l, :], f == 0, False, taken[7], t_col, t_wc[l])
            for f in range(2):
                mm(ps[0:66, 7, 0:D], lhs_n[:, f, l, :], wc[:, f, l, :], False, False)
            p = mm(ps[0:66, 7, 0:D], e65[:, :], bcr[:, l, :], False, True, t_e65, t_bc, mark=True)
            taken[7] = S.do(lambda e: e.copy(rhs_aug[:, l, :], ps[0:66, 7, 0:D]), p)
            for k in range(2):
                for half in range(2):
                    for f in range(2):
                        p = mm(ps[:, 5, half * D:(half + 1) * D], WnT[:, f, l, k * 128:(k + 1) * 128],
                               wc[:, 2 * half + f, l, :], f == 0, f == 1, taken[6], taken[5],
                               mark=(half == 1 and f == 1))
                taken[5] = S.do(lambda e, k=k: e.copy(W12[:, k, l, :], ps[:, 5, :]), p)

        def norm(frm, to, i0, i1):
            a = (V.sem, V.n)
            for i in range(i0, i1):
                a2 = V.do(lambda e, i=i: e.bn_aggr(mv[:, i, :], stats[:, i, :]), a)
            a = V.do(lambda e: e.tensor_scalar(rv[:, 0, i0:i1], mv[:, i0:i1, 1], EPS_LN, None, ALU.add), a2)
            a = V.do(lambda e: e.reciprocal(rv[:, 1, i0:i1], rv[:, 0, i0:i1]), a)
            b = S.do(lambda e: e.activation(rstd[:, i0:i1], rv[:, 1, i0:i1], ACT.Sqrt), a)
            return [V.do(lambda e, i=i: e.tensor_scalar(to[:, i, :], frm[:, i, :], mv[:, i, 0:1], rstd[:, i:i + 1],
                                                        ALU.subtract, ALU.mult), b) for i in range(i0, i1)]

        for i in range(NT):
            V.do(lambda e, i=i: e.bn_stats(stats[:, i, :], xin[:, i, :]), t_x)
        t_xn = norm(xin, xn, 0, NT)
        combine(0)

        def to_feature_major(frm, to, banks, when, free_at):
            done = []
            for i in range(NT):
                b = banks[i % 2]
                for k in range(2):
                    p = tr(ps[:, b, k * TP:(k + 1) * TP], frm[:, i, k * 128:(k + 1) * 128], TP, when[i],
                           *(done[i - 2:i - 1] if i >= 2 else free_at), mark=(k == 1))
                done.append(S.do(lambda e, i=i, b=b: e.copy(to[:, :, i * TP:(i + 1) * TP],
                                                            ps[:, b, 0:2 * TP].rearrange("p (k t) -> p k t", k=2)), p))
            return done

        for k in range(2):
            t_wqg = V.do(lambda e, k=k: e.tensor_scalar(wq[:, k, :], wq[:, k, :], gpT[:, k:k + 1], None, ALU.mult),
                         t_wq, t_gp)
        t_xnT = to_feature_major(xn, hT, (2, 3), t_xn, [])
        ss = small[0:TP, 8:8 + NT]
        nrm = small[0:TP, 16:16 + NT]
        s16 = small[0:TP, 24:24 + NT]
        a = V.do(lambda e: e.scalar_tensor_tensor(out=ss, in0=mv[:, :, 1], scalar=float(D), in1=rv[:, 1, :], op0=ALU.mult,
                                                  op1=ALU.mult), idx_free)
        a = S.do(lambda e: e.activation(nrm, ss, ACT.Sqrt), a)
        a = V.do(lambda e: e.tensor_scalar(nrm, nrm, EPS_NORM, float(1.0 / np.sqrt(D)), ALU.max, ALU.mult), a)
        t_s16 = V.do(lambda e: e.reciprocal(s16, nrm), a)
        t_xx = G.do(lambda e: e.tensor_tensor(xx, xin[:, :, :], xn[:, :, :], ALU.add), t_xn[-1], idx_free, t_bd)
        q_ev = []
        for i in range(NT):
            b = i % 2
            for k in range(2):
                p = mm(ps[0:TP, b, 0:3 * HID], hT[:, k, i * TP:(i + 1) * TP], wq[:, k, :], k == 0, k == 1, t_wqg,
                       t_xnT[i], t_til, *(q_ev[i - 2:i - 1]), mark=(k == 1))
            q_ev.append(S.do(lambda e, i=i, b=b: e.activation(qkv[:, i, :], ps[0:TP, b, 0:3 * HID], ACT.Copy,
                                                              scale=s16[:, i:i + 1]), p, t_s16, idx_free))
        km = small[:, 32:36]
        for i in range(NT):
            b, c = (2, i) if i < 4 else (3, 0)
            p = tr(ps[:, b, c * TP:(c + 1) * TP], qkv[:, i, HID:2 * HID], TP, q_ev[i], t_xnT[-1], mark=True)
        V.do(lambda e: e.tensor_reduce(out=km[:, 0:1], in_=ps[:, 2, 0:4 * TP], axis=AX.X, op=ALU.max), p)
        V.do(lambda e: e.tensor_reduce(out=km[:, 1:2], in_=ps[:, 3, 0:TP], axis=AX.X, op=ALU.max))
        a = V.do(lambda e: e.tensor_reduce(out=km[:, 2:3], in_=mk[:, :], axis=AX.X, op=ALU.max), t_mk)
        a = V.do(lambda e: e.tensor_reduce(out=km[:, 3:4], in_=km[:, 0:3], axis=AX.X, op=ALU.max), a)
        kdiag = small[:, 40:168]
        a = V.do(lambda e: e.tensor_scalar(kdiag, ident[:, :], km[:, 3:4], None, ALU.mult), a, t_id)
        v_kd = a
        p_kmax = mm(ps[:, 4, 0:HID], ones[:, :], kdiag, True, True, a, t_onef, mark=True)
        qv = qkv[:, :, 0:HID].rearrange("p t (h d) -> p t h d", h=H)
        qs = small[0:TP, 176:176 + NT * H]
        qb = qs.rearrange("p (t h) -> p t h", t=NT).unsqueeze(3).broadcast_to([TP, NT, H, DH])
        a = V.do(lambda e: e.tensor_reduce(out=qs.rearrange("p (t h) -> p t h", t=NT), in_=qv, axis=AX.X, op=ALU.max),
                 q_ev[-1])
        a = V.do(lambda e: e.tensor_tensor(qv, qv, qb, ALU.subtract), a)
        a = S.do(lambda e: e.activation(qkv[:, :, 0:HID], qkv[:, :, 0:HID], ACT.Exp), a)
        Em = small[0:MEM, 200:200 + HID]
        V.do(lambda e: e.tensor_tensor(Em, mkT[:, :], ps[0:MEM, 4, 0:HID], ALU.subtract), p_kmax, t_mkT)
        v1 = V.do(lambda e: e.tensor_tensor(Ek, qkv[:, :, HID:2 * HID],
                                            ps[0:TP, 4, 0:HID].unsqueeze(1).broadcast_to([TP, NT, HID]), ALU.subtract),
                  p_kmax, idx_free)
        S.do(lambda e: e.activation(Em, Em, ACT.Exp), v1)
        s_E = S.do(lambda e: e.activation(Ek, Ek, ACT.Exp))
        combine(1)
        a = V.do(lambda e: e.tensor_reduce(out=qs.rearrange("p (t h) -> p t h", t=NT), in_=qv, axis=AX.X, op=ALU.add),
                 a)
        a = V.do(lambda e: e.reciprocal(qs, qs), a)
        v_q = V.do(lambda e: e.tensor_tensor(qv, qv, qb, ALU.mult), a)
        for i in range(NT):
            mm(ps[:, 0, 0:HID], qkv[:, i, 2 * HID:], Ek[:, i, :], i == 0, False, s_E, q_ev[-1])
        p_ctx = mm(ps[:, 0, 0:HID], mvT[:, :], Em, False, True, t_mvT, mark=True)
        for i in range(NT):
            mm(ps[:, 1, 0:1], Ek[:, i, :], ones[0:TP, 0:1], i == 0, False)
        p_ks = mm(ps[:, 1, 0:1], Em, ones[0:MEM, 0:1], False, True, mark=True)
        ctxm = small[:, 340:340 + HID]
        rks = small[:, 330:331]
        a1 = V.do(lambda e: e.tensor_tensor(ctxm, ps[:, 0, 0:HID], bd[:, :], ALU.mult), p_ctx, t_bd)
        a2 = V.do(lambda e: e.reciprocal(rks, ps[:, 1, 0:1]), p_ks)
        for i in range(NT):
            b, c = (3, i) if i < 4 else (4, 0)
            p_q = tr(ps[:, b, c * TP:(c + 1) * TP], qkv[:, i, 0:HID], TP, v_q, v_kd, mark=True)
        S.do(lambda e: e.copy(qT[:, 0:4 * TP], ps[:, 3, 0:4 * TP]), p_q, idx_free)
        s_qT = S.do(lambda e: e.copy(qT[:, 4 * TP:], ps[:, 4, 0:TP]))
        p_cw = mm(ps[:, 2, 0:D], ctxm, wo[:, :], True, True, a1, t_wo, v_kd, mark=True)
        ctxw = small[:, 480:480 + D]
        v_cw = V.do(lambda e: e.tensor_scalar(ctxw, ps[:, 2, 0:D], rks, None, ALU.mult), p_cw, a2)
        ss2 = small[0:TP, 740:740 + NT]
        v_mo = []
        for i in range(NT):
            b = i % 2
            p = mm(ps[0:TP, b, 0:D], qT[:, i * TP:(i + 1) * TP], ctxw, True, True, s_qT, v_cw, a1, a2, *(v_mo[i - 2:i - 1]),
                   mark=True)
            v_mo.append(V.do(lambda e, i=i, b=b: e.tensor_tensor(mo[:, i, :], ps[0:TP, b, 0:D], bout_b[:, :], ALU.add),
                             p, t_bo))
            a = S.do(lambda e, i=i: e.activation(sq[:, i, :], mo[:, i, :], ACT.Square, accum_out=ss2[:, i:i + 1]), v_mo[i])
        a = S.do(lambda e: e.activation(ss2, ss2, ACT.Sqrt), a)
        combine(2)
        t_W12, t_raug = taken[5], taken[7]
        for k in range(2):
            tr(ps[:, 4, k * 256:k * 256 + 128], w1[:, 0, k * 128:(k + 1) * 128], 128, t_w1[0], s_qT)
            p = tr(ps[:, 4, k * 256 + 128:k * 256 + 255], w1[0:127, 1, k * 128:(k + 1) * 128], 127, t_w1[1], mark=True)
        t_w1T = S.do(lambda e: e.copy(w1T[:, :, 0:NODES], ps[:, 4, :].rearrange("p (k n) -> p k n", k=2)[:, :, 0:NODES]),
                     p)
        a = V.do(lambda e: e.tensor_scalar(ss2, ss2, EPS_NORM, float(1.0 / np.sqrt(D)), ALU.max, ALU.mult), a)
        a = V.do(lambda e: e.reciprocal(ss2, ss2), a)
        for i in range(NT):
            b2 = V.do(lambda e, i=i: e.scalar_tensor_tensor(out=mo[:, i, :], in0=mo[:, i, :], scalar=ss2[:, i:i + 1],
                                                            in1=gout_b[:, :], op0=ALU.mult, op1=ALU.mult), a, t_go)
        t_acc = V.do(lambda e: e.tensor_tensor(acc[:, :, :], mo, xx, ALU.add), b2, t_xx)

        for b in range(8):
            mm(ps[:, b, :], zeros_b[:, 0:128], zeros_b[:, :], True, True, t_zero, t_acc, s_qT, t_W12, t_raug, t_w1T,
               mark=True)
        ON_ACT = EC - 1

        def edges_pe(e):
            with e.Fori(0, NG // EB) as it:
                tiles = tiles_of(it, mybir.EngineType.PE, 0, 2 * EB)
                for b in range(EB):
                    with e.Fori(tiles[b], tiles[EB + b]) as t:
                        e.wait_ge(s_hot, it * EB + (b + 1))
                        e.wait_ge(s_esp, it * EB + (b + 1))
                        r = nc.snap(t - tiles[b], engines=[mybir.EngineType.PE], min_val=0, max_val=NT - 1)
                        for c in range(EC):
                            lhsT = hot_dst[:, b, c, bass.ds(r * TP, TP)]
                            for to, rhs in ((ps_flat[0:TP, bass.ds(t * 512, 512)], hot_src[:, b, c, 0:512]),
                                            (ps_flat[0:TP, bass.ds(t * 512, DE)], esplit[:, b, 0, c * DE:(c + 1) * DE]),
                                            (ps_flat[0:TP, bass.ds(t * 512, DE)], esplit[:, b, 1, c * DE:(c + 1) * DE]),
                                            (ps_flat[0:TP, bass.ds(t * 256 + NT * 512, N - A0)],
                                             hot_src[:, b, c, 512:DS + N])):
                                e.matmul(to, lhsT, rhs, start=False, stop=False, skip_group_check=True)
                    e.matmul(ps_flat[:, NT * 768:NT * 768 + 1], zeros_b[:, 0:128], zeros_b[:, 0:1], start=False,
                             stop=False, skip_group_check=True).then_inc(s_hotfree, 1)
        G.do(lambda e: e.memset(reg_hot[0:TP, 0:n_src].bitcast(BF16).rearrange("p (b r) -> p b r", b=EB * EC)[:, :, DE:DE + 1],
                                1.0), t_acc)
        t_ones = G.do(lambda e: e.memset(
            reg_hot[0:TP, 0:n_src].bitcast(BF16).rearrange("p (b r) -> p b r", b=EB * EC)[:, :, DE + 1:DS], 0.0))
        def tiles_of(it, engine, at, n):
            _, values = nc.values_load_multi_w_load_instructions(
                tiles_i[0:1, bass.ds(it, 1), at:at + n].rearrange("p o c -> p (o c)"),
                engines=[engine], min_val=0, max_val=NT,
                skip_runtime_bounds_check_because="counts of tile starts, at most NT")
            return values
        T.run(lambda e: e.wait_ge(*t_til))
        T.run(lambda e: e.wait_ge(*t_ones))
        T.run(edges_pe)
        edges_done = (s_hotfree, EB + NG)

        def edge_groups(e, body):
            with e.Fori(0, NG // EB) as it:
                for b in range(EB):
                    body(it * EB + b, b)

        def edges_dve(e):
            e.wait_ge(*t_acc)
            e.wait_ge(*t_til)
            with e.Fori(0, NG // EB) as it:
                touched = tiles_of(it, mybir.EngineType.DVE, 8, EB)
                for b in range(EB):
                    g = it * EB + b

                    def dst_hot(at, n):
                        for c in range(EC):
                            ins = e.tensor_scalar(hot_dst[:, b, c, at:at + n], iota[0:TP, at:at + n],
                                                  idxT[:, 1, c, bass.ds(g, 1)], None, ALU.is_equal)
                        return ins
                    e.wait_ge(s_hotfree, g + 1)
                    dst_hot(0, 2 * TP)
                    with e.If(touched[b] > 2):
                        dst_hot(2 * TP, N - 2 * TP)
                    for c in range(EC):
                        if c != ON_ACT:
                            ins = e.tensor_scalar(hot_src[:, b, c, DS:], iota[0:TP, :], idxT[:, 0, c, bass.ds(g, 1)],
                                                  None, ALU.is_equal)
                    ins.then_inc(s_hot, 1)
        V.run(lambda e: e.wait_ge(*t_io))
        V.run(lambda e: e.wait_ge(*t_idx))
        V.run(edges_dve)

        def edges_act(e):
            e.wait_ge(*t_acc)
            e.wait_ge(*t_io)
            e.wait_ge(*t_idx)
            for q in range(3):
                e.wait_ge(*t_e[q])

            def group(g, b):
                one_hot = hot_src[:, b, ON_ACT, DS:]
                e.wait_ge(s_hotfree, g + 1)
                e.copy(hot_src[:, b, :, 0:DE],
                       e_all[:, bass.ds(g, 1), :].rearrange("p o (c f) -> p (o c) f", c=EC)).then_inc(s_hi, 1)
                e.activation(one_hot, iota[0:TP, :], ACT.Square, scale=-1.0,
                             bias=idxT[:, 0, ON_ACT, bass.ds(g, 1)]).then_inc(s_dist, 1)
                e.wait_ge(s_dist, g + 1)
                e.activation(one_hot, one_hot, ACT.Relu, scale=-1.0, bias=1.0)
                e.wait_ge(s_r1, g + 1)
                e.copy(esplit[:, b, 0, :], erest[:, b, :]).then_inc(s_mid, 1)
            edge_groups(e, group)
        S.run(edges_act)

        def edges_pool(e):
            e.wait_ge(*t_idx)

            def group(g, b):
                e.wait_ge(s_hi, g + 1)
                e.tensor_tensor(erest[:, b, :].rearrange("p (c f) -> p c f", c=EC),
                                e_all[:, bass.ds(g, 1), :].rearrange("p o (c f) -> p (o c) f", c=EC),
                                hot_src[:, b, :, 0:DE], ALU.subtract).then_inc(s_r1, 1)
                e.wait_ge(s_mid, g + 1)
                e.tensor_tensor(esplit[:, b, 1, :], erest[:, b, :], esplit[:, b, 0, :],
                                ALU.subtract).then_inc(s_esp, 1)
            edge_groups(e, group)
        G.run(edges_pool)

        tail = ps_flat[0:TP, NT * 512:NT * 768].rearrange("p (t c) -> p t c", t=NT)[:, :, 0:N - A0]
        a = V.do(lambda e: e.tensor_scalar(cnt[:, :], ps[0:TP, 0:NT, DE], 1.0, None, ALU.max), edges_done)
        v_rc = V.do(lambda e: e.reciprocal(rc[:, :], cnt[:, :]), a)
        a = V.do(lambda e: e.tensor_tensor(E_sb[:, :, 0:DE + 1], ps[0:TP, 0:NT, 0:DE + 1],
                                           rc[:, :].unsqueeze(2).broadcast_to([TP, NT, DE + 1]), ALU.mult), v_rc)
        for t in range(3):
            s_A = S.do(lambda e, t=t: e.activation(A[:, t, 0:A0], ps[0:TP, t, DS:512], ACT.Copy, scale=rc[:, t:t + 1]),
                       a)
        for t in range(3, NT):
            v_A = V.do(lambda e, t=t: e.tensor_scalar(A[:, t, 0:A0], ps[0:TP, t, DS:512], rc[:, t:t + 1], None, ALU.mult),
                       v_rc)
        V.do(lambda e: e.tensor_tensor(A[:, :, A0:N], tail, rc[:, :].unsqueeze(2).broadcast_to([TP, NT, N - A0]),
                                                ALU.mult), v_rc)
        v_E = V.do(lambda e: e.memset(E_sb[:, :, DE + 1:DS], 1.0))
        at_ev = []
        for j in range(NT):
            b = 2 * (j % 2)
            for i in range(NT):
                to = ps[0:TP, b, i * TP:(i + 1) * TP] if i < 4 else ps[0:TP, b + 1, 0:TP]
                p = tr(to, A[:, i, j * TP:(j + 1) * TP], TP, s_A, v_A if (j + 1) * TP <= A0 else v_E, *(at_ev[j - 2:j - 1]), mark=(i == NT - 1))
            S.do(lambda e, j=j, b=b: e.copy(AT[:, j, 0:4 * TP], ps[0:TP, b, 0:4 * TP]), p)
            at_ev.append(S.do(lambda e, j=j, b=b: e.copy(AT[:, j, 4 * TP:], ps[0:TP, b + 1, 0:TP])))
        t_AT = at_ev[-1]
        for i in range(NT):
            b, c = (4, i) if i < 4 else (5, 0)
            p = tr(ps[0:66, b, c * TP:(c + 1) * TP], E_sb[:, i, :], TP, v_E, s_A, mark=True)
        V.do(lambda e: e.tensor_copy(ET[:, 0:4 * TP], ps[0:66, 4, 0:4 * TP]), p)
        v_ET = V.do(lambda e: e.tensor_copy(ET[:, 4 * TP:], ps[0:66, 5, 0:TP]))

        L = {n: sem(f"l_{n}") for n in ("z2", "z2e", "y", "st", "ag", "v", "r", "sq", "xh", "t", "hT", "gb")}
        gb = sb("gb", [128, 2, 2])
        tick = sb("tick", [TP, 1])

        def of_layer(w, it, *rest):
            return w[(slice(None), *rest[:-1], bass.ds(it, 1), rest[-1])].rearrange("p o d -> p (o d)")

        AHEAD = 3

        def h_w2(e, it, tiles):
            for i in tiles:
                e.wait_ge(L["hT"], it * NT + (i + 1))
                for k in range(2):
                    ins = e.matmul(ps[0:TP, i, 0:D], hT[:, k, i * TP:(i + 1) * TP],
                                   of_layer(W12, it, k, slice(D, 2 * D)), start=(k == 0), stop=(k == 1))
                ins.then_inc(L["z2"], 1)

        def layer_pe(e, it, last):
            h_w2(e, it, range(AHEAD, NT))
            for i in range(NT):
                e.wait_ge(L["z2e"], it * NT + (i + 1))
                for k in range(2):
                    e.matmul(ps[0:TP, i, 0:D], hT[:, k, i * TP:(i + 1) * TP], of_layer(W12, it, k, slice(0, D)),
                             start=(k == 0), stop=False)
                e.matmul(ps[0:TP, i, 0:D], ET[:, i * TP:(i + 1) * TP], of_layer(rhs_aug, it, slice(0, D)),
                         start=False, stop=False)

            def back(i):
                e.wait_ge(L["xh"], it * NT + i + 1)
                if i >= 3:
                    e.wait_ge(L["hT"], it * NT + NT + (i - 2))
                for k in range(2):
                    ins = e.transpose(ps[:, 5 + i % 3, k * TP:(k + 1) * TP],
                                      xhat[:, i, k * 128:(k + 1) * 128], ident[0:TP, 0:TP])
                ins.then_inc(L["t"], 1)
            for i in range(NT):
                for j in range(NT):
                    ins = e.matmul(ps[0:TP, i, 0:D], AT[:, j, i * TP:(i + 1) * TP], z2[:, j, :],
                                   start=False, stop=(j == NT - 1))
                ins.then_inc(L["y"], 1)
                if i >= 2 and not last:
                    back(i - 2)
            if not last:
                back(NT - 2)
                h_w2(e, it + 1, range(AHEAD))
                back(NT - 1)

        def layer_dve(e, it, tiles):
            def stats_of(i):
                e.wait_ge(L["y"], it * NT + i + 1)
                e.bn_stats(stats[:, i, :], ps[0:TP, i, 0:D]).then_inc(L["st"], 1)
                e.wait_ge(L["st"], it * NT + i + 1)
                e.tensor_copy(tick[:, :], stats[:, i, 0:1])
                e.bn_aggr(mv[:, i, :], stats[:, i, :]).then_inc(L["ag"], 1)
                e.wait_ge(L["ag"], it * NT + i + 1)
                e.tensor_scalar(rv[:, 0, i:i + 1], mv[:, i, 1:2], EPS_LN, None, ALU.add).then_inc(L["v"], 1)
                e.wait_ge(L["v"], it * NT + i + 1)
                e.reciprocal(rv[:, 1, i:i + 1], rv[:, 0, i:i + 1]).then_inc(L["r"], 1)

            def scale(i):
                e.wait_ge(L["sq"], it * NT + i + 1)
                e.tensor_scalar(xhat[:, i, :], ps[0:TP, i, 0:D], mv[:, i, 0:1], rstd[:, i:i + 1], ALU.subtract,
                                ALU.mult).then_inc(L["xh"], 1)
            for i in tiles:
                stats_of(i)
                scale(i)

        def layer_act(e, it, last):
            for i in range(NT):
                e.wait_ge(L["z2"], it * NT + i + 1)
                e.copy(z2[:, i, :], ps[0:TP, i, 0:D]).then_inc(L["z2e"], 1)
            if not last:
                e.copy(gb[:, 0, :], gT[:, :, bass.ds(it, 1)].rearrange("p k o -> p (k o)"))
                e.copy(gb[:, 1, :], bT[:, :, bass.ds(it, 1)].rearrange("p k o -> p (k o)")).then_inc(L["gb"], 1)

            def relu(i):
                if i == 0:
                    e.wait_ge(L["gb"], it + 1)
                e.wait_ge(L["t"], it * NT + i + 1)
                for k in range(2):
                    ins = e.activation(hT[:, k, i * TP:(i + 1) * TP],
                                       ps[:, 5 + i % 3, k * TP:(k + 1) * TP], ACT.Relu,
                                       bias=gb[:, 1, k:k + 1], scale=gb[:, 0, k:k + 1])
                ins.then_inc(L["hT"], 1)
            for i in range(NT):
                e.wait_ge(L["r"], it * NT + i + 1)
                e.activation(rstd[:, i:i + 1], rv[:, 1, i:i + 1], ACT.Sqrt).then_inc(L["sq"], 1)
                if i >= 2 and not last:
                    relu(i - 2)
            if not last:
                for i in range(NT - 2, NT):
                    relu(i)

        def layers(lane, start, body):
            def emit(e):
                start(e)
                with e.Fori(0, NL - 1) as it:
                    body(e, it, False)
                body(e, NL - 1, True)
            lane.run(emit)

        def start_pe(e):
            for w in (t_AT, v_ET, t_W12, t_raug, *t_xnT):
                e.wait_ge(*w)
            e.sem_inc(L["hT"], NT)
            h_w2(e, 0, range(AHEAD))

        def start_act(e):
            for k in range(2):
                e.wait_ge(*vec["g", k])
                e.wait_ge(*vec["b", k])
        layers(T, start_pe, layer_pe)
        layers(S, start_act, layer_act)

        def layers_dve(e):
            with e.Fori(0, NL - 1) as it:
                layer_dve(e, it, range(NT))
        V.run(layers_dve)

        xf = xn
        t_x1 = []

        def tile_end(i):
            a = G.do(lambda e: e.tensor_tensor(y[:, i, :], xhat[:, i, :], gamma_b[:, :], ALU.mult),
                     (L["xh"], (NL - 1) * NT + i + 1), t_gl)
            a = G.do(lambda e: e.tensor_tensor(y[:, i, :], y[:, i, :], beta_b[:, :], ALU.add), a, t_bl)
            t_x1.append(V.do(lambda e: e.scalar_tensor_tensor(out=acc[:, i, :], in0=y[:, i, :], scalar=0.0,
                                                              in1=acc[:, i, :], op0=ALU.max, op1=ALU.add), a, t_acc))
            V.do(lambda e: e.bn_stats(stats[:, i, :], acc[:, i, :]), t_x1[i])
        for i in range(NT):
            V.run(lambda e, i=i: layer_dve(e, NL - 1, [i]))
            if i >= 1:
                tile_end(i - 1)
        t_xf = norm(acc, xf, 0, NT - 1)
        tile_end(NT - 1)
        t_xf += norm(acc, xf, NT - 1, NT)
        a = G.do(lambda e: e.memset(sel, 1.0), edges_done)
        a = G.do(lambda e: e.affine_select(out=sel, in_=sel, compare_op=ALU.is_ge, fill=0.0, base=0,
                                           pattern=[[-3, LEVELS], [0, 128]], channel_multiplier=1), a)
        t_sel = G.do(lambda e: e.affine_select(out=sel, in_=sel, compare_op=ALU.is_ge, fill=0.0, base=2,
                                               pattern=[[3, LEVELS], [0, 128]], channel_multiplier=-1), a)

        for l in SORTED:
            for row, value in enumerate((l * R, 2 ** l - 1)):
                t_first = G.do(lambda e, l=l, row=row, value=value: e.memset(first[:, row, COLS[l]], float(value)),
                               edges_done, v_ET)

        t_xfT = to_feature_major(xf, hT, (5, 6), t_xf, [])
        xp = reg_edge[0:TP, 8100:8100 + 3 * NT * D // 2].bitcast(BF16).rearrange("p (q t d) -> p q t d", q=3, t=NT)
        xrest = y
        a = S.do(lambda e: e.copy(xp[:, 0, :, :], xf[:, :, :]), t_xf[-1])
        a = G.do(lambda e: e.tensor_tensor(xrest, xf[:, :, :], xp[:, 0, :, :], ALU.subtract), a, t_x1[-1])
        a = S.do(lambda e: e.copy(xp[:, 1, :, :], xrest), a)
        t_xp = G.do(lambda e: e.tensor_tensor(xp[:, 2, :, :], xrest, xp[:, 1, :, :], ALU.subtract), a)
        logit = part(reg_edge, 0, TP, NT, 256)
        gw = part(reg_edge, 1280, TP, NT, 256)
        path = part(reg_edge, 2560, TP, NT, 256)
        pos = part(reg_edge, 3840, TP, NT, 256)
        lg_ev = []
        for i in range(NT):
            b = i % 2
            for k in range(2):
                p = mm(ps[0:TP, b, 0:NODES], hT[:, k, i * TP:(i + 1) * TP], w1T[:, k, 0:NODES], k == 0, k == 1,
                       t_xfT[i], t_w1T, t_x1[-1], *(lg_ev[i - 2:i - 1]), mark=(k == 1))
            lg_ev.append(V.do(lambda e, i=i, b=b: e.tensor_tensor(logit[:, i, 0:NODES], ps[0:TP, b, 0:NODES],
                                                                  b1_b[:, :], ALU.add), p, t_b1))
        a = lg_ev[-1]
        v0 = V.do(lambda e: e.tensor_scalar(pos[:, :, 0:NODES], logit[:, :, 0:NODES], 0.0, None, ALU.is_gt), a)
        s_ab = S.do(lambda e: e.activation(gw[:, :, 0:NODES], logit[:, :, 0:NODES], ACT.Abs), a)
        s_gw = S.do(lambda e: e.activation(gw[:, :, 0:NODES], gw[:, :, 0:NODES], ACT.Gelu), s_ab)
        a = V.do(lambda e: e.memset(path[:, :, 0:1], 1.0), a)
        for l in range(LEVELS - 1):
            n = 2 ** l
            parent = path[:, :, n - 1:2 * n - 1]
            kids = path[:, :, 2 * n - 1:4 * n - 1].rearrange("p t (k two) -> p t k two", two=2)
            a = V.do(lambda e, n=n, parent=parent, kids=kids: e.tensor_tensor(kids[:, :, :, 1], parent,
                                                                              pos[:, :, n - 1:2 * n - 1], ALU.mult),
                     a, v0)
            a = V.do(lambda e, parent=parent, kids=kids: e.tensor_tensor(kids[:, :, :, 0], parent, kids[:, :, :, 1],
                                                                         ALU.subtract), a)
        leafm = path[:, :, LEAVES - 1:NODES]
        rb = part(reg_edge, 5120, TP, NT, HID)
        cols = sb("cols", [TP, NT, LEVELS])
        colp = sb("colp", [TP, NT, LEVELS, 3], BF16)
        colr = sb("colr", [TP, NT, LEVELS])
        leafb = part(reg_edge, 5760, TP, 320).bitcast(BF16).rearrange("p (t n) -> p t n", t=NT)
        under = part(reg_edge, 6080, TP, 320).bitcast(BF16).rearrange("p (t n) -> p t n", t=NT)
        v_path = a
        for i in range(NT):
            b, c = 5 + i // 2, i % 2
            for k in range(2):
                p = mm(ps[0:TP, b, c * D:(c + 1) * D], hT[:, k, i * TP:(i + 1) * TP], w_res[:, 0, k, :], k == 0, k == 1,
                       t_res[0], t_xfT[-1], mark=(k == 1))
        for i in range(NT):
            s_root = S.do(lambda e, i=i: e.activation(root[:, i, :], ps[0:TP, 5 + i // 2, (i % 2) * D:(i % 2 + 1) * D],
                                                      ACT.Copy, scale=gw[:, i, 0:1]), p, s_gw)
        g_gw = G.do(lambda e: e.tensor_tensor(gw[:, :, 0:NODES], gw[:, :, 0:NODES], path[:, :, 0:NODES], ALU.mult),
                    v_path, s_root)
        g_root = G.do(lambda e: e.tensor_tensor(acc[:, :, :], acc[:, :, :], root, ALU.add), s_root, t_x1[-1])
        s_leafb = S.do(lambda e: e.copy(leafb, leafm), v_path)
        v2 = V.do(lambda e: e.tensor_tensor(rb, leafm, iota[0:TP, 0:LEAVES].unsqueeze(1).broadcast_to([TP, NT, LEAVES]),
                                            ALU.mult), v_path)
        v2 = V.do(lambda e: e.tensor_reduce(out=cols[:, :, 0], in_=rb, axis=AX.X, op=ALU.add), v2)
        for i in range(NT):
            v3 = V.do(lambda e, i=i: e.tensor_scalar(under[:, i, :], iota[0:TP, 0:LEAVES], cols[:, i, 0:1], None,
                                                     ALU.is_gt), v2)
        for j in range(NT):
            p_pre = mm(ps[:, 2, 0:LEAVES], ones_b[0:TP, :], under[:, j, :], j == 0, j == NT - 1, v3, t_one, mark=True)
        for i in range(NT):
            to = ps[0:TP, 3, i * LEAVES:(i + 1) * LEAVES] if i < 4 else ps[0:TP, 4, 0:LEAVES]
            for j in range(i):
                mm(to, ones_b[0:TP, 0:TP], leafb[:, j, :], j == 0, False, s_leafb)
            p_rk = mm(to, below[:, :], leafb[:, i, :], i == 0, True, t_be, s_leafb, mark=True)

        gt_ev = []
        for i in range(NT):
            b = i % 2
            tr(ps[:, b, 0:TP], gw[:, i, 0:128], TP, g_gw, *(gt_ev[i - 2:i - 1]))
            p = tr(ps[0:127, b, TP:2 * TP], gw[:, i, 128:NODES], TP, mark=True)
            S.do(lambda e, i=i, b=b: e.copy(gwT[:, 0, i * TP:(i + 1) * TP], ps[:, b, 0:TP]), p)
            gt_ev.append(S.do(lambda e, i=i, b=b: e.copy(gwT[0:127, 1, i * TP:(i + 1) * TP], ps[0:127, b, TP:2 * TP])))
        t_gwT = gt_ev[-1]

        G4 = part(reg_edge, 6400, 128, NW - 1, LEAVES)
        F4 = sb("F4", [128, LEVELS, NW - 1])
        cmp = part(reg_edge, 6912, 128, UC, NW - 1)
        v_pre = V.do(lambda e: e.tensor_copy(pre[:, :], ps[:, 2, 0:LEAVES]), p_pre)
        rank_low = sb("rank_low", [TP, NT])
        rank = sb("rank", [TP, NT])
        a = V.do(lambda e: e.tensor_tensor(rb, leafm, pre[0:TP, :].unsqueeze(1).broadcast_to([TP, NT, LEAVES]), ALU.mult),
                 v_pre)
        v_low = V.do(lambda e: e.tensor_reduce(out=rank_low[:, :], in_=rb, axis=AX.X, op=ALU.add), a)
        V.do(lambda e: e.tensor_tensor(rb[:, 0:4, :], leafm[:, 0:4, :],
                                       ps[0:TP, 3, :].rearrange("p (t n) -> p t n", t=4), ALU.mult), p_rk, v_low)
        a = V.do(lambda e: e.tensor_tensor(rb[:, 4, :], leafm[:, 4, :], ps[0:TP, 4, 0:LEAVES], ALU.mult))
        a = V.do(lambda e: e.tensor_reduce(out=rank[:, :], in_=rb, axis=AX.X, op=ALU.add), a)
        v_rank = V.do(lambda e: e.tensor_tensor(rank[:, :], rank[:, :], rank_low[:, :], ALU.add), a)
        v_Pm = [V.do(lambda e, i=i: e.tensor_scalar(Pm[:, i, :], iota[0:TP, :], rank[:, i:i + 1], None,
                                                    ALU.is_equal), v_rank) for i in range(NT)]
        for l in SORTED:
            v_cols = V.do(lambda e, l=l: e.tensor_reduce(out=cols[:, :, l], in_=gw[:, :, 2 ** l - 1:2 ** (l + 1) - 1],
                                                         axis=AX.X, op=ALU.add), g_gw)
        a = V.do(lambda e: e.tensor_copy(colp[:, :, :, 0], cols[:, :, :]), v_cols)
        a = V.do(lambda e: e.tensor_tensor(colr[:, :, :], cols[:, :, :], colp[:, :, :, 0], ALU.subtract), a)
        a = V.do(lambda e: e.tensor_copy(colp[:, :, :, 1], colr[:, :, :]), a)
        v_colp = V.do(lambda e: e.tensor_tensor(colp[:, :, :, 2], colr[:, :, :], colp[:, :, :, 1], ALU.subtract), a)
        for w in range(1, NW):
            a2 = V.do(lambda e, w=w: e.tensor_scalar(G4[:, w - 1, :], pre[:, :], float(w * WIN), None, ALU.is_le), v_pre)
        for l in range(1, LEVELS):
            step = LEAVES >> l
            a = V.do(lambda e, l=l, step=step: e.tensor_reduce(out=F4[:, l, :], in_=G4[:, :, step::step], axis=AX.X,
                                                               op=ALU.add), a2)
        for w in range(1, NW):
            v_F4 = V.do(lambda e, w=w: e.tensor_scalar(F4[:, 1:, w - 1], F4[:, 1:, w - 1], float(w), None, ALU.add), a)
        for l in SORTED:
            n = COLS[l].stop - COLS[l].start
            a = V.do(lambda e, l=l, n=n: e.tensor_tensor(cmp[:, COLS[l], :],
                                                         kk[:, COLS[l]].unsqueeze(2).broadcast_to([128, n, NW - 1]),
                                                         F4[:, l, :].unsqueeze(1).broadcast_to([128, n, NW - 1]),
                                                         ALU.is_ge), v_F4, t_kk)
        a = V.do(lambda e: e.tensor_reduce(out=win[:, :], in_=cmp, axis=AX.X, op=ALU.add), a)
        t_nid = V.do(lambda e: e.tensor_tensor(nid[:, :], kk[:, :], win[:, :], ALU.subtract), a)
        V.do(lambda e: e.scalar_tensor_tensor(out=tabs[:, 0, :], in0=win[0:1, :], scalar=float(WIN), in1=first[:, 0, :],
                                              op0=ALU.mult, op1=ALU.add), t_nid, t_first)
        V.do(lambda e: e.tensor_scalar(tabs[:, 1, :], win[0:1, :], float(D), None, ALU.mult))
        for l in range(1, RES):
            V.do(lambda e, l=l: e.tensor_scalar(tabs[:, 3, COLS[l]], nid[0:1, COLS[l]], float(2 * D),
                                                float((2 ** l - 1) * 2 * D), ALU.mult, ALU.add), t_nid)
        t_tab = V.do(lambda e: e.tensor_tensor(tabs[:, 2, :], nid[0:1, :], first[:, 1, :], ALU.add))

        half = ((0, 512), (512, R))
        def sort_tokens(k, n):
            b, (c0, c1) = (0, 1, 2, 7)[n + 2 * k], half[n]
            for q in range(3):
                for i in range(NT):
                    p = mm(ps[:, b, 0:c1 - c0], xp[:, q, i, k * 128:(k + 1) * 128], Pm[:, i, c0:c1],
                           q == 0 and i == 0, q == 2 and i == NT - 1, v_Pm[i], t_xp, v_pre, t_gwT, s_root,
                           mark=(q == 2 and i == NT - 1))
            return S.do(lambda e: e.copy(xsT[:, k, c0:c1], ps[:, b, 0:c1 - c0]), p)
        sort_tokens(0, 0)
        sort_tokens(0, 1)
        for n, (c0, c1) in enumerate(half):
            for i in range(NT):
                p = mm(ps[0:3 * LEVELS, 5 + n, 0:c1 - c0], colp[:, i, :, :].rearrange("p q r -> p (q r)"), Pm[:, i, c0:c1],
                       i == 0, i == NT - 1, v_colp, s_root, mark=(i == NT - 1))
        S.do(lambda e: e.copy(rows[:, 0:512], ps[0:3 * LEVELS, 5, 0:512]), p)
        s_rows = S.do(lambda e: e.copy(rows[:, 512:R], ps[0:3 * LEVELS, 6, 0:R - 512]))
        sort_tokens(1, 0)

        read = {3: v_rank, 5: s_rows}

        def spread(q, b):
            for n, (c0, c1) in enumerate(half):
                p = mm(ps[:, b + n, 0:c1 - c0], sel[:, q, :], rows[:, c0:c1], True, True, t_sel, s_rows, read[b],
                       mark=(n == 1))
            return p

        p = spread(0, 3)
        for n, (c0, c1) in enumerate(half):
            v_leaf = read[3] = V.do(lambda e, n=n, c0=c0, c1=c1: e.tensor_copy(nrow[:, LEVELS - 1, c0:c1],
                                                                               ps[:, 3 + n, 0:c1 - c0]), p, t_xp, g_root, v_Pm[-1])
        ready, weights = {}, {}

        def level_weights(l, b):
            weights[l] = (b, spread(l, b))

        def level_nodes(l):
            return V.do(lambda e: e.tensor_scalar(nrow[:, l, :], nrow[:, LEVELS - 1, :], LEVELS - 1 - l, None,
                                                  ALU.logical_shift_right), v_leaf)

        def level_rows(l):
            level_nodes(l)
            b, p = weights[l]
            for n, (c0, c1) in enumerate(half):
                ready[l] = read[b] = V.do(lambda e, n=n, c0=c0, c1=c1: e.tensor_tensor(
                    xs[:, :, l * R + c0:l * R + c1], xsT[:, :, c0:c1],
                    ps[:, b + n, 0:c1 - c0].unsqueeze(1).broadcast_to([128, 2, c1 - c0]), ALU.mult),
                    p, xs_ev, t_tab, t_gwT)

        def level_on_pool(l, n):
            b, p = weights[l]
            S.do(lambda e: e.copy(weight_sb[:, n, 0:512], ps[:, b, :]), p, v_Pm[-1])
            a = read[b] = S.do(lambda e: e.copy(weight_sb[:, n, 512:R], ps[:, b + 1, 0:R - 512]))
            ready[l] = G.do(lambda e: e.tensor_tensor(
                xs[:, :, l * R:(l + 1) * R], xsT, weight_sb[:, n, :].unsqueeze(1).broadcast_to([128, 2, R]), ALU.mult),
                a, xs_ev, t_tab, t_gwT)
        level_weights(1, 5)
        xs_ev = sort_tokens(1, 1)
        level_weights(LEVELS - 2, 3)
        for b in range(3):
            mm(ps[:, b, :], zeros_b[:, 0:128], zeros_b[:, :], True, True, xs_ev)
        level_rows(1)
        level_on_pool(LEVELS - 2, 0)

        s_lhs, s_use = sem("lhs"), sem("use")
        s_ring = [sem(f"ring{b}") for b in range(RING)]

        def table(engine, row, start, n, top):
            _, values = nc.values_load_multi_w_load_instructions(
                tabs[0:1, row, bass.ds(start, n)], engines=[engine], min_val=0, max_val=top,
                skip_runtime_bounds_check_because="windows are below NW and nodes below their level's size by counting")
            return values

        def mask_unit(e, u, col, b, off):
            e.wait_ge(s_use, u + 1)
            e.scalar_tensor_tensor(out=lhs[:, b % NLHS, :, :],
                                   in0=nrow_flat[:, bass.ds(off, WIN)].unsqueeze(1).broadcast_to([128, 2, WIN]),
                                   scalar=nid[:, bass.ds(col, 1)], in1=xs[:, :, bass.ds(off, WIN)],
                                   op0=ALU.is_equal, op1=ALU.mult).then_inc(s_lhs, 1)

        def multiply_unit(e, u, b, window, rhs, *waits):
            e.wait_ge(s_lhs, u + 1)
            for s, v in waits:
                e.wait_ge(s, v)
            for k in range(2):
                ins = e.matmul(ps_flat[:, bass.ds(window, D)], lhs[:, b % NLHS, k, :], rhs(k), start=False, stop=False,
                               skip_group_check=True)
            ins.then_inc(s_use, 1)

        res_flat = w_res[:, :, :, :].rearrange("p n k d -> p (n k d)")
        dve_offs, pe_wins, pe_mats = {}, {}, {}

        def load_tables(u, n):
            def on_dve(e):
                dve_offs.update(zip(range(u, u + n), table(mybir.EngineType.DVE, 0, u, n, LEVELS * R - WIN)))

            def on_pe(e):
                pe_wins.update(zip(range(u, u + n), table(mybir.EngineType.PE, 1, u, n, (NW - 1) * D)))
                pe_mats.update(zip(range(u, u + n), table(mybir.EngineType.PE, 3, u, n, (NRES - 1) * 2 * D)))
            V.run(on_dve)
            T.run(on_pe)
        T.run(lambda e: e.sem_inc(s_use, NLHS))
        for t in (*t_res, t_tab):
            T.run(lambda e, t=t: e.wait_ge(*t))
        V.run(lambda e: e.wait_ge(*t_tab))
        WEIGHTS_BEFORE = {0: (2, 5), 1: (LEVELS - 1, 3), 2: (3, 3), 4: (4, 5), 6: (5, 3)}
        ROWS_AFTER = {1: 2, 3: 3, 5: 4, 7: 5}
        for u in range(U_RES):
            if u % RING == 0:
                load_tables(u, min(RING, U_RES - u))
            if u in WEIGHTS_BEFORE:
                level_weights(*WEIGHTS_BEFORE[u])
            if u == 1:
                level_on_pool(LEVELS - 1, 1)
            if u in BASE:
                V.run(lambda e, l=BASE.index(u, 1): e.wait_ge(*ready[l]))
            V.run(lambda e, u=u: mask_unit(e, u, u, u, dve_offs[u]))
            T.run(lambda e, u=u: multiply_unit(e, u, u, pe_wins[u], lambda k: res_flat[:, bass.ds(pe_mats[u] + k * D, D)]))
            if u in ROWS_AFTER:
                level_rows(ROWS_AFTER[u])
        v_nodes = level_nodes(LEVELS - 2)
        assert sorted(ready) == list(SORTED)

        rowid = sb("rowid", [128, NW])
        v_diag = V.do(lambda e: e.tensor_tensor(diag, ident[0:TP, 0:TP].unsqueeze(1).broadcast_to([TP, NT, TP]),
                                                rank[:, :].unsqueeze(2).broadcast_to([TP, NT, TP]), ALU.mult),
                      v_rank, ready[LEVELS - 1])
        for c, (i0, i1) in enumerate(((0, 4), (4, NT))):
            p = mm(ps[:, 5 + c, 0:(i1 - i0) * TP], ones[0:TP, :], diag[:, i0:i1, :].rearrange("p t n -> p (t n)"), True,
                   True, v_diag, read[5], mark=True)
            s_row = S.do(lambda e, c=c, i0=i0, i1=i1: e.copy(rank_row[:, i0 * TP:i1 * TP], ps[:, 5 + c, 0:(i1 - i0) * TP]),
                         p)
        for w in range(NW):
            g_rowid = G.do(lambda e, w=w: e.tensor_scalar(rowid[:, w:w + 1], row0[:, :], float(w * WIN), None, ALU.add),
                           t_row)
        for w in range(NW):
            t_PmT = G.do(lambda e, w=w: e.tensor_scalar(PmT[:, w, :], rank_row, rowid[:, w:w + 1], None, ALU.is_equal),
                         s_row, g_rowid)

        n_ring = (U - U_RES) // RING

        def ring_steps(e, step):
            with e.Fori(0, n_ring) as it:
                step(it, it * RING, RING)
            if (U - U_RES) % RING:
                step(n_ring, n_ring * RING, (U - U_RES) % RING)

        def units_dve(e):
            for w in (v_nodes, *ready.values()):
                e.wait_ge(*w)

            def step(it, v, n):
                offs = table(mybir.EngineType.DVE, 0, v + (U_RES + T_PAD), n, LEVELS * R - WIN)
                for m in range(n):
                    mask_unit(e, v + (U_RES + m), v + (U_RES + T_PAD + m), U_RES + m, offs[m])
            ring_steps(e, step)
        V.run(units_dve)

        def units_pe(e):
            def step(it, v, n):
                wins = table(mybir.EngineType.PE, 1, v + (U_RES + T_PAD), n, (NW - 1) * D)
                for b in range(n):
                    multiply_unit(e, v + (U_RES + b), U_RES + b, wins[b], lambda k, b=b: ring[:, b, k, :],
                                  (s_ring[b], it * 16 + 16))
            ring_steps(e, step)
        T.run(units_pe)
        units_done = (s_use, NLHS + U)

        def units_load(e):
            e.wait_ge(*t_tab)
            e.wait_ge(*t_raug)
            e.wait_ge(*q_ev[-1])

            def fill(v, n, waits):
                nodes = table(mybir.EngineType.SP, 2, v + (U_RES + T_PAD), n, NODES - 1)
                for b in range(n):
                    if waits:
                        e.wait_ge(s_use, v + (b + U_RES - RING + 1 + NLHS))
                    e.dma_start(ring[:, b, :, :],
                                w2s[bass.ds(nodes[b], 1), :, :].rearrange("o (k p) d -> p (o k) d", p=128)
                                ).then_inc(s_ring[b], 16)
            fill(0, RING, False)
            with e.Fori(1, n_ring) as it:
                fill(it * RING, RING, True)
            if (U - U_RES) % RING:
                fill(n_ring * RING, (U - U_RES) % RING, True)
        Y.run(units_load)

        os_ = part(reg_edge, 0, 128, NW, D)
        s_os = S.do(lambda e: e.copy(os_[:, 0:2, :], ps_flat[:, 0:2 * D].rearrange("p (w d) -> p w d", w=2)), units_done)
        v_os = V.do(lambda e: e.tensor_copy(os_[:, 2:, :], ps_flat[:, 2 * D:NW * D].rearrange("p (w d) -> p w d", w=NW - 2)),
                    units_done)
        fin = part(reg_edge, NW * D, TP, NT, D)
        for i in range(NT):
            for k, n in ((0, 128), (1, 127)):
                mm(ps[0:TP, 3 + i, 0:D], gwT[0:n, k, i * TP:(i + 1) * TP], b2t[0:n, k, :], k == 0, False, *t_b2,
                   s_row, *read.values())
        f_ev = []
        for i in range(NT):
            for w in range(NW):
                p = mm(ps[0:TP, 3 + i, 0:D], PmT[:, w, i * TP:(i + 1) * TP], os_[:, w, :], False, w == NW - 1, s_os, v_os,
                       t_PmT, mark=(w == NW - 1))
            f_ev.append(V.do(lambda e, i=i: e.tensor_tensor(fin[:, i, :], ps[0:TP, 3 + i, 0:D], acc[:, i, :], ALU.add), p, g_root))
        s_out = sem("stored")
        out_v = out.rearrange("(t p) d -> p t d", p=TP)

        def store(e):
            for i in range(NT):
                e.wait_ge(*f_ev[i])
                e.dma_start(out_v[:, i, :], fin[:, i, :]).then_inc(s_out, 16)
            e.wait_ge(s_out, 16 * NT)
        Y.run(store)

        block = ctx.enter_context(nc.Block())
        for name, lane in (("sync", Y), ("gpsimd", G), ("scalar", S), ("vector", V), ("tensor", T)):
            def program(eng, lane=lane):
                for emit in lane.queue:
                    emit(eng)
            {"sync": block.sync, "gpsimd": block.gpsimd, "scalar": block.scalar, "vector": block.vector,
             "tensor": block.tensor}[name](program)


_INS = ["x", "src", "dst", "edge_attr_64", "L0_gnn_Wn", "L0_gnn_bn", "L0_gnn_We", "L0_gnn_be", "L0_gnn_Wc", "L0_gnn_bc",
        "L0_gnn_gamma", "L0_gnn_beta", "L0_mix_w_qkv", "L0_mix_mem_kv", "L0_mix_w_out", "L0_mix_b_out",
        "L0_mix_g_out", "L0_mix_g_pre", "L0_ffn_w1s", "L0_ffn_b1s", "L0_ffn_w2s", "L0_ffn_b2s"]


def kernel(**inputs):
    import numpy as _np
    import concourse.bacc as _bacc
    from concourse import mybir as _mybir
    from concourse.bass_utils import run_bass_kernel_spmd as _run

    nc = _bacc.Bacc("TRN2", target_bir_lowering=False, num_devices=1)
    arrays, args = {}, []
    for name in _INS:
        a = _np.ascontiguousarray(inputs[name])
        arrays[f"in_{name}_dram"] = a
        args.append(nc.dram_tensor(f"in_{name}_dram", a.shape, _mybir.dt.from_np(a.dtype), kind="ExternalInput").ap())
    out = nc.dram_tensor("out_0_dram", (N, D), F32, kind="ExternalOutput").ap()
    graph_layer(nc, *args, out)
    r = _run(nc, [arrays], core_ids=[0])
    return r.results[0]["out_0_dram"]
```
